# Optimizing a Trainium2 kernel written in Bass

```python
import numpy as np
import jax
import jax.numpy as jnp

def _softmax(x, axis=-1):
    return jax.nn.softmax(x, axis=axis)

def _gelu(x):
    return jax.nn.gelu(x, approximate=True)

def _silu(x):
    return jax.nn.silu(x)

def _sigmoid(x):
    return jax.nn.sigmoid(x)

def _layernorm(x, axis=-1, eps=1e-05):
    m = jnp.mean(x, axis=axis, keepdims=True)
    v = jnp.var(x, axis=axis, keepdims=True)
    return (x - m) / jnp.sqrt(v + eps)

def _scatter_add(tgt, idx, src, axis=0):
    return tgt.at[idx].add(src)

def _segment_sum(src, seg, n):
    return jax.ops.segment_sum(src, seg, n)
kernel_name = 'mk_perceiver_d2_seqx_r2_d7f2dc'

def setup_inputs(seed: int=0):
    np.random.seed(seed)
    _w = jnp.asarray

    def _rec_inputs():
        import jax
        import jax.numpy as jnp
        _rk = jax.random.key(seed)
        x = -0.0003929 + 0.9999 * jax.random.normal(jax.random.fold_in(_rk, 1), (1, 512, 512), jnp.float32)
        _lenS = 512 - jax.random.randint(jax.random.fold_in(_rk, 7), (1,), 0, max(1, 512 // 4) + 1, jnp.int32)
        _lenS2 = 8192 - jax.random.randint(jax.random.fold_in(_rk, 8), (1,), 0, max(1, 8192 // 4) + 1, jnp.int32)
        _ctx_1024P = jax.random.normal(jax.random.fold_in(_rk, 11), (1, 16, 512), jnp.float32)
        _ctx_1024c = jax.random.dirichlet(jax.random.fold_in(_rk, 511), 0.3 * jnp.ones((16,), jnp.float32), (1, 8192))
        _ctx_1024t = jnp.einsum('bsk,bkd->bsd', _ctx_1024c, _ctx_1024P)
        _ctx_1024t = _ctx_1024t * jax.lax.rsqrt(jnp.mean(jnp.square(_ctx_1024t)) + 1e-12) * 0.953939
        ctx_1024 = 2.81802e-05 + 1.00001 * (_ctx_1024t + 0.3 * jax.random.normal(jax.random.fold_in(_rk, 611), (1, 8192, 512), jnp.float32))
        _validS = jnp.arange(512)[None, :] < _lenS[:, None]
        _validS2 = jnp.arange(8192)[None, :] < _lenS2[:, None]
        _causal = jnp.tril(jnp.ones((512, 512), dtype=bool))
        mask_S2_ik0 = jnp.where(_validS2[0], 0, 1).astype(jnp.int32)
        return (x, ctx_1024, mask_S2_ik0)
    x, ctx_1024, mask_S2_ik0 = _rec_inputs()

    def _L0_xattn_setup():
        import jax, jax.numpy as jnp
        import numpy as np
        DIM = 512
        NUM_HEADS = 8
        SCALE = (DIM // NUM_HEADS) ** (-0.5)
        key = jax.random.key(seed)
        k1, k2, k3, k4, k5, k6 = jax.random.split(key, 6)
        B, N, M, C = (8, 1024, 1024, DIM)
        x = jax.random.normal(k1, (B, N, C), dtype=jnp.float32)
        support = jax.random.normal(k2, (B, M, C), dtype=jnp.float32)
        attn_mask = jax.random.randint(k3, (M,), 0, 2, dtype=jnp.int32)
        qkv_w = jax.random.normal(k4, (3 * C, C), dtype=jnp.float32) * C ** (-0.5)
        proj_w = jax.random.normal(k5, (C, C), dtype=jnp.float32) * C ** (-0.5)
        proj_b = jax.random.normal(k6, (C,), dtype=jnp.float32) * 0.01
        return {'x': x, 'support': support, 'attn_mask': attn_mask, 'qkv_w': qkv_w, 'proj_w': proj_w, 'proj_b': proj_b}
    _L0_xattn_all = _L0_xattn_setup()
    _L0_xattn_in = {k: v for k, v in _L0_xattn_all.items() if k in ('qkv_w', 'proj_w', 'proj_b')}
    del _L0_xattn_all

    def _L0_attn_setup():
        import jax, jax.numpy as jnp
        import numpy as np
        D_MODEL = 512
        NHEAD = 16
        HEAD_DIM = D_MODEL // NHEAD
        B, L = (4, 2048)
        LN_EPS = 1e-05

        def _retention(v, lam):

            def step(state, v_t):
                state = lam[None, :, None] * state + v_t
                return (state, state)
            v_l_first = jnp.swapaxes(v, 0, 1)
            init = jnp.zeros(v_l_first.shape[1:], dtype=v.dtype)
            _, states = jax.lax.scan(step, init, v_l_first)
            return jnp.swapaxes(states, 0, 1)
        key = jax.random.key(seed)
        ks = jax.random.split(key, 8)
        x = jax.random.normal(ks[0], (B, L, D_MODEL), dtype=jnp.float32)
        sin = jnp.zeros((L, HEAD_DIM), dtype=jnp.float32)
        cos = jnp.zeros((L, HEAD_DIM), dtype=jnp.float32)
        decay = jax.random.uniform(ks[1], (NHEAD, 2, 1), dtype=jnp.float32)
        scale = 0.02
        Wq = jax.random.normal(ks[2], (D_MODEL, D_MODEL), dtype=jnp.float32) * scale
        Wv = jax.random.normal(ks[3], (D_MODEL, D_MODEL), dtype=jnp.float32) * scale
        Wo = jax.random.normal(ks[4], (D_MODEL, D_MODEL), dtype=jnp.float32) * scale
        Wg = jax.random.normal(ks[5], (D_MODEL, D_MODEL), dtype=jnp.float32) * scale
        ln_g = jnp.ones((D_MODEL,), dtype=jnp.float32)
        ln_b = jnp.zeros((D_MODEL,), dtype=jnp.float32)
        return {'x': x, 'sin': sin, 'cos': cos, 'decay': decay, 'Wq': Wq, 'Wv': Wv, 'Wo': Wo, 'Wg': Wg, 'ln_g': ln_g, 'ln_b': ln_b}
    _L0_attn_all = _L0_attn_setup()
    _L0_attn_in = {k: v for k, v in _L0_attn_all.items() if k in ('sin', 'cos', 'decay', 'Wq', 'Wv', 'Wo', 'Wg', 'ln_g', 'ln_b')}
    del _L0_attn_all

    def _L0_ffn_setup():
        import jax, jax.numpy as jnp
        import numpy as np
        BLOCK = 32
        W_BITS = 4
        ACT_BITS = 16

        def act_qdq(x):
            qmax = 2.0 ** (ACT_BITS - 1) - 1.0
            scale = jnp.maximum(jnp.max(jnp.abs(x)) / qmax, 1e-12)
            return jnp.clip(jnp.round(x / scale), -qmax - 1.0, qmax) * scale

        def fixed_qdq_u16(x):
            scale = 1.0 / 65536.0
            return jnp.clip(jnp.round(x / scale), 0.0, 65535.0) * scale

        def lpbq_dequant(w):
            O, I = w.shape
            qmax = 2.0 ** (W_BITS - 1) - 1.0
            wb = w.reshape(O, I // BLOCK, BLOCK)
            s = jnp.maximum(jnp.max(jnp.abs(wb), axis=-1, keepdims=True) / qmax, 1e-12)
            wq = jnp.clip(jnp.round(wb / s), -qmax - 1.0, qmax) * s
            return wq.reshape(O, I)
        key = jax.random.key(seed)
        k1, k2, k3, k4 = jax.random.split(key, 4)
        B, S, H, I = (2, 2048, 512, 1536)
        x = jax.random.normal(k1, (B, S, H), jnp.float32)
        w_gate = jax.random.normal(k2, (I, H), jnp.float32) * 0.02
        w_up = jax.random.normal(k3, (I, H), jnp.float32) * 0.02
        w_down = jax.random.normal(k4, (H, I), jnp.float32) * 0.02
        return {'x': x, 'w_gate': w_gate, 'w_up': w_up, 'w_down': w_down}
    _L0_ffn_all = _L0_ffn_setup()
    _L0_ffn_in = {k: v for k, v in _L0_ffn_all.items() if k in ('w_gate', 'w_up', 'w_down')}
    del _L0_ffn_all

    def _L1_xattn_setup():
        import jax, jax.numpy as jnp
        import numpy as np
        N_HEAD = 16
        key = jax.random.key(seed)
        ks = jax.random.split(key, 5)
        b, l, d = (4, 1024, 512)
        dh = d // N_HEAD
        return {'q': jax.random.normal(ks[0], (b, l, d), dtype=jnp.float32), 'kv': jax.random.normal(ks[1], (b, l, d), dtype=jnp.float32), 'Wq': jax.random.normal(ks[2], (d, d), dtype=jnp.float32) * 0.02, 'Wkv': jax.random.normal(ks[3], (2 * dh, d), dtype=jnp.float32) * 0.02, 'Wc': jax.random.normal(ks[4], (d, d), dtype=jnp.float32) * 0.02}
    _L1_xattn_all = _L1_xattn_setup()
    _L1_xattn_in = {k: v for k, v in _L1_xattn_all.items() if k in ('Wq', 'Wkv', 'Wc')}
    del _L1_xattn_all

    def _L1_attn_setup():
        import jax, jax.numpy as jnp
        import numpy as np
        from jax import lax
        D_MODEL = 512
        EXPAND = 2
        D_INNER = EXPAND * D_MODEL
        HEADDIM = 64
        NHEADS = D_INNER // HEADDIM
        D_STATE = 128
        D_CONV = 4
        NGROUPS = 1
        CONV_DIM = D_INNER + 2 * NGROUPS * D_STATE
        D_IN_PROJ = 2 * D_INNER + 2 * NGROUPS * D_STATE + NHEADS
        BATCH, SEQLEN = (2, 1024)
        EPS = 1e-05

        def _causal_depthwise_conv(x, w, b):
            K = w.shape[1]
            xp = jnp.pad(x, ((0, 0), (K - 1, 0), (0, 0)))
            L = x.shape[1]
            out = b[None, None, :]
            for k in range(K):
                out = out + xp[:, k:k + L, :] * w[:, k][None, None, :]
            return out

        def _ssd_scan(dt, A, x, Bm, Cm):
            Bsz = x.shape[0]
            dA = jnp.exp(dt * A[None, None, :])
            dtx = dt[..., None] * x

            def step(h, inp):
                dA_t, dtx_t, B_t, C_t = inp
                h = h * dA_t[:, :, None, None] + dtx_t[..., None] * B_t[:, None, None, :]
                y = jnp.einsum('bhpn,bn->bhp', h, C_t)
                return (h, y)
            h0 = jnp.zeros((Bsz, NHEADS, HEADDIM, D_STATE), x.dtype)
            _, ys = lax.scan(step, h0, (dA.transpose(1, 0, 2), dtx.transpose(1, 0, 2, 3), Bm.transpose(1, 0, 2), Cm.transpose(1, 0, 2)))
            return ys.transpose(1, 0, 2, 3)
        key = jax.random.key(seed)
        ks = jax.random.split(key, 10)
        u = jax.random.normal(ks[0], (BATCH, SEQLEN, D_MODEL), jnp.float32)
        W_in = jax.random.normal(ks[1], (D_IN_PROJ, D_MODEL), jnp.float32) * D_MODEL ** (-0.5)
        conv_w = jax.random.normal(ks[2], (CONV_DIM, D_CONV), jnp.float32) * D_CONV ** (-0.5)
        conv_b = jnp.zeros((CONV_DIM,), jnp.float32)
        dt_bias = jnp.log(jnp.exp(jax.random.uniform(ks[3], (NHEADS,), jnp.float32, minval=0.001, maxval=0.1)) - 1.0)
        A_log = jnp.log(jax.random.uniform(ks[4], (NHEADS,), jnp.float32, minval=1.0, maxval=16.0))
        D = jnp.ones((NHEADS,), jnp.float32)
        norm_w = jnp.ones((D_INNER,), jnp.float32)
        W_out = jax.random.normal(ks[5], (D_MODEL, D_INNER), jnp.float32) * D_INNER ** (-0.5)
        return {'u': u, 'W_in': W_in, 'conv_w': conv_w, 'conv_b': conv_b, 'dt_bias': dt_bias, 'A_log': A_log, 'D': D, 'norm_w': norm_w, 'W_out': W_out}
    _L1_attn_all = _L1_attn_setup()
    _L1_attn_in = {k: v for k, v in _L1_attn_all.items() if k in ('W_in', 'conv_w', 'conv_b', 'dt_bias', 'A_log', 'D', 'norm_w', 'W_out')}
    del _L1_attn_all

    def _L1_ffn_setup():
        import jax, jax.numpy as jnp
        import numpy as np
        B, S, D_MODEL, D_HIDDEN = (4, 1024, 512, 2048)

        def act_quant(x):
            scale = 127.0 / jnp.clip(jnp.max(jnp.abs(x), axis=-1, keepdims=True), 1e-05)
            return jnp.clip(jnp.round(x * scale), -128, 127) / scale

        def weight_quant(w):
            scale = 1.0 / jnp.clip(jnp.mean(jnp.abs(w)), 1e-05)
            return jnp.clip(jnp.round(w * scale), -1, 1) / scale

        def bit_linear(x, w):
            xq = x + jax.lax.stop_gradient(act_quant(x) - x)
            wq = w + jax.lax.stop_gradient(weight_quant(w) - w)
            return jnp.einsum('bsd,hd->bsh', xq, wq)

        def depthwise_conv1d(x_bcl, w, b):
            y = jax.lax.conv_general_dilated(x_bcl, w, window_strides=(1,), padding=[(1, 1)], dimension_numbers=('NCH', 'OIH', 'NCH'), feature_group_count=x_bcl.shape[1])
            return y + b[None, :, None]
        key = jax.random.key(seed)
        ks = jax.random.split(key, 5)
        lim1 = 1.0 / np.sqrt(D_MODEL)
        lim2 = 1.0 / np.sqrt(D_HIDDEN)
        limc = 1.0 / np.sqrt(3.0)
        return {'x': jax.random.normal(ks[0], (B, S, D_MODEL), dtype=jnp.float32), 'w1': jax.random.uniform(ks[1], (D_HIDDEN, D_MODEL), jnp.float32, -lim1, lim1), 'conv_w': jax.random.uniform(ks[2], (D_HIDDEN, 1, 3), jnp.float32, -limc, limc), 'conv_b': jax.random.uniform(ks[3], (D_HIDDEN,), jnp.float32, -limc, limc), 'w2': jax.random.uniform(ks[4], (D_MODEL, D_HIDDEN), jnp.float32, -lim2, lim2)}
    _L1_ffn_all = _L1_ffn_setup()
    _L1_ffn_in = {k: v for k, v in _L1_ffn_all.items() if k in ('w1', 'conv_w', 'conv_b', 'w2')}
    del _L1_ffn_all
    return {'x': x, 'ctx_1024': ctx_1024, 'mask_S2_ik0': mask_S2_ik0, 'L0_xattn_qkv_w': _L0_xattn_in['qkv_w'], 'L0_xattn_proj_w': _L0_xattn_in['proj_w'], 'L0_xattn_proj_b': _L0_xattn_in['proj_b'], 'L0_attn_sin': _L0_attn_in['sin'], 'L0_attn_cos': _L0_attn_in['cos'], 'L0_attn_decay': _L0_attn_in['decay'], 'L0_attn_Wq': _L0_attn_in['Wq'], 'L0_attn_Wv': _L0_attn_in['Wv'], 'L0_attn_Wo': _L0_attn_in['Wo'], 'L0_attn_Wg': _L0_attn_in['Wg'], 'L0_attn_ln_g': _L0_attn_in['ln_g'], 'L0_attn_ln_b': _L0_attn_in['ln_b'], 'L0_ffn_w_gate': _L0_ffn_in['w_gate'], 'L0_ffn_w_up': _L0_ffn_in['w_up'], 'L0_ffn_w_down': _L0_ffn_in['w_down'], 'L1_xattn_Wq': _L1_xattn_in['Wq'], 'L1_xattn_Wkv': _L1_xattn_in['Wkv'], 'L1_xattn_Wc': _L1_xattn_in['Wc'], 'L1_attn_W_in': _L1_attn_in['W_in'], 'L1_attn_conv_w': _L1_attn_in['conv_w'], 'L1_attn_conv_b': _L1_attn_in['conv_b'], 'L1_attn_dt_bias': _L1_attn_in['dt_bias'], 'L1_attn_A_log': _L1_attn_in['A_log'], 'L1_attn_D': _L1_attn_in['D'], 'L1_attn_norm_w': _L1_attn_in['norm_w'], 'L1_attn_W_out': _L1_attn_in['W_out'], 'L1_ffn_w1': _L1_ffn_in['w1'], 'L1_ffn_conv_w': _L1_ffn_in['conv_w'], 'L1_ffn_conv_b': _L1_ffn_in['conv_b'], 'L1_ffn_w2': _L1_ffn_in['w2']}

def reference(x, ctx_1024, mask_S2_ik0, L0_xattn_qkv_w, L0_xattn_proj_w, L0_xattn_proj_b, L0_attn_sin, L0_attn_cos, L0_attn_decay, L0_attn_Wq, L0_attn_Wv, L0_attn_Wo, L0_attn_Wg, L0_attn_ln_g, L0_attn_ln_b, L0_ffn_w_gate, L0_ffn_w_up, L0_ffn_w_down, L1_xattn_Wq, L1_xattn_Wkv, L1_xattn_Wc, L1_attn_W_in, L1_attn_conv_w, L1_attn_conv_b, L1_attn_dt_bias, L1_attn_A_log, L1_attn_D, L1_attn_norm_w, L1_attn_W_out, L1_ffn_w1, L1_ffn_conv_w, L1_ffn_conv_b, L1_ffn_w2):
    import jax
    import jax.numpy as jnp

    def _L0_xattn_ref(x, support, attn_mask, qkv_w, proj_w, proj_b):
        import jax, jax.numpy as jnp
        import numpy as np
        DIM = 512
        NUM_HEADS = 8
        SCALE = (DIM // NUM_HEADS) ** (-0.5)
        B, N, C = x.shape
        wq, wk, wv = (qkv_w[:C], qkv_w[C:2 * C], qkv_w[2 * C:])
        q = jnp.einsum('bnc,dc->bnd', x, wq)
        k = jnp.einsum('bmc,dc->bmd', support, wk)
        v = jnp.einsum('bmc,dc->bmd', support, wv)
        attn = jnp.einsum('bnd,bmd->bnm', q, k) * SCALE
        attn = jax.nn.softmax(attn, axis=-1)
        attn = jnp.where(attn_mask[None, None, :] == 0, 0.0, attn)
        out = jnp.einsum('bnm,bmd->bnd', attn, v)
        out = jnp.swapaxes(out, 1, 2).reshape(B, N, C)
        out = jnp.einsum('bnc,dc->bnd', out, proj_w) + proj_b
        return out

    def _L0_attn_ref(x, sin, cos, decay, Wq, Wv, Wo, Wg, ln_g, ln_b):
        import jax, jax.numpy as jnp
        import numpy as np
        D_MODEL = 512
        NHEAD = 16
        HEAD_DIM = D_MODEL // NHEAD
        B, L = (4, 2048)
        LN_EPS = 1e-05

        def _retention(v, lam):

            def step(state, v_t):
                state = lam[None, :, None] * state + v_t
                return (state, state)
            v_l_first = jnp.swapaxes(v, 0, 1)
            init = jnp.zeros(v_l_first.shape[1:], dtype=v.dtype)
            _, states = jax.lax.scan(step, init, v_l_first)
            return jnp.swapaxes(states, 0, 1)
        del sin, cos
        Bx, Lx, D = x.shape
        H = decay.shape[0]
        Dh = D // H
        q = (x @ Wq.T).reshape(Bx, Lx, H, Dh)
        v = (x @ Wv.T).reshape(Bx, Lx, H, Dh)
        lam = decay[:, 1, 0]
        state = _retention(v, lam)
        y = (q * state).reshape(Bx, Lx, D)
        mu = jnp.mean(y, axis=-1, keepdims=True)
        var = jnp.mean(jnp.square(y - mu), axis=-1, keepdims=True)
        y = (y - mu) * jax.lax.rsqrt(var + LN_EPS) * ln_g + ln_b
        gate = jax.nn.silu(x @ Wg.T)
        y = y * gate
        return y @ Wo.T

    def _L0_ffn_ref(x, w_gate, w_up, w_down):
        import jax, jax.numpy as jnp
        import numpy as np
        BLOCK = 32
        W_BITS = 4
        ACT_BITS = 16

        def act_qdq(x):
            qmax = 2.0 ** (ACT_BITS - 1) - 1.0
            scale = jnp.maximum(jnp.max(jnp.abs(x)) / qmax, 1e-12)
            return jnp.clip(jnp.round(x / scale), -qmax - 1.0, qmax) * scale

        def fixed_qdq_u16(x):
            scale = 1.0 / 65536.0
            return jnp.clip(jnp.round(x / scale), 0.0, 65535.0) * scale

        def lpbq_dequant(w):
            O, I = w.shape
            qmax = 2.0 ** (W_BITS - 1) - 1.0
            wb = w.reshape(O, I // BLOCK, BLOCK)
            s = jnp.maximum(jnp.max(jnp.abs(wb), axis=-1, keepdims=True) / qmax, 1e-12)
            wq = jnp.clip(jnp.round(wb / s), -qmax - 1.0, qmax) * s
            return wq.reshape(O, I)
        x = act_qdq(x)
        up = act_qdq(x @ lpbq_dequant(w_up).T)
        gate = act_qdq(x @ lpbq_dequant(w_gate).T)
        sig = fixed_qdq_u16(jax.nn.sigmoid(gate))
        gate = act_qdq(gate * sig)
        o = act_qdq(gate * up)
        return o @ lpbq_dequant(w_down).T

    def _L1_xattn_ref(q, kv, Wq, Wkv, Wc):
        import jax, jax.numpy as jnp
        import numpy as np
        N_HEAD = 16
        b, l, d = q.shape
        h = N_HEAD
        dh = d // h
        qp = jnp.einsum('bld,ed->ble', q, Wq)
        scores = jnp.einsum('bld,bmd->blm', qp, kv)
        idx = jnp.argmax(scores, axis=-1)
        mem = jnp.take_along_axis(kv, idx[..., None], axis=1)
        mkv = jnp.einsum('bld,ed->ble', mem, Wkv)
        mk, mv = jnp.split(mkv, 2, axis=-1)
        qh = qp.reshape(b, l, h, dh).transpose(0, 2, 1, 3)
        scale = 1.0 / np.sqrt(dh).astype(np.float32)
        logits = jnp.einsum('bhld,bmd->bhlm', qh, mk) * scale
        attn = jax.nn.softmax(logits, axis=-1)
        out = jnp.einsum('bhlm,bmd->bhld', attn, mv)
        out = out.transpose(0, 2, 1, 3).reshape(b, l, d)
        return jnp.einsum('bld,ed->ble', out, Wc)

    def _L1_attn_ref(u, W_in, conv_w, conv_b, dt_bias, A_log, D, norm_w, W_out):
        import jax, jax.numpy as jnp
        import numpy as np
        from jax import lax
        D_MODEL = 512
        EXPAND = 2
        D_INNER = EXPAND * D_MODEL
        HEADDIM = 64
        NHEADS = D_INNER // HEADDIM
        D_STATE = 128
        D_CONV = 4
        NGROUPS = 1
        CONV_DIM = D_INNER + 2 * NGROUPS * D_STATE
        D_IN_PROJ = 2 * D_INNER + 2 * NGROUPS * D_STATE + NHEADS
        BATCH, SEQLEN = (2, 1024)
        EPS = 1e-05

        def _causal_depthwise_conv(x, w, b):
            K = w.shape[1]
            xp = jnp.pad(x, ((0, 0), (K - 1, 0), (0, 0)))
            L = x.shape[1]
            out = b[None, None, :]
            for k in range(K):
                out = out + xp[:, k:k + L, :] * w[:, k][None, None, :]
            return out

        def _ssd_scan(dt, A, x, Bm, Cm):
            Bsz = x.shape[0]
            dA = jnp.exp(dt * A[None, None, :])
            dtx = dt[..., None] * x

            def step(h, inp):
                dA_t, dtx_t, B_t, C_t = inp
                h = h * dA_t[:, :, None, None] + dtx_t[..., None] * B_t[:, None, None, :]
                y = jnp.einsum('bhpn,bn->bhp', h, C_t)
                return (h, y)
            h0 = jnp.zeros((Bsz, NHEADS, HEADDIM, D_STATE), x.dtype)
            _, ys = lax.scan(step, h0, (dA.transpose(1, 0, 2), dtx.transpose(1, 0, 2, 3), Bm.transpose(1, 0, 2), Cm.transpose(1, 0, 2)))
            return ys.transpose(1, 0, 2, 3)
        Bsz, L, _ = u.shape
        zxbcdt = jnp.einsum('bld,ed->ble', u, W_in)
        z = zxbcdt[..., :D_INNER]
        xBC = zxbcdt[..., D_INNER:D_INNER + CONV_DIM]
        dt = zxbcdt[..., D_INNER + CONV_DIM:]
        xBC = jax.nn.silu(_causal_depthwise_conv(xBC, conv_w, conv_b))
        x = xBC[..., :D_INNER].reshape(Bsz, L, NHEADS, HEADDIM)
        Bm = xBC[..., D_INNER:D_INNER + D_STATE]
        Cm = xBC[..., D_INNER + D_STATE:]
        dt = jax.nn.softplus(dt + dt_bias[None, None, :])
        A = -jnp.exp(A_log)
        y = _ssd_scan(dt, A, x, Bm, Cm)
        y = y + D[None, None, :, None] * x
        y = y.reshape(Bsz, L, D_INNER)
        y = y * jax.nn.silu(z)
        y = y * lax.rsqrt(jnp.mean(y * y, axis=-1, keepdims=True) + EPS) * norm_w[None, None, :]
        return jnp.einsum('ble,de->bld', y, W_out)

    def _L1_ffn_ref(x, w1, conv_w, conv_b, w2):
        import jax, jax.numpy as jnp
        import numpy as np
        B, S, D_MODEL, D_HIDDEN = (4, 1024, 512, 2048)

        def act_quant(x):
            scale = 127.0 / jnp.clip(jnp.max(jnp.abs(x), axis=-1, keepdims=True), 1e-05)
            return jnp.clip(jnp.round(x * scale), -128, 127) / scale

        def weight_quant(w):
            scale = 1.0 / jnp.clip(jnp.mean(jnp.abs(w)), 1e-05)
            return jnp.clip(jnp.round(w * scale), -1, 1) / scale

        def bit_linear(x, w):
            xq = x + jax.lax.stop_gradient(act_quant(x) - x)
            wq = w + jax.lax.stop_gradient(weight_quant(w) - w)
            return jnp.einsum('bsd,hd->bsh', xq, wq)

        def depthwise_conv1d(x_bcl, w, b):
            y = jax.lax.conv_general_dilated(x_bcl, w, window_strides=(1,), padding=[(1, 1)], dimension_numbers=('NCH', 'OIH', 'NCH'), feature_group_count=x_bcl.shape[1])
            return y + b[None, :, None]
        h = bit_linear(x, w1)
        h = depthwise_conv1d(h.transpose(0, 2, 1), conv_w, conv_b)
        h = h.transpose(0, 2, 1)
        h = jax.nn.silu(h)
        return bit_linear(h, w2)
    x = x + _L0_xattn_ref(_layernorm(x, axis=-1), ctx_1024, mask_S2_ik0, L0_xattn_qkv_w, L0_xattn_proj_w, L0_xattn_proj_b)
    x = x + _L0_attn_ref(_layernorm(x, axis=-1), L0_attn_sin, L0_attn_cos, L0_attn_decay, L0_attn_Wq, L0_attn_Wv, L0_attn_Wo, L0_attn_Wg, L0_attn_ln_g, L0_attn_ln_b)
    x = x + _L0_ffn_ref(_layernorm(x, axis=-1), L0_ffn_w_gate, L0_ffn_w_up, L0_ffn_w_down)
    x = x + _L1_xattn_ref(_layernorm(x, axis=-1), ctx_1024, L1_xattn_Wq, L1_xattn_Wkv, L1_xattn_Wc)
    x = x + _L1_attn_ref(_layernorm(x, axis=-1), L1_attn_W_in, L1_attn_conv_w, L1_attn_conv_b, L1_attn_dt_bias, L1_attn_A_log, L1_attn_D, L1_attn_norm_w, L1_attn_W_out)
    x = x + _L1_ffn_ref(_layernorm(x, axis=-1), L1_ffn_w1, L1_ffn_conv_w, L1_ffn_conv_b, L1_ffn_w2)
    return x

_drawn_inputs = setup_inputs


def setup_inputs(seed=0):
    import zlib

    import numpy as np

    out = dict(_drawn_inputs(seed))
    spreads = {'L0_attn_sin': (0.0, 0.1),
     'L0_attn_cos': (0.0, 0.1),
     'L0_attn_ln_g': (1.0, 0.544),
     'L0_attn_ln_b': (0.0, 0.57),
     'L1_attn_conv_b': (0.0, 0.1),
     'L1_attn_D': (1.0, 0.2),
     'L1_attn_norm_w': (1.0, 0.2)}
    factors = {'L0_xattn_proj_b': 3.394}
    for name, (base, spread) in spreads.items():
        noise = np.random.default_rng([zlib.crc32(name.encode()), seed]).standard_normal(out[name].shape)
        drawn = base * np.exp(spread * noise) if base else spread * noise
        out[name] = jnp.asarray(drawn.astype(out[name].dtype))
    for name, factor in factors.items():
        out[name] = (out[name] * factor).astype(out[name].dtype)
    return out
```

```python
from contextlib import ExitStack

import concourse.bass as bass
from concourse import mybir

F32 = mybir.dt.float32
F16 = mybir.dt.float16
BF16 = mybir.dt.bfloat16
I32 = mybir.dt.int32
U32 = mybir.dt.uint32
ALU = mybir.AluOpType
ACT = mybir.ActivationFunctionType
AX = mybir.AxisListType
RMAX = bass.bass_isa.ReduceOp.max
RADD = bass.bass_isa.ReduceOp.add

P = 128
D = 512
DT = D // P
N = 512
NT = N // P
M = 8192
MT = M // P
CH = 4
NCH = MT // CH
PAIRS = NCH // 2
EPS = 1e-5
ROUND = 12582912.0
FF0 = 1536
F0T = FF0 // P
QB = 32
ATT_H = 16
DH = D // ATT_H
SSM_H = 16
SSM_P = 64
SSM_I = SSM_H * SSM_P
SSM_N = 128
CONV = SSM_I + 2 * SSM_N
CVT = CONV // P
IT = SSM_I // P
PROJ = 2 * SSM_I + 2 * SSM_N + SSM_H
FF1 = 2048
F1T = FF1 // P
NEG = -1e30
Q_SCALE = float(D // 8) ** -0.5


def layout(v, np):
    def arr(name):
        return np.asarray(v[name])

    def blocks32(w):
        o, i = w.shape
        return w.reshape(o // QB, QB, i // P, P // QB, QB).transpose(3, 1, 2, 0, 4).reshape(P, (i // P) * o)

    def columns(x):
        return x.reshape(-1, P).T

    ctx = arr("ctx_1024")[0]
    qkv = arr("L0_xattn_qkv_w")
    wkv = arr("L1_xattn_Wkv")
    w_in = arr("L1_attn_W_in")
    out = {
        "x": arr("x")[0],
        "ctx": ctx,
        "ctxT": ctx.T.reshape(DT, P, NCH, CH * P).transpose(2, 1, 0, 3),
        "mask": arr("mask_S2_ik0").reshape(MT, P).T,
        "wq0": qkv[:D], "wk0": qkv[D:2 * D], "wvT0": qkv[2 * D:].T,
        "projT0": arr("L0_xattn_proj_w").T, "projb0": arr("L0_xattn_proj_b"),
        "lam": columns(np.repeat(arr("L0_attn_decay")[:, 1, 0], D // 16)),
        "lng": columns(arr("L0_attn_ln_g")), "lnb": columns(arr("L0_attn_ln_b")),
        "WvT": arr("L0_attn_Wv").T, "WqT": arr("L0_attn_Wq").T, "WgT": arr("L0_attn_Wg").T,
        "WoT": arr("L0_attn_Wo").T,
        "upB": blocks32(arr("L0_ffn_w_up")), "gateB": blocks32(arr("L0_ffn_w_gate")),
        "downB": blocks32(arr("L0_ffn_w_down")),
        "Wq1T": arr("L1_xattn_Wq").T,
        "Wk1T": np.tile(wkv[:DH].T, (1, P // DH)), "Wv1T": wkv[DH:].T,
        "Wc1T": arr("L1_xattn_Wc").T,
        "WinT": w_in.T,
        "convw": arr("L1_attn_conv_w").reshape(CVT, P, 4).transpose(1, 0, 2), "convb": columns(arr("L1_attn_conv_b")),
        "dtb": arr("L1_attn_dt_bias"), "alog": arr("L1_attn_A_log"), "ssmd": arr("L1_attn_D"),
        "normw": columns(arr("L1_attn_norm_w")), "WoutT": arr("L1_attn_W_out").T,
        "w1T": arr("L1_ffn_w1").T, "fconvw": arr("L1_ffn_conv_w").reshape(F1T, P, 3).transpose(1, 0, 2),
        "fconvb": columns(arr("L1_ffn_conv_b")), "w2T": arr("L1_ffn_w2").T,
    }
    return out


def perceiver_kernel(nc, a, out, stages=6, first=0):
    ctx = ExitStack()
    with ctx:
        def sb(name, shape, dt):
            return ctx.enter_context(nc.sbuf_tensor(name, shape, dt))

        def sem(name):
            return ctx.enter_context(nc.semaphore(name))

        X = sb("X", [P, NT, D], F32)
        XN = sb("XN", [P, NT, D], F32)
        XT = sb("XT", [P, DT, N], F32)
        IDENT = sb("IDENT", [P, P], F32)
        ONES = sb("ONES", [P, P], F32)
        MEANW = sb("MEANW", [P, P], F32)
        UPPER = sb("UPPER", [P, P], F32)
        FUTURE = sb("FUTURE", [P, P], F32)
        ZROW = sb("ZROW", [1, D], F16)
        MASKI = sb("MASKI", [P, MT], I32)
        MASK = sb("MASK", [P, MT], F32)
        EPSC = sb("EPSC", [P, 1], F32)
        STATS = sb("STATS", [P, NT, 6], F32)
        MV = sb("MV", [P, NT, 2], F32)
        STD = sb("STD", [P, NT], F32)
        RSTD = sb("RSTD", [P, NT], F32)
        COLS = sb("COLS", [P, 64], F32)
        SM = sb("SM", [P, 64], F32)
        arena = sb("arena", [P, 178 * 256], F32)
        PS = ctx.enter_context(nc.psum_tensor("PS", [P, 8, 512], F32))

        def view(at, shape, dt=F32):
            size = 2 if dt in (F16, BF16) else 4
            n = 1
            for s in shape:
                n *= s
            v = arena[:, at // 4:(at + n * size) // 4]
            if dt != F32:
                v = v.bitcast(dt)
            if len(shape) == 1:
                return v
            if len(shape) == 2:
                return v.rearrange("p (a b) -> p a b", a=shape[0])
            return v.rearrange("p (a b c) -> p a b c", a=shape[0], b=shape[1])

        K = 1024
        w_in = {i: sem(f"w_in{i}") for i in (0, 1, 3, 4, 5)}
        x_in = sem("x_in")
        mask_in = sem("mask_in")
        bias_in = sem("bias_in")
        const_ready = sem("const_ready")
        x_done = sem("x_done")
        out_psum = sem("out_psum")
        ln_stats = sem("ln_stats")
        ln_var = sem("ln_var")
        ln_std = sem("ln_std")
        ln_rstd = sem("ln_rstd")
        ln_xn = sem("ln_xn")
        xt_psum = sem("xt_psum")
        xt_ready = sem("xt_ready")
        dve_order = sem("dve_order")
        settled = sem("settled")
        act_order = sem("act_order")
        pool_order = sem("pool_order")

        def settle(eng):
            eng.sem_inc(settled, 1)

        def layernorm_dve(dve, stage, link, finish=True):
            stage -= first
            if stage:
                dve.wait_ge(x_done, NT * stage)
            for t in range(NT):
                dve.bn_stats(STATS[:, t, :], X[:, t, :]).then_inc(ln_stats, 1)
            dve.wait_ge(ln_stats, NT * (stage + 1))
            for t in range(NT):
                dve.bn_aggr(MV[:, t, :], STATS[:, t, :]).then_inc(ln_var, 1)
            dve.wait_ge(ln_std, stage + 1)
            dve.reciprocal(RSTD[:, :], STD[:, :]).then_inc(ln_rstd, 1)
            dve.wait_ge(ln_rstd, stage + 1)
            for t in range(NT):
                ins = dve.tensor_scalar(XN[:, t, :], X[:, t, :], MV[:, t, 0:1], RSTD[:, t:t + 1],
                                        ALU.subtract, ALU.mult)
                if finish:
                    ins.then_inc(ln_xn, 1)
                else:
                    ins.then_inc(dve_order, 1)
                    link.add(1)

        def layernorm_act(act, stage):
            stage -= first
            act.wait_ge(ln_var, NT * (stage + 1))
            act.activation(STD[:, :], MV[:, :, 1], ACT.Sqrt, bias=EPSC[:, 0:1]).then_inc(ln_std, 1)

        def transpose_x_pe(pe, stage):
            stage -= first
            pe.wait_ge(ln_xn, NT * (stage + 1))
            for c in range(DT):
                for t in range(NT):
                    ins = pe.transpose(PS[:, c, t * P:(t + 1) * P], XN[:, t, c * P:(c + 1) * P], IDENT[:, :])
                ins.then_inc(xt_psum, 1)

        def transpose_x_act(act, stage):
            stage -= first
            for c in range(DT):
                act.wait_ge(xt_psum, DT * stage + c + 1)
                act.copy(XT[:, c, :], PS[:, c, :]).then_inc(xt_ready, 1)

        class Order:

            def __init__(self, eng, s):
                self.eng, self.s, self.n = eng, s, 0

            def add(self, n):
                self.n += n

            def __call__(self, ins):
                self.n += 1
                ins.then_inc(self.s, 1)
                self.eng.wait_ge(self.s, self.n)

            def note(self, ins):
                self.n += 1
                ins.then_inc(self.s, 1)

            def wait(self):
                self.eng.wait_ge(self.s, self.n)

        ST = view(0, [MT, N])
        CR = view(128 * K, [2, CH, 512])
        CHI = view(144 * K, [2, CH, 512], F16)
        CLO = view(152 * K, [2, CH, 512], F16)
        QHI = view(160 * K, [DT, N], F16)
        QLO = view(164 * K, [DT, N], F16)
        PHI = view(160 * K, [2, N], F16)
        PLO = view(162 * K, [2, N], F16)
        PSUMS = view(164 * K, [N])
        RUNMAX = view(168 * K, [N])
        COLMAX = view(170 * K, [N])
        WQ = view(0, [DT, D])
        WK = view(8 * K, [DT, D])
        WQK = view(16 * K, [DT, D])
        WVT = XN
        PROJT = XT
        O = view(0, [NT, D])
        Z = view(8 * K, [DT, D])
        BIAS = view(16 * K, [D])

        s0_wqk_psum = sem("s0_wqk_psum")
        s0_wqk = sem("s0_wqk")
        s0_q_psum = sem("s0_q_psum")
        s0_q_hi = sem("s0_q_hi")
        s0_q_lo = sem("s0_q_lo")
        s0_chunk = [sem("s0_chunk0"), sem("s0_chunk1")]
        s0_hi = sem("s0_hi")
        s0_lo = sem("s0_lo")
        s0_scores = sem("s0_scores")
        s0_max = sem("s0_max")
        s0_copied = sem("s0_copied")
        s0_colmax = sem("s0_colmax")
        s0_row = [sem("s0_row0"), sem("s0_row1")]
        s0_shift = sem("s0_shift")
        s0_exp = sem("s0_exp")
        s0_p_hi = sem("s0_p_hi")
        s0_p_lo = sem("s0_p_lo")
        s0_sum = sem("s0_sum")
        s0_c_hi = sem("s0_c_hi")
        s0_c_lo = sem("s0_c_lo")
        s0_pv = sem("s0_pv")
        s0_close = sem("s0_close")
        s0_den = sem("s0_den")
        s0_mask = sem("s0_mask")
        s0_o = sem("s0_o")
        s0_z_psum = sem("s0_z_psum")
        s0_z = sem("s0_z")
        s0_primed = sem("s0_primed")

        ctxT = a["ctxT"]
        ctx_rows = a["ctx"].rearrange("(k j p) c -> k p j c", j=CH, p=P)

        BANKS = 8
        AHEAD_SPLIT = 2
        AHEAD_TILES = CH + 1
        AHEAD_BANK = BANKS

        def s0_sp(sp):
            sp.dma_start(WQ, a["wq0"].rearrange("(t p) c -> p t c", p=P)).then_inc(w_in[0], 16)
            sp.dma_start(WK, a["wk0"].rearrange("(t p) c -> p t c", p=P)).then_inc(w_in[0], 16)
            sp.dma_start(MASKI[:, :], a["mask"]).then_inc(mask_in, 16)
            sp.wait_ge(s0_primed, 1)
            with sp.Fori(0, PAIRS) as i:
                for b in range(2):
                    sp.wait_ge(s0_hi, i * 2 + b + 1)
                    sp.wait_ge(s0_lo, i * 2 + b + 1)
                    sp.dma_start(CR[:, b], a["ctxT"][i * 2 + b]).then_inc(s0_chunk[b], 16)
            sp.dma_start(WVT[:, :, :], a["wvT0"].rearrange("(t p) c -> p t c", p=P)).then_inc(w_in[0], 16)
            sp.dma_start(PROJT[:, :, :], a["projT0"].rearrange("(t p) c -> p t c", p=P)).then_inc(w_in[0], 16)
            sp.wait_ge(s0_hi, NCH + AHEAD_SPLIT)
            sp.wait_ge(s0_lo, NCH + AHEAD_SPLIT)
            with sp.Fori(0, PAIRS) as i:
                for b in range(2):
                    sp.wait_ge(s0_c_hi, (i * 2 + b) * CH + 1)
                    sp.wait_ge(s0_c_lo, (i * 2 + b) * CH + 1)
                    sp.dma_start(CR[:, b], ctx_rows[i * 2 + b]).then_inc(s0_row[b], 16)
            sp.wait_ge(s0_close, 1)
            sp.dma_start(BIAS, a["projb0"].partition_broadcast(P)).then_inc(bias_in, 16)

        def setup_pool(pool, link):
            link(pool.memset(IDENT[:, :], 0.0))
            link(pool.affine_select(out=IDENT[:, :], in_=IDENT[:, :], compare_op=ALU.not_equal, fill=1.0,
                                    base=0, pattern=[[-1, P]], channel_multiplier=1))
            link(pool.memset(ONES[:, :], 1.0))
            link(pool.affine_select(out=UPPER[:, :], in_=ONES[:, :], compare_op=ALU.is_ge, fill=0.0,
                                    base=0, pattern=[[1, P]], channel_multiplier=-1))
            link(pool.memset(FUTURE[:, :], 0.0))
            link(pool.affine_select(out=FUTURE[:, :], in_=FUTURE[:, :], compare_op=ALU.is_ge, fill=NEG,
                                    base=0, pattern=[[1, P]], channel_multiplier=-1))
            link(pool.memset(MEANW[:, :], 1.0 / D))
            link(pool.memset(EPSC[:, :], EPS))
            link(pool.memset(ZROW[:, :], 0.0))
            pool.sem_inc(s0_hi, AHEAD_SPLIT)
            pool.sem_inc(s0_lo, AHEAD_SPLIT)
            for s in (s0_scores, s0_c_hi, s0_c_lo, s0_pv):
                pool.sem_inc(s, AHEAD_TILES)
            pool.sem_inc(s0_copied, AHEAD_BANK)
            pool.sem_inc(s0_primed, 1)
            pool.sem_inc(const_ready, 1)
        def s0_pool(pool, link):
            with pool.Fori(0, PAIRS) as i:
                for b in range(2):
                    pool.wait_ge(s0_hi, i * 2 + b + 1 + AHEAD_SPLIT)
                    pool.wait_ge(s0_scores, (i * 2 + b) * CH + 1)
                    pool.tensor_tensor(CLO[:, b], CR[:, b], CHI[:, b], ALU.subtract).then_inc(s0_lo, 1)
            pool.wait_ge(s0_max, MT + 1)
            link(pool.partition_all_reduce(COLMAX, RUNMAX, P, RMAX))
            pool.wait_ge(s0_copied, MT + AHEAD_BANK)
            with pool.Fori(0, MT) as k:
                pool.tensor_tensor(ST[:, k, :], ST[:, k, :], COLMAX, ALU.subtract).then_inc(s0_shift, 1)

        def s0_act(act, link):
            layernorm_act(act, 0)
            for c in range(DT):
                act.wait_ge(s0_wqk_psum, c + 1)
                act.copy(WQK[:, c, :], PS[:, 4 + c, :]).then_inc(s0_wqk, 1)
            transpose_x_act(act, 0)
            for c in range(DT):
                act.wait_ge(s0_q_psum, c + 1)
                act.activation(QHI[:, c, :], PS[:, c, :], ACT.Copy, scale=Q_SCALE).then_inc(s0_q_hi, 1)
            with act.Fori(0, PAIRS) as i:
                for b in range(2):
                    c = i * 2 + b
                    act.wait_ge(s0_chunk[b], i * 16 + 16)
                    act.wait_ge(s0_scores, c * CH + 1)
                    act.copy(CHI[:, b], CR[:, b]).then_inc(s0_hi, 1)
                    for j in range(CH):
                        k = c * CH + j
                        act.wait_ge(s0_scores, k + 1 + AHEAD_TILES)
                        act.activation(ST[:, k, :], PS[:, b * CH + j, :], ACT.Copy).then_inc(s0_copied, 1)
            act.wait_ge(s0_mask, 1)
            with act.Fori(0, PAIRS) as i:
                for b in range(2):
                    c = i * 2 + b
                    act.wait_ge(s0_row[b], i * 16 + 16)
                    act.wait_ge(s0_pv, c * CH + 1)
                    for j in range(CH):
                        act.activation(CHI[:, b, j, :], CR[:, b, j, :], ACT.Copy,
                                       scale=MASK[:, bass.ds(c * CH + j, 1)]).then_inc(s0_c_hi, 1)
                    for j in range(CH):
                        k = c * CH + j
                        act.wait_ge(s0_shift, k + 1)
                        act.activation(ST[:, k, :], ST[:, k, :], ACT.Exp).then_inc(s0_exp, 1)
                        act.wait_ge(s0_exp, k + 1)
                        act.wait_ge(s0_pv, k + 4)
                        settle(act)
                        act.copy(PHI[:, j % 2, :], ST[:, k, :]).then_inc(s0_p_hi, 1)
            for c in range(DT):
                act.wait_ge(s0_z_psum, c + 1)
                act.copy(Z[:, c, :], PS[:, 4 + c, :]).then_inc(s0_z, 1)

        def s0_dve(dve, link):
            layernorm_dve(dve, 0, link)
            dve.wait_ge(mask_in, 16)
            dve.tensor_scalar(MASK[:, :], MASKI[:, :], 0.0, None, ALU.not_equal).then_inc(s0_mask, 1)
            for c in range(DT):
                dve.wait_ge(s0_q_hi, c + 1)
                dve.scalar_tensor_tensor(out=QLO[:, c, :], in0=PS[:, c, :], scalar=Q_SCALE, in1=QHI[:, c, :],
                                         op0=ALU.mult, op1=ALU.subtract).then_inc(s0_q_lo, 1)
            dve.memset(RUNMAX, -3.0e38).then_inc(s0_max, 1)
            with dve.Fori(0, PAIRS) as i:
                for b in range(2):
                    for j in range(CH):
                        k = (i * 2 + b) * CH + j
                        dve.wait_ge(s0_copied, k + 1 + AHEAD_BANK)
                        dve.wait_ge(s0_max, k + 1)
                        dve.tensor_tensor(RUNMAX, ST[:, k, :], RUNMAX, ALU.max).then_inc(s0_max, 1)
            dve.wait_ge(s0_mask, 1)
            dve.memset(PSUMS, 0.0).then_inc(s0_sum, 1)
            with dve.Fori(0, PAIRS) as i:
                for b in range(2):
                    c = i * 2 + b
                    dve.wait_ge(s0_pv, c * CH + 1)
                    for j in range(CH):
                        k = c * CH + j
                        dve.wait_ge(s0_c_hi, k + 1 + AHEAD_TILES)
                        dve.scalar_tensor_tensor(out=CLO[:, b, j, :], in0=CR[:, b, j, :],
                                                 scalar=MASK[:, bass.ds(k, 1)], in1=CHI[:, b, j, :],
                                                 op0=ALU.mult, op1=ALU.subtract).then_inc(s0_c_lo, 1)
                    for j in range(CH):
                        k = c * CH + j
                        dve.wait_ge(s0_p_hi, k + 1)
                        dve.wait_ge(s0_pv, k + 4)
                        dve.tensor_tensor(PLO[:, j % 2, :], ST[:, k, :], PHI[:, j % 2, :],
                                          ALU.subtract).then_inc(s0_p_lo, 1)
                        dve.wait_ge(s0_sum, k + 1)
                        dve.tensor_tensor(PSUMS, PSUMS, ST[:, k, :], ALU.add).then_inc(s0_sum, 1)
            dve.wait_ge(s0_den, 1)
            link(dve.reciprocal(COLS[:, 0:NT], PS[:, 4, 0:NT]))
            for t in range(NT):
                dve.tensor_scalar(O[:, t, :], PS[:, t, :], COLS[:, t:t + 1], None, ALU.mult).then_inc(s0_o, 1)
            dve.wait_ge(bias_in, 16)
            for t in range(NT):
                link(dve.tensor_tensor(X[:, t, :], X[:, t, :], BIAS, ALU.add))
            for t in range(NT):
                dve.wait_ge(out_psum, t + 1)
                dve.tensor_tensor(X[:, t, :], PS[:, t, :], X[:, t, :], ALU.add).then_inc(x_done, 1)

        def s0_pe(pe):
            pe.wait_ge(w_in[0], 32)
            for c in range(DT):
                for d in range(DT):
                    ins = pe.matmul(PS[:, 4 + c, :], WQ[:, d, c * P:(c + 1) * P], WK[:, d, :],
                                    start=(d == 0), stop=(d == DT - 1))
                ins.then_inc(s0_wqk_psum, 1)
            transpose_x_pe(pe, 0)
            pe.wait_ge(xt_ready, DT)
            pe.wait_ge(s0_wqk, DT)
            for e in range(DT):
                for c in range(DT):
                    ins = pe.matmul(PS[:, e, :], WQK[:, c, e * P:(e + 1) * P], XT[:, c, :],
                                    start=(c == 0), stop=(c == DT - 1))
                ins.then_inc(s0_q_psum, 1)
            pe.wait_ge(s0_q_hi, DT)
            pe.wait_ge(s0_q_lo, DT)
            with pe.Fori(0, PAIRS) as i:
                for b in range(2):
                    c = i * 2 + b
                    pe.wait_ge(s0_hi, c + 1 + AHEAD_SPLIT)
                    pe.wait_ge(s0_lo, c + 1 + AHEAD_SPLIT)
                    for j in range(CH):
                        k = c * CH + j
                        pe.wait_ge(s0_copied, k + 1)
                        bank = PS[:, b * CH + j, :]
                        cols = slice(j * P, (j + 1) * P)
                        for e in range(DT):
                            pe.matmul(bank, CHI[:, b, e, cols], QHI[:, e, :], start=(e == 0), stop=False)
                            pe.matmul(bank, CHI[:, b, e, cols], QLO[:, e, :], start=False, stop=False)
                            ins = pe.matmul(bank, CLO[:, b, e, cols], QHI[:, e, :], start=False,
                                            stop=(e == DT - 1))
                        ins.then_inc(s0_scores, 1)
            pe.wait_ge(s0_copied, MT + AHEAD_BANK)
            for t in range(NT):
                pe.matmul(PS[:, t, :], ZROW[:, 0:P], ZROW[:, :], start=True, stop=False)
            with pe.Fori(0, PAIRS) as i:
                for b in range(2):
                    for j in range(CH):
                        k = (i * 2 + b) * CH + j
                        pe.wait_ge(s0_c_hi, k + 1 + AHEAD_TILES)
                        pe.wait_ge(s0_c_lo, k + 1 + AHEAD_TILES)
                        pe.wait_ge(s0_p_hi, k + 1)
                        pe.wait_ge(s0_p_lo, k + 1)
                        for t in range(NT):
                            cols = slice(t * P, (t + 1) * P)
                            pe.matmul(PS[:, t, :], PHI[:, j % 2, cols], CHI[:, b, j, :], start=False, stop=False)
                            pe.matmul(PS[:, t, :], PHI[:, j % 2, cols], CLO[:, b, j, :], start=False, stop=False)
                            ins = pe.matmul(PS[:, t, :], PLO[:, j % 2, cols], CHI[:, b, j, :], start=False, stop=False)
                        ins.then_inc(s0_pv, 1)
            for t in range(NT):
                ins = pe.matmul(PS[:, t, :], ZROW[:, 0:P], ZROW[:, :], start=False, stop=True)
            ins.then_inc(s0_close, 1)
            pe.wait_ge(s0_sum, MT + 1)
            for t in range(NT):
                ins = pe.matmul(PS[:, 4, t:t + 1], PSUMS[:, t * P:(t + 1) * P], ONES[:, 0:1], start=True, stop=True)
            ins.then_inc(s0_den, 1)
            pe.wait_ge(w_in[0], 64)
            pe.wait_ge(s0_o, NT)
            for c in range(DT):
                for t in range(NT):
                    ins = pe.matmul(PS[:, 4 + c, :], O[:, t, c * P:(c + 1) * P], PROJT[:, t, :],
                                    start=(t == 0), stop=(t == NT - 1))
                ins.then_inc(s0_z_psum, 1)
            pe.wait_ge(s0_z, DT)
            for t in range(NT):
                for c in range(DT):
                    ins = pe.matmul(PS[:, t, :], WVT[:, c, t * P:(t + 1) * P], Z[:, c, :],
                                    start=(c == 0), stop=(c == DT - 1))
                ins.then_inc(out_psum, 1)

        RW = view(0, [4, DT, D])
        STATE = view(32 * K, [DT, N])
        Y = view(40 * K, [DT, N])
        GATE = view(48 * K, [DT, N])
        SQ = view(56 * K, [DT, N])
        RSTDB = view(64 * K, [N])
        LAM, LNG, LNB = SM[:, 0:DT], SM[:, DT:2 * DT], SM[:, 2 * DT:3 * DT]

        s1_proj = sem("s1_proj")
        s1_state = sem("s1_state")
        s1_y = sem("s1_y")
        s1_gate = sem("s1_gate")
        s1_mean = sem("s1_mean")
        s1_cent = sem("s1_cent")
        s1_sq = sem("s1_sq")
        s1_var = sem("s1_var")
        s1_std = sem("s1_std")
        s1_rstd = sem("s1_rstd")
        s1_mod = sem("s1_mod")

        def s1_sp(sp):
            sp.wait_ge(x_done, NT * (1 - first))
            for n, name in enumerate(("WvT", "WqT", "WgT", "WoT")):
                sp.dma_start(RW[:, n], a[name].rearrange("(t p) c -> p t c", p=P)).then_inc(w_in[1], 16)
            for dst, name in ((LAM, "lam"), (LNG, "lng"), (LNB, "lnb")):
                sp.dma_start(dst, a[name]).then_inc(w_in[1], 16)

        def s1_pool(pool, link):
            pass

        def s1_act(act, link):
            layernorm_act(act, 1)
            transpose_x_act(act, 1)
            for e in range(DT):
                act.wait_ge(s1_proj, 3 * e + 3)
                act.activation(GATE[:, e, :], PS[:, (3 * e + 2) % 8, :], ACT.Silu).then_inc(s1_gate, 1)
            for e in range(DT):
                act.wait_ge(s1_cent, e + 1)
                act.activation(SQ[:, e, :], Y[:, e, :], ACT.Square).then_inc(s1_sq, 1)
            act.wait_ge(s1_var, 1)
            act.activation(RSTDB, PS[:, 5, :], ACT.Sqrt, bias=EPSC[:, 0:1]).then_inc(s1_std, 1)

        def s1_dve(dve, link):
            layernorm_dve(dve, 1, link)
            dve.wait_ge(w_in[1], 7 * 16)
            for e in range(DT):
                dve.wait_ge(s1_proj, 3 * e + 1)
                dve.tensor_tensor_scan(STATE[:, e, :], LAM[:, e:e + 1].to_broadcast([P, N]), PS[:, (3 * e) % 8, :],
                                       0.0, ALU.mult, ALU.add).then_inc(s1_state, 1)
                dve.wait_ge(s1_state, e + 1)
                dve.wait_ge(s1_proj, 3 * e + 2)
                dve.tensor_tensor(Y[:, e, :], PS[:, (3 * e + 1) % 8, :], STATE[:, e, :],
                                  ALU.mult).then_inc(s1_y, 1)
            dve.wait_ge(s1_y, DT)
            dve.wait_ge(s1_mean, 1)
            for e in range(DT):
                dve.tensor_tensor(Y[:, e, :], Y[:, e, :], PS[:, 4, :], ALU.subtract).then_inc(s1_cent, 1)
            dve.wait_ge(s1_std, 1)
            dve.reciprocal(RSTDB, RSTDB).then_inc(s1_rstd, 1)
            dve.wait_ge(s1_rstd, 1)
            dve.wait_ge(s1_gate, DT)
            for e in range(DT):
                link(dve.scalar_tensor_tensor(out=Y[:, e, :], in0=Y[:, e, :], scalar=LNG[:, e:e + 1], in1=RSTDB,
                                              op0=ALU.mult, op1=ALU.mult))
                dve.scalar_tensor_tensor(out=Y[:, e, :], in0=Y[:, e, :], scalar=LNB[:, e:e + 1], in1=GATE[:, e, :],
                                         op0=ALU.add, op1=ALU.mult).then_inc(s1_mod, 1)
            for t in range(NT):
                dve.wait_ge(out_psum, NT * (1 - first) + t + 1)
                dve.tensor_tensor(X[:, t, :], PS[:, t, :], X[:, t, :], ALU.add).then_inc(x_done, 1)

        def s1_pe(pe):
            transpose_x_pe(pe, 1)
            pe.wait_ge(xt_ready, DT * (2 - first))
            pe.wait_ge(w_in[1], 7 * 16)
            for e in range(DT):
                for n in range(3):
                    g = 3 * e + n
                    if g >= 8:
                        pe.wait_ge((s1_state, s1_y, s1_gate)[(g - 8) % 3], (g - 8) // 3 + 1)
                    for c in range(DT):
                        ins = pe.matmul(PS[:, g % 8, :], RW[:, n, c, e * P:(e + 1) * P], XT[:, c, :],
                                        start=(c == 0), stop=(c == DT - 1))
                    ins.then_inc(s1_proj, 1)
            pe.wait_ge(s1_y, DT)
            pe.wait_ge(s1_gate, DT)
            for e in range(DT):
                ins = pe.matmul(PS[:, 4, :], MEANW[:, :], Y[:, e, :], start=(e == 0), stop=(e == DT - 1))
            ins.then_inc(s1_mean, 1)
            for e in range(DT):
                pe.wait_ge(s1_sq, e + 1)
                ins = pe.matmul(PS[:, 5, :], MEANW[:, :], SQ[:, e, :], start=(e == 0), stop=(e == DT - 1))
            ins.then_inc(s1_var, 1)
            pe.wait_ge(s1_mod, DT)
            for t in range(NT):
                for e in range(DT):
                    ins = pe.matmul(PS[:, t, :], Y[:, e, t * P:(t + 1) * P], RW[:, 3, e, :],
                                    start=(e == 0), stop=(e == DT - 1))
                ins.then_inc(out_psum, 1)

        FW = view(0, [3, F0T * D])
        FRAW = view(72 * K, [F0T * D])
        UP = view(96 * K, [F0T, N])
        GT = view(120 * K, [F0T, N])
        SG = view(144 * K, [F0T, N])
        NBLK = F0T * D // QB
        BSC = view(168 * K, [NBLK])
        BRC = view(169 * K, [NBLK])
        UPW = FW[:, 0].rearrange("p (t o) -> p t o", t=DT)
        GTW = FW[:, 1].rearrange("p (t o) -> p t o", t=DT)
        DNW = FW[:, 2].rearrange("p (t o) -> p t o", t=F0T)
        AM = COLS[:, 8:13]
        AR = COLS[:, 16:21]
        SC = COLS[:, 24:29]
        RC = COLS[:, 32:37]

        s2_raw = sem("s2_raw")
        s2_rawfree = sem("s2_rawfree")
        s2_w = sem("s2_w")
        s2_mag = sem("s2_mag")
        s2_all = sem("s2_all")
        s2_up_psum = sem("s2_up_psum")
        s2_up = sem("s2_up")
        s2_gt_psum = sem("s2_gt_psum")
        s2_gt = sem("s2_gt")
        s2_gtq = sem("s2_gtq")
        s2_sig = sem("s2_sig")
        s2_h = sem("s2_h")

        def s2_sp(sp):
            sp.wait_ge(x_done, NT * (2 - first))
            for n, name in enumerate(("upB", "gateB", "downB")):
                if n:
                    sp.wait_ge(s2_rawfree, n)
                sp.dma_start(FRAW, a[name]).then_inc(s2_raw, 16)

        def s2_pool(pool, link):
            for n in range(5):
                pool.wait_ge(s2_mag, n + 1)
                pool.partition_all_reduce(AR[:, n:n + 1], AM[:, n:n + 1], P, RMAX).then_inc(s2_all, 1)

        def s2_act(act, link):
            layernorm_act(act, 2)
            transpose_x_act(act, 2)
            for g in range(F0T):
                act.wait_ge(s2_up_psum, g + 1)
                act.copy(UP[:, g, :], PS[:, (2 * g) % 8, :]).then_inc(s2_up, 1)
            act.wait_ge(s2_gtq, 1)
            act.activation(SG, GT, ACT.Sigmoid).then_inc(s2_sig, 1)

        def s2_dve(dve, link):
            def scale_of(n, qmax):
                dve.wait_ge(s2_all, n + 1)
                link(dve.tensor_scalar(SC[:, n:n + 1], AR[:, n:n + 1], 1.0 / qmax, 1e-12, ALU.mult, ALU.max))
                link(dve.reciprocal(RC[:, n:n + 1], SC[:, n:n + 1]))

            def quantise(v, n):
                link(dve.tensor_scalar(v, v, RC[:, n:n + 1], ROUND, ALU.mult, ALU.add))
                return dve.tensor_scalar(v, v, ROUND, SC[:, n:n + 1], ALU.subtract, ALU.mult)

            def magnitude(n, v):
                dve.tensor_reduce(AM[:, n:n + 1], v, AX.XY, ALU.max, apply_absolute_value=True).then_inc(s2_mag, 1)

            def dequantise(n):
                dve.wait_ge(s2_raw, 16 * (n + 1))
                w = FRAW.rearrange("p (k s) -> p k s", s=QB)
                link(dve.tensor_reduce(BSC, w, AX.X, ALU.max, apply_absolute_value=True))
                link(dve.tensor_scalar(BSC, BSC, 1.0 / 7.0, 1e-12, ALU.mult, ALU.max))
                link(dve.reciprocal(BRC, BSC))
                link(dve.tensor_tensor(w, w, BRC.unsqueeze(2).to_broadcast([P, NBLK, QB]), ALU.mult))
                link(dve.tensor_scalar(FRAW, FRAW, ROUND, ROUND, ALU.add, ALU.subtract))
                link(dve.tensor_tensor(w, w, BSC.unsqueeze(2).to_broadcast([P, NBLK, QB]), ALU.mult))
                dve.transpose(FW[:, n, :], FRAW).then_inc(s2_w, 1)
                dve.wait_ge(s2_w, n + 1)
                dve.sem_inc(s2_rawfree, 1)

            layernorm_dve(dve, 2, link, finish=False)
            link.wait()
            magnitude(0, XN[:, :, :])
            scale_of(0, 32767.0)
            link(dve.tensor_scalar(XN[:, :, :], XN[:, :, :], RC[:, 0:1], ROUND, ALU.mult, ALU.add))
            for t in range(NT):
                dve.tensor_scalar(XN[:, t, :], XN[:, t, :], ROUND, SC[:, 0:1], ALU.subtract, ALU.mult).then_inc(ln_xn, 1)
            for n in range(3):
                dequantise(n)
            for g in range(F0T):
                dve.wait_ge(s2_gt_psum, g + 1)
                dve.tensor_copy(GT[:, g, :], PS[:, (2 * g + 1) % 8, :]).then_inc(s2_gt, 1)
            dve.wait_ge(s2_gt, F0T)
            magnitude(2 - 1, GT)
            dve.wait_ge(s2_up, F0T)
            magnitude(2, UP)
            scale_of(1, 32767.0)
            quantise(GT, 1).then_inc(s2_gtq, 1)
            scale_of(2, 32767.0)
            link(quantise(UP, 2))
            dve.wait_ge(s2_gtq, 1)
            dve.wait_ge(s2_sig, 1)
            link(dve.tensor_scalar(SG, SG, 65536.0, ROUND, ALU.mult, ALU.add))
            link(dve.tensor_scalar(SG, SG, ROUND, 65535.0, ALU.subtract, ALU.min))
            link(dve.scalar_tensor_tensor(out=GT, in0=SG, scalar=1.0 / 65536.0, in1=GT, op0=ALU.mult, op1=ALU.mult))
            magnitude(3, GT)
            scale_of(3, 32767.0)
            link(quantise(GT, 3))
            link(dve.tensor_tensor(GT, GT, UP, ALU.mult))
            magnitude(4, GT)
            scale_of(4, 32767.0)
            quantise(GT, 4).then_inc(s2_h, 1)
            for t in range(NT):
                dve.wait_ge(out_psum, NT * (2 - first) + t + 1)
                dve.tensor_tensor(X[:, t, :], PS[:, t, :], X[:, t, :], ALU.add).then_inc(x_done, 1)

        def s2_pe(pe):
            transpose_x_pe(pe, 2)
            pe.wait_ge(xt_ready, DT * (3 - first))
            pe.wait_ge(s2_w, 2)
            for g in range(F0T):
                if g >= 4:
                    pe.wait_ge(s2_up, g - 3)
                    pe.wait_ge(s2_gt, g - 3)
                for w, bank, done in ((UPW, (2 * g) % 8, s2_up_psum), (GTW, (2 * g + 1) % 8, s2_gt_psum)):
                    for c in range(DT):
                        ins = pe.matmul(PS[:, bank, :], w[:, c, g * P:(g + 1) * P], XT[:, c, :],
                                        start=(c == 0), stop=(c == DT - 1))
                    ins.then_inc(done, 1)
            pe.wait_ge(s2_w, 3)
            pe.wait_ge(s2_h, 1)
            for t in range(NT):
                for g in range(F0T):
                    ins = pe.matmul(PS[:, t, :], GT[:, g, t * P:(t + 1) * P], DNW[:, g, :],
                                    start=(g == 0), stop=(g == F0T - 1))
                ins.then_inc(out_psum, 1)

        WQ1 = view(0, [DT, D])
        WK1 = view(8 * K, [DT, P])
        WV1 = view(10 * K, [DT, DH])
        WC1 = view(12 * K, [DT, D])
        QS = view(20 * K, [DT, N])
        MEM = view(28 * K, [NT, D])
        MEMT = view(36 * K, [DT, N])
        MKT = view(44 * K, [N])
        MVAL = view(46 * K, [NT, DH])
        PB = view(48 * K, [3, N])
        PTB = view(54 * K, [4, NT, P])
        ATT = view(62 * K, [NT, D])
        ATTT = view(70 * K, [DT, N])
        TOP8 = view(78 * K, [2, NT, 8])
        IDX8 = view(79 * K, [2, NT, 8], U32)
        TOPV = view(80 * K, [NCH, NT])
        TOPI = view(81 * K, [NCH, NT])
        FROM_END = view(82 * K, [NCH, NT], I32)
        FROM_ENDF = view(83 * K, [NCH, NT])
        BEST = view(84 * K, [NT])
        MEMIDX = view(85 * K, [NT], U32)
        NMAX = view(86 * K, [NT * ATT_H])
        RS3 = view(87 * K, [NT, ATT_H])
        UNITS = NT * ATT_H

        s3_q_psum = sem("s3_q_psum")
        s3_q_hi = sem("s3_q_hi")
        s3_q_lo = sem("s3_q_lo")
        s3_qs = sem("s3_qs")
        s3_chunk = [sem("s3_chunk0"), sem("s3_chunk1")]
        s3_hi = sem("s3_hi")
        s3_lo = sem("s3_lo")
        s3_scores = sem("s3_scores")
        s3_max = sem("s3_max")
        s3_idx = sem("s3_idx")
        s3_iota = sem("s3_iota")
        s3_memidx = sem("s3_memidx")
        s3_mem = sem("s3_mem")
        s3_memt_psum = sem("s3_memt_psum")
        s3_memt = sem("s3_memt")
        s3_kv_psum = sem("s3_kv_psum")
        s3_kv = sem("s3_kv")
        s3_logits = sem("s3_logits")
        s3_nmax = sem("s3_nmax")
        s3_p = sem("s3_p")
        s3_pt_psum = sem("s3_pt_psum")
        s3_pt = [sem("s3_pt_even"), sem("s3_pt_odd")]
        s3_pv = sem("s3_pv")
        s3_att = sem("s3_att")
        s3_attt_psum = sem("s3_attt_psum")
        s3_attt = sem("s3_attt")
        s3_primed = sem("s3_primed")

        def s3_sp(sp):
            sp.wait_ge(x_done, NT * (3 - first))
            sp.dma_start(WQ1, a["Wq1T"].rearrange("(t p) c -> p t c", p=P)).then_inc(w_in[3], 16)
            sp.dma_start(WK1, a["Wk1T"].rearrange("(t p) c -> p t c", p=P)).then_inc(w_in[3], 16)
            sp.dma_start(WV1, a["Wv1T"].rearrange("(t p) c -> p t c", p=P)).then_inc(w_in[3], 16)
            sp.dma_start(WC1, a["Wc1T"].rearrange("(t p) c -> p t c", p=P)).then_inc(w_in[3], 16)
            sp.wait_ge(s3_primed, 1)
            with sp.Fori(0, PAIRS) as i:
                for b in range(2):
                    sp.wait_ge(s3_hi, i * 2 + b + 1)
                    sp.wait_ge(s3_lo, i * 2 + b + 1)
                    sp.dma_start(CR[:, b], a["ctxT"][i * 2 + b]).then_inc(s3_chunk[b], 16)

        def s3_pool(pool, link):
            pool.sem_inc(s3_hi, AHEAD_SPLIT)
            pool.sem_inc(s3_lo, AHEAD_SPLIT)
            pool.sem_inc(s3_scores, AHEAD_TILES)
            pool.sem_inc(s3_idx, AHEAD_BANK)
            pool.sem_inc(s3_primed, 1)
            pool.wait_ge(x_done, NT * (3 - first))
            pool.iota(FROM_END, pattern=[[-CH * P, NCH], [0, NT]], base=M, channel_multiplier=0).then_inc(s3_iota, 1)
            with pool.Fori(0, PAIRS) as i:
                for b in range(2):
                    pool.wait_ge(s3_hi, i * 2 + b + 1 + AHEAD_SPLIT)
                    pool.wait_ge(s3_scores, (i * 2 + b) * CH + 1)
                    pool.tensor_tensor(CLO[:, b], CR[:, b], CHI[:, b], ALU.subtract).then_inc(s3_lo, 1)
            for t in range(NT):
                pool.wait_ge(s3_memidx, 1)
                pool.indirect_dma_start(out=MEM[:, t, :], out_offset=None, in_=a["ctx"],
                                        in_offset=bass.IndirectOffsetOnAxis(ap=MEMIDX[:, t:t + 1], axis=0)
                                        ).then_inc(s3_mem, 16)

        def s3_act(act, link):
            layernorm_act(act, 3)
            transpose_x_act(act, 3)
            for e in range(DT):
                act.wait_ge(s3_q_psum, e + 1)
                act.copy(QHI[:, e, :], PS[:, 4 + e, :]).then_inc(s3_q_hi, 1)
                act.wait_ge(s3_q_lo, e + 1)
                act.activation(QS[:, e, :], PS[:, 4 + e, :], ACT.Copy, scale=float(DH) ** -0.5).then_inc(s3_qs, 1)
            with act.Fori(0, PAIRS) as i:
                for b in range(2):
                    act.wait_ge(s3_chunk[b], i * 16 + 16)
                    act.wait_ge(s3_scores, (i * 2 + b) * CH + 1)
                    act.copy(CHI[:, b], CR[:, b]).then_inc(s3_hi, 1)
            for c in range(DT):
                act.wait_ge(s3_memt_psum, c + 1)
                act.copy(MEMT[:, c, :], PS[:, c, :]).then_inc(s3_memt, 1)

            def turn(u):
                act.wait_ge(s3_pt_psum, u + 1)
                if u >= 4:
                    act.wait_ge(s3_pv, u - 3)
                act.copy(PTB[:, u % 4].rearrange("p a b -> p (a b)"), PS[:, 4 + u % 2, :]).then_inc(s3_pt[1], 1)

            for u in range(UNITS):
                act.wait_ge(s3_nmax, u + 1)
                if u >= 3:
                    act.wait_ge(s3_pt_psum, u - 2)
                act.activation(PB[:, u % 3, :], PS[:, u % 4, :], ACT.Exp, bias=NMAX[:, u:u + 1],
                               accum_out=RS3[:, u // ATT_H, u % ATT_H:u % ATT_H + 1]).then_inc(s3_p, 1)
                if u >= 1 and (u - 1) % 2:
                    turn(u - 1)
            turn(UNITS - 1)
            for c in range(DT):
                act.wait_ge(s3_attt_psum, c + 1)
                act.copy(ATTT[:, c, :], PS[:, c, :]).then_inc(s3_attt, 1)

        def s3_dve(dve, link):
            layernorm_dve(dve, 3, link)
            for e in range(DT):
                dve.wait_ge(s3_q_hi, e + 1)
                dve.tensor_tensor(QLO[:, e, :], PS[:, 4 + e, :], QHI[:, e, :], ALU.subtract).then_inc(s3_q_lo, 1)
            with dve.Fori(0, PAIRS) as i:
                for b in range(2):
                    c = i * 2 + b
                    for t in range(NT):
                        dve.wait_ge(s3_scores, c * CH + t + 1 + AHEAD_TILES)
                        settle(dve)
                        dve.max(TOP8[:, b, t, :], PS[:, b * CH + t, :]).then_inc(s3_max, 1)
                    for t in range(NT):
                        dve.wait_ge(s3_max, c * CH + t + 1)
                        settle(dve)
                        dve.max_index(IDX8[:, b, t, :], TOP8[:, b, t, :], PS[:, b * CH + t, :]).then_inc(s3_idx, 1)
                    dve.tensor_copy(TOPV[:, c, :], TOP8[:, b, :, 0])
                    dve.wait_ge(s3_idx, c * CH + CH + AHEAD_BANK)
                    dve.tensor_copy(TOPI[:, c, :], IDX8[:, b, :, 0])
            dve.wait_ge(s3_iota, 1)
            link(dve.tensor_copy(FROM_ENDF, FROM_END))
            link(dve.tensor_reduce(BEST, TOPV.rearrange("p c t -> p t c"), AX.X, ALU.max))
            link(dve.tensor_tensor(TOPI, FROM_ENDF, TOPI, ALU.subtract))
            link(dve.tensor_tensor(TOPV, TOPV, BEST.unsqueeze(1).to_broadcast([P, NCH, NT]), ALU.is_equal))
            link(dve.tensor_tensor(TOPI, TOPI, TOPV, ALU.mult))
            link(dve.tensor_reduce(BEST, TOPI.rearrange("p c t -> p t c"), AX.X, ALU.max))
            dve.tensor_scalar(MEMIDX, BEST, -1.0, float(M), ALU.mult, ALU.add).then_inc(s3_memidx, 1)
            dve.wait_ge(s3_kv_psum, 2)
            dve.tensor_copy(MKT, PS[:, 4, :]).then_inc(s3_kv, 1)
            dve.tensor_copy(MVAL.rearrange("p a b -> p (a b)"), PS[:, 5, 0:NT * DH]).then_inc(s3_kv, 1)

            def turn(u):
                dve.wait_ge(s3_pt_psum, u + 1)
                if u >= 4:
                    dve.wait_ge(s3_pv, u - 3)
                dve.tensor_copy(PTB[:, u % 4].rearrange("p a b -> p (a b)"), PS[:, 4 + u % 2, :]).then_inc(s3_pt[0], 1)

            def norm(t):
                dve.wait_ge(s3_pv, ATT_H * (t + 1))
                link(dve.reciprocal(RS3[:, t, :], RS3[:, t, :]))
                dve.tensor_tensor(ATT[:, t, :].rearrange("p (h d) -> p h d", h=ATT_H),
                                  PS[:, 6 + t % 2, :].rearrange("p (h d) -> p h d", h=ATT_H),
                                  RS3[:, t, :].unsqueeze(2).to_broadcast([P, ATT_H, DH]),
                                  ALU.mult).then_inc(s3_att, 1)

            for u in range(UNITS):
                dve.wait_ge(s3_logits, u + 1)
                dve.tensor_reduce(NMAX[:, u:u + 1], PS[:, u % 4, :], AX.X, ALU.max, negate=True).then_inc(s3_nmax, 1)
                if u >= 1 and (u - 1) % 2 == 0:
                    turn(u - 1)
                if u >= ATT_H and u % ATT_H == 3:
                    norm(u // ATT_H - 1)
            norm(NT - 1)
            for t in range(NT):
                dve.wait_ge(out_psum, NT * (3 - first) + t + 1)
                dve.tensor_tensor(X[:, t, :], PS[:, 4 + t, :], X[:, t, :], ALU.add).then_inc(x_done, 1)

        def s3_pe(pe):
            transpose_x_pe(pe, 3)
            pe.wait_ge(xt_ready, DT * (4 - first))
            pe.wait_ge(w_in[3], 64)
            for e in range(DT):
                for c in range(DT):
                    ins = pe.matmul(PS[:, 4 + e, :], WQ1[:, c, e * P:(e + 1) * P], XT[:, c, :],
                                    start=(c == 0), stop=(c == DT - 1))
                ins.then_inc(s3_q_psum, 1)
            pe.wait_ge(s3_q_lo, DT)
            pe.wait_ge(s3_qs, DT)
            with pe.Fori(0, PAIRS) as i:
                for b in range(2):
                    c = i * 2 + b
                    pe.wait_ge(s3_hi, c + 1 + AHEAD_SPLIT)
                    pe.wait_ge(s3_lo, c + 1 + AHEAD_SPLIT)
                    for t in range(NT):
                        pe.wait_ge(s3_idx, c * CH + t + 1)
                        bank = PS[:, b * CH + t, :]
                        cols = slice(t * P, (t + 1) * P)
                        for e in range(DT):
                            pe.matmul(bank, QHI[:, e, cols], CHI[:, b, e, :], start=(e == 0), stop=False)
                            pe.matmul(bank, QHI[:, e, cols], CLO[:, b, e, :], start=False, stop=False)
                            ins = pe.matmul(bank, QLO[:, e, cols], CHI[:, b, e, :], start=False,
                                            stop=(e == DT - 1))
                        ins.then_inc(s3_scores, 1)
            pe.wait_ge(s3_idx, MT + AHEAD_BANK)
            pe.wait_ge(s3_mem, 16 * NT)
            for c in range(DT):
                for t in range(NT):
                    ins = pe.transpose(PS[:, c, t * P:(t + 1) * P], MEM[:, t, c * P:(c + 1) * P], IDENT[:, :])
                ins.then_inc(s3_memt_psum, 1)
            pe.wait_ge(s3_memt, DT)
            for c in range(DT):
                ins = pe.matmul(PS[:, 4, :], WK1[:, c, :], MEMT[:, c, :], start=(c == 0), stop=(c == DT - 1))
            ins.then_inc(s3_kv_psum, 1)
            for t in range(NT):
                for c in range(DT):
                    ins = pe.matmul(PS[:, 5, t * DH:(t + 1) * DH], MEMT[:, c, t * P:(t + 1) * P], WV1[:, c, :],
                                    start=(c == 0), stop=(c == DT - 1))
            ins.then_inc(s3_kv_psum, 1)
            pe.wait_ge(s3_kv, 2)

            def logits(u):
                t, h = u // ATT_H, u % ATT_H
                rows = slice(DH * (h % 4), DH * (h % 4) + DH)
                if u >= 4:
                    pe.wait_ge(s3_p, u - 3)
                pe.matmul(PS[:, u % 4, :], QS[rows, h // 4, t * P:(t + 1) * P], MKT[rows, :],
                          start=True, stop=True).then_inc(s3_logits, 1)

            def turn(u):
                pe.wait_ge(s3_p, u + 1)
                if u >= 2:
                    pe.wait_ge(s3_pt[u % 2], u // 2)
                for m in range(NT):
                    ins = pe.transpose(PS[:, 4 + u % 2, m * P:(m + 1) * P], PB[:, u % 3, m * P:(m + 1) * P],
                                       IDENT[:, :])
                ins.then_inc(s3_pt_psum, 1)

            def weigh(u):
                t, h = u // ATT_H, u % ATT_H
                pe.wait_ge(s3_pt[u % 2], u // 2 + 1)
                if t >= 2:
                    pe.wait_ge(s3_att, t - 1)
                for m in range(NT):
                    ins = pe.matmul(PS[:, 6 + t % 2, h * DH:(h + 1) * DH], PTB[:, u % 4, m, :], MVAL[:, m, :],
                                    start=(m == 0), stop=(m == NT - 1))
                ins.then_inc(s3_pv, 1)

            for u in range(UNITS + 2):
                if u < UNITS:
                    logits(u)
                if 1 <= u <= UNITS:
                    turn(u - 1)
                if u >= 2:
                    weigh(u - 2)
            pe.wait_ge(s3_att, NT)
            for c in range(DT):
                for t in range(NT):
                    ins = pe.transpose(PS[:, c, t * P:(t + 1) * P], ATT[:, t, c * P:(c + 1) * P], IDENT[:, :])
                ins.then_inc(s3_attt_psum, 1)
            pe.wait_ge(s3_attt, DT)
            for t in range(NT):
                for c in range(DT):
                    ins = pe.matmul(PS[:, 4 + t, :], ATTT[:, c, t * P:(t + 1) * P], WC1[:, c, :],
                                    start=(c == 0), stop=(c == DT - 1))
                ins.then_inc(out_psum, 1)

        WIN = view(0, [DT, PROJ])
        WOUT = view(37 * K, [IT, D])
        XBC = view(53 * K, [CVT, N + 3])
        CV = view(74 * K, [CVT, N])
        ZG = view(94 * K, [NT, SSM_I])
        YS = view(110 * K, [NT, SSM_I])
        DTX = view(126 * K, [SSM_I])
        WDTX = view(130 * K, [SSM_I])
        DECAY = view(134 * K, [SSM_H, P])
        BNAT = view(142 * K, [P])
        HS = view(143 * K, [SSM_I])
        TMP = view(147 * K, [SSM_I])
        YT = view(151 * K, [IT, N])
        SMALL = 167 * K
        CONVW = view(SMALL, [CVT, 4])
        CONVB = view(SMALL + 256, [CVT])
        DTB = view(SMALL + 512, [SSM_H])
        ALOG = view(SMALL + 768, [SSM_H])
        SSMD = view(SMALL + 1024, [SSM_H])
        NORMW = view(SMALL + 1280, [IT])
        DTV = view(SMALL + 1536, [NT, SSM_H])
        DTA = view(SMALL + 1792, [NT, SSM_H])
        DTE = view(SMALL + 2048, [NT, SSM_H])
        LA = view(SMALL + 2304, [3, SSM_H])
        ELA = view(SMALL + 2560, [3, SSM_H])
        NLA = view(SMALL + 2816, [SSM_H])
        MS = view(SMALL + 3072, [NT])
        RMS = view(SMALL + 3328, [NT])

        s4_conv_psum = sem("s4_conv_psum")
        s4_conv_in = sem("s4_conv_in")
        s4_pad = sem("s4_pad")
        s4_conv = sem("s4_conv")
        s4_cv = sem("s4_cv")
        s4_dt_psum = sem("s4_dt_psum")
        s4_dtb = sem("s4_dtb")
        s4_softplus = sem("s4_softplus")
        s4_dta = sem("s4_dta")
        s4_z_psum = sem("s4_z_psum")
        s4_z = sem("s4_z")
        s4_small = sem("s4_small")
        s4_read = sem("s4_read")
        s4_la = sem("s4_la")
        s4_ela = sem("s4_ela")
        s4_decay_psum = sem("s4_decay_psum")
        s4_decay = sem("s4_decay")
        s4_mix = sem("s4_mix")
        s4_wdtx = sem("s4_wdtx")
        s4_intra = sem("s4_intra")
        s4_inter = sem("s4_inter")
        s4_add = sem("s4_add")
        s4_state = sem("s4_state")
        s4_hs = sem("s4_hs")
        s4_ys = sem("s4_ys")
        s4_ms = sem("s4_ms")
        s4_rms = sem("s4_rms")
        s4_yn = sem("s4_yn")
        s4_yt_psum = sem("s4_yt_psum")
        s4_yt = sem("s4_yt")

        def heads(v, n=SSM_H):
            return v.rearrange("p (h c) -> p h c", h=n)

        def s4_sp(sp):
            sp.wait_ge(x_done, NT * (4 - first))
            sp.dma_start(WIN, a["WinT"].rearrange("(t p) c -> p t c", p=P)).then_inc(w_in[4], 16)
            sp.dma_start(WOUT, a["WoutT"].rearrange("(t p) c -> p t c", p=P)).then_inc(w_in[4], 16)
            for dst, name in ((CONVW, "convw"), (CONVB, "convb"), (NORMW, "normw")):
                sp.dma_start(dst, a[name]).then_inc(w_in[4], 16)
            for dst, name in ((DTB, "dtb"), (ALOG, "alog"), (SSMD, "ssmd")):
                sp.dma_start(dst, a[name].partition_broadcast(P)).then_inc(w_in[4], 16)

        def s4_pool(pool, link):
            pool.wait_ge(x_done, NT * (4 - first))
            pool.memset(XBC[:, :, 0:3], 0.0).then_inc(s4_pad, 1)

        def s4_act(act, link):
            layernorm_act(act, 4)
            transpose_x_act(act, 4)
            for g in range(CVT):
                act.wait_ge(s4_conv_psum, g + 1)
                act.copy(XBC[:, g, 3:], PS[:, g % 4, :]).then_inc(s4_conv_in, 1)
            act.wait_ge(s4_dtb, 1)
            link(act.activation(DTE, DTV, ACT.Abs))
            link(act.activation(DTE, DTE, ACT.Exp, scale=-1.0))
            link(act.activation(ALOG, ALOG, ACT.Exp))
            act.activation(DTE, DTE, ACT.Ln, bias=1.0).then_inc(s4_softplus, 1)
            for g in range(CVT):
                act.wait_ge(s4_conv, g + 1)
                act.activation(CV[:, g, :], CV[:, g, :], ACT.Silu).then_inc(s4_cv, 1)
            for g in range(2 * NT):
                act.wait_ge(s4_z_psum, g + 1)
                act.activation(ZG[:, g // 2, (g % 2) * 512:(g % 2 + 1) * 512], PS[:, 4 + g % 2, :],
                               ACT.Silu).then_inc(s4_z, 1)
            for q in range(NT):
                act.wait_ge(s4_la, q + 1)
                act.activation(ELA, LA, ACT.Exp).then_inc(s4_ela, 1)
                if q:
                    act.wait_ge(s4_intra, q)
                for h in range(SSM_H):
                    act.wait_ge(s4_decay_psum, (SSM_H * q + h) // 4 + 1)
                    ins = act.activation(DECAY[:, h, :], PS[:, 4 + h // 4, (h % 4) * P:(h % 4 + 1) * P], ACT.Exp,
                                         bias=NLA[:, h:h + 1])
                    if h % 4 == 3:
                        ins.then_inc(s4_decay, 1)
            for q in range(NT):
                act.wait_ge(s4_ys, q + 1)
                act.activation(YT[:, 0:2, :].rearrange("p a b -> p (a b)"), YS[:, q, :], ACT.Square, accum_out=MS[:, q:q + 1]).then_inc(s4_ms, 1)
                act.wait_ge(s4_ms, q + 1)
            act.activation(RMS, MS, ACT.Sqrt, scale=1.0 / SSM_I, bias=EPSC[:, 0:1]).then_inc(s4_rms, 1)
            for c in range(IT):
                act.wait_ge(s4_yt_psum, c + 1)
                act.activation(YT[:, c, :], PS[:, c % 4, :], ACT.Copy, scale=NORMW[:, c:c + 1]).then_inc(s4_yt, 1)

        def s4_dve(dve, link):
            layernorm_dve(dve, 4, link)
            dve.wait_ge(w_in[4], 8 * 16)
            dve.wait_ge(s4_dt_psum, 1)
            dve.tensor_tensor(DTV, PS[:, 6, 0:NT * SSM_H].rearrange("p (t h) -> p t h", t=NT),
                              DTB.unsqueeze(1).to_broadcast([P, NT, SSM_H]), ALU.add).then_inc(s4_dtb, 1)
            dve.wait_ge(s4_softplus, 1)
            link(dve.scalar_tensor_tensor(out=DTV, in0=DTV, scalar=0.0, in1=DTE, op0=ALU.max, op1=ALU.add))
            link(dve.tensor_scalar(ALOG, ALOG, -1.0, None, ALU.mult))
            dve.tensor_tensor(DTA, DTV, ALOG.unsqueeze(1).to_broadcast([P, NT, SSM_H]), ALU.mult).then_inc(s4_dta, 1)
            dve.wait_ge(s4_pad, 1)
            for g in range(CVT):
                dve.wait_ge(s4_conv_in, g + 1)
                link(dve.tensor_scalar(CV[:, g, :], XBC[:, g, 0:N], CONVW[:, g, 0:1], CONVB[:, g:g + 1],
                                       ALU.mult, ALU.add))
                for k in range(1, 4):
                    ins = dve.scalar_tensor_tensor(out=CV[:, g, :], in0=XBC[:, g, k:k + N], scalar=CONVW[:, g, k:k + 1],
                                                   in1=CV[:, g, :], op0=ALU.mult, op1=ALU.add)
                    if k < 3:
                        link(ins)
                    else:
                        ins.then_inc(s4_conv, 1)
            dve.memset(HS, 0.0).then_inc(s4_hs, 1)
            for q in range(NT):
                dve.wait_ge(s4_small, q + 1)
                if q:
                    dve.wait_ge(s4_decay, 4 * q)
                link(dve.tensor_copy(LA[:, 0, :], PS[:, 2, P:P + SSM_H]))
                link(dve.tensor_copy(LA[:, 2, :], PS[:, 2, P + SSM_H:P + 2 * SSM_H]))
                link(dve.tensor_scalar(NLA, LA[:, 0, :], -1.0, None, ALU.mult))
                dve.tensor_tensor(LA[:, 1, :], LA[:, 2, :], LA[:, 0, :], ALU.subtract).then_inc(s4_la, 1)
                link(dve.tensor_copy(BNAT, PS[:, 2, 0:P]))
                xs = PS[:, 0:2, :].rearrange("p a (h c) -> p (a h) c", c=SSM_P)
                link(dve.tensor_tensor(heads(DTX), xs, DTV[:, q, :].unsqueeze(2).to_broadcast([P, SSM_H, SSM_P]),
                                       ALU.mult))
                dve.tensor_tensor(heads(YS[:, q, :]), xs, SSMD.unsqueeze(2).to_broadcast([P, SSM_H, SSM_P]),
                                  ALU.mult).then_inc(s4_read, 1)
                dve.wait_ge(s4_ela, q + 1)
                dve.tensor_tensor(heads(WDTX), heads(DTX), ELA[:, 1, :].unsqueeze(2).to_broadcast([P, SSM_H, SSM_P]),
                                  ALU.mult).then_inc(s4_wdtx, 1)
                for g in range(4):
                    dve.wait_ge(s4_decay, 4 * q + g + 1)
                    dve.tensor_tensor(DECAY[:, 4 * g:4 * g + 4, :], DECAY[:, 4 * g:4 * g + 4, :],
                                      PS[:, 3, 0:P].unsqueeze(1).to_broadcast([P, 4, P]), ALU.mult).then_inc(s4_mix, 1)
                dve.wait_ge(s4_read, q + 1)
                dve.wait_ge(s4_intra, q + 1)
                link(dve.tensor_tensor(YS[:, q, :], PS[:, 0:2, :].rearrange("p a b -> p (a b)"), YS[:, q, :], ALU.add))
                if q:
                    dve.wait_ge(s4_inter, q)
                    link(dve.tensor_tensor(heads(TMP), PS[:, 4:6, :].rearrange("p a (h c) -> p (a h) c", c=SSM_P),
                                           ELA[:, 0, :].unsqueeze(2).to_broadcast([P, SSM_H, SSM_P]), ALU.mult))
                    link(dve.tensor_tensor(YS[:, q, :], YS[:, q, :], TMP, ALU.add))
                dve.wait_ge(s4_z, 2 * q + 2)
                dve.tensor_tensor(YS[:, q, :], YS[:, q, :], ZG[:, q, :], ALU.mult).then_inc(s4_ys, 1)
                dve.wait_ge(s4_hs, q + 1)
                link(dve.tensor_tensor(heads(HS), heads(HS), ELA[:, 2, :].unsqueeze(2).to_broadcast([P, SSM_H, SSM_P]),
                                       ALU.mult))
                dve.wait_ge(s4_state, q + 1)
                dve.tensor_tensor(HS, HS, PS[:, 6:8, :].rearrange("p a b -> p (a b)"), ALU.add).then_inc(s4_hs, 1)
            dve.wait_ge(s4_rms, 1)
            link(dve.reciprocal(RMS, RMS))
            for q in range(NT):
                dve.tensor_scalar(YS[:, q, :], YS[:, q, :], RMS[:, q:q + 1], None, ALU.mult).then_inc(s4_yn, 1)
            for t in range(NT):
                dve.wait_ge(out_psum, NT * (4 - first) + t + 1)
                dve.tensor_tensor(X[:, t, :], PS[:, 4 + t, :], X[:, t, :], ALU.add).then_inc(x_done, 1)

        def s4_pe(pe):
            transpose_x_pe(pe, 4)
            pe.wait_ge(xt_ready, DT * (5 - first))
            pe.wait_ge(w_in[4], 8 * 16)
            for g in range(CVT):
                if g >= 4:
                    pe.wait_ge(s4_conv_in, g - 3)
                for c in range(DT):
                    ins = pe.matmul(PS[:, g % 4, :], WIN[:, c, SSM_I + g * P:SSM_I + (g + 1) * P], XT[:, c, :],
                                    start=(c == 0), stop=(c == DT - 1))
                ins.then_inc(s4_conv_psum, 1)
            for t in range(NT):
                for c in range(DT):
                    ins = pe.matmul(PS[:, 6, t * SSM_H:(t + 1) * SSM_H], XT[:, c, t * P:(t + 1) * P],
                                    WIN[:, c, PROJ - SSM_H:PROJ], start=(c == 0), stop=(c == DT - 1))
            ins.then_inc(s4_dt_psum, 1)
            for g in range(2 * NT):
                if g >= 2:
                    pe.wait_ge(s4_z, g - 1)
                t, half = g // 2, g % 2
                for c in range(DT):
                    ins = pe.matmul(PS[:, 4 + half, :], XT[:, c, t * P:(t + 1) * P],
                                    WIN[:, c, half * 512:(half + 1) * 512], start=(c == 0), stop=(c == DT - 1))
                ins.then_inc(s4_z_psum, 1)
            pe.wait_ge(s4_dta, 1)
            pe.wait_ge(s4_cv, CVT)
            pe.wait_ge(s4_z, 2 * NT)
            for q in range(NT):
                cols = slice(q * P, (q + 1) * P)
                if q:
                    pe.wait_ge(s4_ys, q)
                    pe.wait_ge(s4_hs, q + 1)
                for c in range(IT):
                    pe.transpose(PS[:, c // 4, (c % 4) * P:(c % 4 + 1) * P], CV[:, c, cols], IDENT[:, :])
                pe.transpose(PS[:, 2, 0:P], CV[:, IT, cols], IDENT[:, :])
                pe.matmul(PS[:, 2, P:P + SSM_H], UPPER[:, :], DTA[:, q, :], start=True, stop=True)
                pe.matmul(PS[:, 2, P + SSM_H:P + 2 * SSM_H], ONES[:, :], DTA[:, q, :], start=True, stop=True)
                pe.matmul(PS[:, 3, 0:P], CV[:, IT, cols], CV[:, IT + 1, cols], start=True, stop=True).then_inc(s4_small, 1)
                for g in range(4):
                    for h in range(4):
                        at = PS[:, 4 + g, h * P:(h + 1) * P]
                        pe.matmul(at, IDENT[:, :], FUTURE[:, :], start=True, stop=False)
                        ins = pe.matmul(at, DTA[:, q, 4 * g + h:4 * g + h + 1].to_broadcast([P, P]), UPPER[:, :],
                                        start=False, stop=True)
                    ins.then_inc(s4_decay_psum, 1)
                pe.wait_ge(s4_read, q + 1)
                for h in range(SSM_H):
                    pe.wait_ge(s4_mix, 4 * q + h // 4 + 1)
                    ins = pe.matmul(PS[:, h // 8, (h % 8) * SSM_P:(h % 8 + 1) * SSM_P], DECAY[:, h, :],
                                    DTX[:, h * SSM_P:(h + 1) * SSM_P], start=True, stop=True)
                ins.then_inc(s4_intra, 1)
                if q:
                    for half in range(2):
                        ins = pe.matmul(PS[:, 4 + half, :], CV[:, IT + 1, cols], HS[:, half * 512:(half + 1) * 512],
                                        start=True, stop=True)
                    ins.then_inc(s4_inter, 1)
                pe.wait_ge(s4_wdtx, q + 1)
                for half in range(2):
                    ins = pe.matmul(PS[:, 6 + half, :], BNAT, WDTX[:, half * 512:(half + 1) * 512], start=True, stop=True)
                ins.then_inc(s4_state, 1)
            pe.wait_ge(s4_yn, NT)
            pe.wait_ge(s4_hs, NT + 1)
            for c in range(IT):
                if c >= 4:
                    pe.wait_ge(s4_yt, c - 3)
                for t in range(NT):
                    ins = pe.transpose(PS[:, c % 4, t * P:(t + 1) * P], YS[:, t, c * P:(c + 1) * P], IDENT[:, :])
                ins.then_inc(s4_yt_psum, 1)
            pe.wait_ge(s4_yt, IT)
            for t in range(NT):
                for c in range(IT):
                    ins = pe.matmul(PS[:, 4 + t, :], YT[:, c, t * P:(t + 1) * P], WOUT[:, c, :],
                                    start=(c == 0), stop=(c == IT - 1))
                ins.then_inc(out_psum, 1)

        W1F = view(0, [DT, FF1])
        W2F = view(32 * K, [F1T, D])
        W1B = view(64 * K, [DT, FF1], BF16)
        W2B = view(80 * K, [F1T, D], BF16)
        XQT = view(96 * K, [DT, N], BF16)
        HT = view(104 * K, [F1T, N + 2])
        CO = view(0, [F1T, N])
        HQ = view(32 * K, [F1T, N], BF16)
        ROWSC = view(137 * K, [N])
        AMX = view(139 * K, [N])
        AMB = view(141 * K, [N])
        HSC = view(143 * K, [N])
        FCW = view(145 * K, [F1T, 3])
        FCB = view(146 * K, [F1T])
        HABS = view(147 * K, [2, N])
        XCL = COLS[:, 0:4]
        XSC = COLS[:, 4:8]
        XINV = COLS[:, 8:12]
        WSUM = COLS[:, 12:14]
        WALL = COLS[:, 14:16]
        WMEAN = COLS[:, 16:18]
        WREC = COLS[:, 18:20]
        OSC = COLS[:, 20:24]

        s5_abs = sem("s5_abs")
        s5_wall = sem("s5_wall")
        s5_w = sem("s5_w")
        s5_xinv = sem("s5_xinv")
        s5_row_psum = sem("s5_row_psum")
        s5_row = sem("s5_row")
        s5_pad = sem("s5_pad")
        s5_h_psum = sem("s5_h_psum")
        s5_h = sem("s5_h")
        s5_conv = sem("s5_conv")
        s5_silu = sem("s5_silu")
        s5_habs = sem("s5_habs")
        s5_mag = sem("s5_mag")
        s5_amb = sem("s5_amb")
        s5_col_psum = sem("s5_col_psum")
        s5_hq = sem("s5_hq")
        s5_amb2 = sem("s5_amb2")

        def s5_sp(sp):
            sp.wait_ge(x_done, NT * (5 - first))
            sp.dma_start(W1F, a["w1T"].rearrange("(t p) c -> p t c", p=P)).then_inc(w_in[5], 16)
            sp.dma_start(W2F, a["w2T"].rearrange("(t p) c -> p t c", p=P)).then_inc(w_in[5], 16)
            sp.dma_start(FCW, a["fconvw"]).then_inc(w_in[5], 16)
            sp.dma_start(FCB, a["fconvb"]).then_inc(w_in[5], 16)

        def s5_pool(pool, link):
            pool.wait_ge(x_done, NT * (5 - first))
            pool.memset(HT[:, :, 0:1], 0.0)
            pool.memset(HT[:, :, N + 1:N + 2], 0.0).then_inc(s5_pad, 1)
            pool.wait_ge(s5_abs, 2)
            pool.partition_all_reduce(WALL, WSUM, P, RADD).then_inc(s5_wall, 1)
            pool.wait_ge(s5_mag, F1T + 1)
            pool.partition_all_reduce(AMB, AMX, P, RMAX).then_inc(s5_amb, 1)

        def s5_act(act, link):
            layernorm_act(act, 5)
            act.wait_ge(w_in[5], 64)
            for n, (w, junk) in enumerate(((W1F, W1B), (W2F, W2B))):
                act.activation(junk, w, ACT.Abs, accum_out=WSUM[:, n:n + 1]).then_inc(s5_abs, 1)
            for c in range(DT):
                act.wait_ge(xt_psum, DT * (5 - first) + c + 1)
                act.copy(XQT[:, c, :], PS[:, c, :]).then_inc(xt_ready, 1)
            for g in range(F1T):
                act.wait_ge(s5_conv, g + 1)
                act.activation(CO[:, g, :], CO[:, g, :], ACT.Silu).then_inc(s5_silu, 1)
                act.wait_ge(s5_silu, g + 1)
                if g >= 2:
                    act.wait_ge(s5_mag, g)
                act.activation(HABS[:, g % 2, :], CO[:, g, :], ACT.Abs).then_inc(s5_habs, 1)

        def s5_dve(dve, link):
            layernorm_dve(dve, 5, link, finish=False)
            link.wait()
            link(dve.tensor_reduce(XCL, XN[:, :, :], AX.X, ALU.max, apply_absolute_value=True))
            link(dve.tensor_scalar(XCL, XCL, 1e-5, None, ALU.max))
            link(dve.reciprocal(XSC, XCL))
            link(dve.tensor_scalar(XSC, XSC, 127.0, None, ALU.mult))
            for t in range(NT):
                link(dve.tensor_scalar(XN[:, t, :], XN[:, t, :], XSC[:, t:t + 1], ROUND, ALU.mult, ALU.add))
                dve.tensor_scalar(XN[:, t, :], XN[:, t, :], ROUND, None, ALU.subtract).then_inc(ln_xn, 1)
            dve.wait_ge(s5_wall, 1)
            link(dve.tensor_scalar(WMEAN, WALL, 1.0 / (FF1 * D), 1e-5, ALU.mult, ALU.max))
            link(dve.reciprocal(WREC, WMEAN))
            dve.tensor_scalar(XINV, XCL, 1.0 / 127.0, WMEAN[:, 0:1], ALU.mult, ALU.mult).then_inc(s5_xinv, 1)
            for n, (w, q) in enumerate(((W1F, W1B), (W2F, W2B))):
                link(dve.tensor_scalar(w, w, WREC[:, n:n + 1], 1.0, ALU.mult, ALU.min))
                link(dve.tensor_scalar(w, w, -1.0, ROUND, ALU.max, ALU.add))
                dve.tensor_scalar(q, w, ROUND, None, ALU.subtract).then_inc(s5_w, 1)
            dve.wait_ge(s5_row_psum, 1)
            dve.tensor_copy(ROWSC, PS[:, 4, :]).then_inc(s5_row, 1)
            dve.wait_ge(s5_row, 1)
            dve.wait_ge(s5_w, 2)
            dve.wait_ge(s5_pad, 1)
            dve.memset(AMX, 0.0).then_inc(s5_mag, 1)

            def magnitude(g):
                dve.wait_ge(s5_habs, g + 1)
                dve.wait_ge(s5_mag, g + 1)
                dve.tensor_tensor(AMX, HABS[:, g % 2, :], AMX, ALU.max).then_inc(s5_mag, 1)

            for g in range(F1T):
                dve.wait_ge(s5_h_psum, g + 1)
                dve.tensor_tensor(HT[:, g, 1:N + 1], PS[:, g % 8, :], ROWSC, ALU.mult).then_inc(s5_h, 1)
                dve.wait_ge(s5_h, g + 1)
                link(dve.tensor_scalar(CO[:, g, :], HT[:, g, 0:N], FCW[:, g, 0:1], FCB[:, g:g + 1], ALU.mult, ALU.add))
                link(dve.scalar_tensor_tensor(out=CO[:, g, :], in0=HT[:, g, 1:N + 1], scalar=FCW[:, g, 1:2],
                                              in1=CO[:, g, :], op0=ALU.mult, op1=ALU.add))
                dve.scalar_tensor_tensor(out=CO[:, g, :], in0=HT[:, g, 2:N + 2], scalar=FCW[:, g, 2:3],
                                         in1=CO[:, g, :], op0=ALU.mult, op1=ALU.add).then_inc(s5_conv, 1)
                if g:
                    magnitude(g - 1)
            magnitude(F1T - 1)
            dve.wait_ge(s5_amb, 1)
            dve.tensor_scalar(AMB, AMB, 1e-5, None, ALU.max).then_inc(s5_amb2, 1)
            dve.wait_ge(s5_amb2, 1)
            link(dve.reciprocal(HSC, AMB))
            link(dve.tensor_scalar(HSC, HSC, 127.0, None, ALU.mult))
            for g in range(F1T):
                link(dve.tensor_tensor(CO[:, g, :], CO[:, g, :], HSC, ALU.mult))
                dve.tensor_scalar(HQ[:, g, :], CO[:, g, :], ROUND, ROUND, ALU.add, ALU.subtract).then_inc(s5_hq, 1)
            dve.wait_ge(s5_col_psum, 1)
            link(dve.tensor_scalar(OSC, PS[:, 4, 0:NT], 1.0 / 127.0, WMEAN[:, 1:2], ALU.mult, ALU.mult))
            for t in range(NT):
                dve.wait_ge(out_psum, NT * (5 - first) + t + 1)
                dve.scalar_tensor_tensor(out=X[:, t, :], in0=PS[:, t, :], scalar=OSC[:, t:t + 1], in1=X[:, t, :],
                                         op0=ALU.mult, op1=ALU.add).then_inc(x_done, 1)

        def s5_pe(pe):
            transpose_x_pe(pe, 5)
            pe.wait_ge(s5_xinv, 1)
            for t in range(NT):
                ins = pe.matmul(PS[:, 4, t * P:(t + 1) * P], XINV[:, t:t + 1].to_broadcast([P, P]), IDENT[:, :],
                                start=True, stop=True)
            ins.then_inc(s5_row_psum, 1)
            pe.wait_ge(xt_ready, DT * (6 - first))
            pe.wait_ge(s5_w, 1)
            pe.wait_ge(s5_row, 1)
            for g in range(F1T):
                if g >= 8:
                    pe.wait_ge(s5_h, g - 7)
                for c in range(DT):
                    ins = pe.matmul(PS[:, g % 8, :], W1B[:, c, g * P:(g + 1) * P], XQT[:, c, :],
                                    start=(c == 0), stop=(c == DT - 1))
                ins.then_inc(s5_h_psum, 1)
            pe.wait_ge(s5_amb2, 1)
            for t in range(NT):
                ins = pe.matmul(PS[:, 4, t:t + 1], AMB[0:1, t * P:(t + 1) * P], ONES[0:1, 0:1], start=True, stop=True)
            ins.then_inc(s5_col_psum, 1)
            pe.wait_ge(s5_w, 2)
            pe.wait_ge(s5_hq, F1T)
            for t in range(NT):
                for g in range(F1T):
                    ins = pe.matmul(PS[:, t, :], HQ[:, g, t * P:(t + 1) * P], W2B[:, g, :],
                                    start=(g == 0), stop=(g == F1T - 1))
                ins.then_inc(out_psum, 1)

        SP_PARTS = [s0_sp, s1_sp, s2_sp, s3_sp, s4_sp, s5_sp]
        POOL_PARTS = [s0_pool, s1_pool, s2_pool, s3_pool, s4_pool, s5_pool]
        ACT_PARTS = [s0_act, s1_act, s2_act, s3_act, s4_act, s5_act]
        DVE_PARTS = [s0_dve, s1_dve, s2_dve, s3_dve, s4_dve, s5_dve]
        PE_PARTS = [s0_pe, s1_pe, s2_pe, s3_pe, s4_pe, s5_pe]
        out_done = sem("out_done")
        block = ctx.enter_context(nc.Block())

        @block.sync
        def _(sp):
            sp.dma_start(X[:, :, :], a["x"].rearrange("(t p) c -> p t c", p=P)).then_inc(x_in, 16)
            for part in SP_PARTS[first:stages]:
                part(sp)
            sp.wait_ge(x_done, NT * (stages - first))
            sp.dma_start(out.rearrange("(t p) c -> p t c", p=P), X[:, :, :]).then_inc(out_done, 16)
            sp.wait_ge(out_done, 16)

        @block.gpsimd
        def _(pool):
            link = Order(pool, pool_order)
            setup_pool(pool, link)
            for part in POOL_PARTS[first:stages]:
                part(pool, link)

        @block.scalar
        def _(act):
            link = Order(act, act_order)
            act.wait_ge(const_ready, 1)
            for part in ACT_PARTS[first:stages]:
                part(act, link)

        @block.vector
        def _(dve):
            link = Order(dve, dve_order)
            dve.wait_ge(x_in, 16)
            dve.wait_ge(const_ready, 1)
            for part in DVE_PARTS[first:stages]:
                part(dve, link)

        @block.tensor
        def _(pe):
            pe.wait_ge(const_ready, 1)
            for part in PE_PARTS[first:stages]:
                part(pe)


def kernel(**inputs):
    import numpy as np
    import concourse.bacc as bacc
    from concourse import mybir as mb
    from concourse.bass_utils import run_bass_kernel_spmd

    nc = bacc.Bacc("TRN2", target_bir_lowering=False, num_devices=1)
    arrays, aps = {}, {}
    for name, value in layout(inputs, np).items():
        value = np.ascontiguousarray(value)
        arrays[f"in_{name}"] = value
        aps[name] = nc.dram_tensor(f"in_{name}", value.shape, mb.dt.from_np(value.dtype), kind="ExternalInput").ap()
    out = nc.dram_tensor("out_latents", (N, D), F32, kind="ExternalOutput").ap()
    perceiver_kernel(nc, aps, out)
    r = run_bass_kernel_spmd(nc, [arrays], core_ids=[0])
    return r.results[0]["out_latents"].reshape(1, N, D)
```

```python
from contextlib import ExitStack

import concourse.bass as bass
from concourse import mybir

F32 = mybir.dt.float32
F16 = mybir.dt.float16
BF16 = mybir.dt.bfloat16
I32 = mybir.dt.int32
U32 = mybir.dt.uint32
ALU = mybir.AluOpType
ACT = mybir.ActivationFunctionType
AX = mybir.AxisListType
RMAX = bass.bass_isa.ReduceOp.max
RADD = bass.bass_isa.ReduceOp.add

P = 128
D = 512
DT = D // P
N = 512
NT = N // P
M = 8192
MT = M // P
CH = 4
NCH = MT // CH
PAIRS = NCH // 2
EPS = 1e-5
ROUND = 12582912.0
FF0 = 1536
F0T = FF0 // P
QB = 32
ATT_H = 16
DH = D // ATT_H
SSM_H = 16
SSM_P = 64
SSM_I = SSM_H * SSM_P
SSM_N = 128
CONV = SSM_I + 2 * SSM_N
CVT = CONV // P
IT = SSM_I // P
PROJ = 2 * SSM_I + 2 * SSM_N + SSM_H
FF1 = 2048
F1T = FF1 // P
NEG = -1e30
Q_SCALE = float(D // 8) ** -0.5


def layout(v, np):
    def arr(name):
        return np.asarray(v[name])

    def blocks32(w):
        o, i = w.shape
        return w.reshape(o // QB, QB, i // P, P // QB, QB).transpose(3, 1, 2, 0, 4).reshape(P, (i // P) * o)

    def columns(x):
        return x.reshape(-1, P).T

    ctx = arr("ctx_1024")[0]
    qkv = arr("L0_xattn_qkv_w")
    wkv = arr("L1_xattn_Wkv")
    w_in = arr("L1_attn_W_in")
    out = {
        "x": arr("x")[0],
        "ctx": ctx,
        "ctxT": ctx.T.reshape(DT, P, NCH, CH * P).transpose(2, 1, 0, 3),
        "mask": arr("mask_S2_ik0").reshape(MT, P).T,
        "wq0": qkv[:D], "wk0": qkv[D:2 * D], "wvT0": qkv[2 * D:].T,
        "projT0": arr("L0_xattn_proj_w").T, "projb0": arr("L0_xattn_proj_b"),
        "lam": columns(np.repeat(arr("L0_attn_decay")[:, 1, 0], D // 16)),
        "lng": columns(arr("L0_attn_ln_g")), "lnb": columns(arr("L0_attn_ln_b")),
        "WvT": arr("L0_attn_Wv").T, "WqT": arr("L0_attn_Wq").T, "WgT": arr("L0_attn_Wg").T,
        "WoT": arr("L0_attn_Wo").T,
        "ffnB": np.concatenate([blocks32(arr("L0_ffn_w_" + n)).reshape(P, 4, FF0) for n in ("up", "gate", "down")],
                               axis=1).transpose(1, 0, 2),
        "Wq1T": arr("L1_xattn_Wq").T,
        "Wk1T": np.tile(wkv[:DH].T, (1, P // DH)), "Wv1T": wkv[DH:].T,
        "Wc1T": arr("L1_xattn_Wc").T,
        "WinT": w_in.T,
        "convw": arr("L1_attn_conv_w").reshape(CVT, P, 4).transpose(1, 0, 2), "convb": columns(arr("L1_attn_conv_b")),
        "dtb": arr("L1_attn_dt_bias"), "alog": arr("L1_attn_A_log"), "ssmd": arr("L1_attn_D"),
        "normw": columns(arr("L1_attn_norm_w")), "WoutT": arr("L1_attn_W_out").T,
        "w12": np.concatenate([arr("L1_ffn_w1").T.reshape(DT, P, FF1),
                               arr("L1_ffn_w2").T.reshape(4, F1T // 4, P, D).transpose(0, 2, 1, 3).reshape(4, P, FF1)]),
        "fconvw": arr("L1_ffn_conv_w").reshape(F1T, P, 3).transpose(1, 0, 2),
        "fconvb": columns(arr("L1_ffn_conv_b")),
    }
    return out


def perceiver_kernel(nc, a, out):
    ctx = ExitStack()
    with ctx:
        def sb(name, shape, dt):
            return ctx.enter_context(nc.sbuf_tensor(name, shape, dt))

        def sem(name):
            return ctx.enter_context(nc.semaphore(name))

        X = sb("X", [P, NT, D], F32)
        XN = sb("XN", [P, NT, D], F32)
        XT = sb("XT", [P, DT, N], F32)
        IDENT = sb("IDENT", [P, P], F32)
        ONES = sb("ONES", [P, P], F32)
        MEANW = sb("MEANW", [P, P], F32)
        UPPER = sb("UPPER", [P, P], F32)
        IDENTB = sb("IDENTB", [P, P], BF16)
        FUTUREB = sb("FUTUREB", [P, P], BF16)
        ZROW = sb("ZROW", [1, D], F16)
        MASKI = sb("MASKI", [P, MT], I32)
        MASK = sb("MASK", [P, MT], F32)
        W_RECIP = sb("W_RECIP", [P, 8], F32)
        W_MEAN = sb("W_MEAN", [P, 2], F32)
        MASKC = sb("MASKC", [P, 2, CH], F32)
        EPSC = sb("EPSC", [P, 1], F32)
        STATS = sb("STATS", [P, NT, 6], F32)
        MV = sb("MV", [P, NT, 2], F32)
        STD = sb("STD", [P, NT], F32)
        RSTD = sb("RSTD", [P, NT], F32)
        COLS = sb("COLS", [P, 64], F32)
        SM = sb("SM", [P, 64], F32)
        arena = sb("arena", [P, 178 * 256], F32)
        PS = ctx.enter_context(nc.psum_tensor("PS", [P, 8, 512], F32))

        def view(at, shape, dt=F32):
            size = 2 if dt in (F16, BF16) else 4
            n = 1
            for s in shape:
                n *= s
            v = arena[:, at // 4:(at + n * size) // 4]
            if dt != F32:
                v = v.bitcast(dt)
            if len(shape) == 1:
                return v
            if len(shape) == 2:
                return v.rearrange("p (a b) -> p a b", a=shape[0])
            return v.rearrange("p (a b c) -> p a b c", a=shape[0], b=shape[1])

        K = 1024
        def marks(*names):
            return {name: n + 1 for n, name in enumerate(names)}

        PE_MARK = marks("s0_close", "s0_den", "s1_mean", "s1_var", "s4_dt_psum", "s5_row_psum", "s5_col_psum")
        DVE_MARK = marks("s0_mask", "s1_rstd", "w_scale", "s3_memidx", "s4_dtb", "s4_dta", "s5_xinv", "s5_row", "s5_amb2")
        ACT_MARK = marks("s1_std", "s4_softplus", "s4_rms")
        POOL_MARK = marks("s0_primed", "const_ready", "s1_wall", "s3_primed", "s3_iota", "s4_pad", "s5_pad", "s5_amb")
        pe_marks = sem("pe_marks")
        dve_marks = sem("dve_marks")
        act_marks = sem("act_marks")
        pool_marks = sem("pool_marks")
        w_in = {i: sem(f"w_in{i}") for i in (0, 1, 3, 4, 5)}
        raw_in = [sem(f"raw_in{i}") for i in range(4)]
        small_in = sem("small_in")
        x_in = sem("x_in")
        mask_in = sem("mask_in")
        bias_in = sem("bias_in")
        x_done = sem("x_done")
        out_psum = sem("out_psum")
        ln_stats = sem("ln_stats")
        ln_var = sem("ln_var")
        ln_std = sem("ln_std")
        ln_rstd = sem("ln_rstd")
        ln_xn = sem("ln_xn")
        xt_psum = sem("xt_psum")
        xt_ready = sem("xt_ready")
        dve_order = sem("dve_order")
        settled = sem("settled")
        act_order = sem("act_order")
        pool_order = sem("pool_order")

        def settle(eng):
            eng.sem_inc(settled, 1)

        def layernorm_dve(dve, stage, link, finish=True):
            if stage:
                dve.wait_ge(x_done, NT * stage)
            for t in range(NT):
                dve.bn_stats(STATS[:, t, :], X[:, t, :]).then_inc(ln_stats, 1)
            dve.wait_ge(ln_stats, NT * (stage + 1))
            for t in range(NT):
                dve.bn_aggr(MV[:, t, :], STATS[:, t, :]).then_inc(ln_var, 1)
            dve.wait_ge(ln_std, stage + 1)
            dve.reciprocal(RSTD[:, :], STD[:, :]).then_inc(ln_rstd, 1)
            dve.wait_ge(ln_rstd, stage + 1)
            for t in range(NT):
                ins = dve.tensor_scalar(XN[:, t, :], X[:, t, :], MV[:, t, 0:1], RSTD[:, t:t + 1],
                                        ALU.subtract, ALU.mult)
                if finish:
                    ins.then_inc(ln_xn, 1)
                else:
                    ins.then_inc(dve_order, 1)
                    link.add(1)

        def layernorm_act(act, stage):
            act.wait_ge(ln_var, NT * (stage + 1))
            act.activation(STD[:, :], MV[:, :, 1], ACT.Sqrt, bias=EPSC[:, 0:1]).then_inc(ln_std, 1)

        def transpose_x_pe(pe, stage):
            pe.wait_ge(ln_xn, NT * (stage + 1))
            for c in range(DT):
                for t in range(NT):
                    ins = pe.transpose(PS[:, c, t * P:(t + 1) * P], XN[:, t, c * P:(c + 1) * P], IDENT[:, :])
                ins.then_inc(xt_psum, 1)

        def transpose_x_act(act, stage):
            for c in range(DT):
                act.wait_ge(xt_psum, DT * stage + c + 1)
                act.copy(XT[:, c, :], PS[:, c, :]).then_inc(xt_ready, 1)

        class Order:

            def __init__(self, eng, s):
                self.eng, self.s, self.n = eng, s, 0

            def add(self, n):
                self.n += n

            def __call__(self, ins):
                self.n += 1
                ins.then_inc(self.s, 1)
                self.eng.wait_ge(self.s, self.n)

            def note(self, ins):
                self.n += 1
                ins.then_inc(self.s, 1)

            def wait(self):
                self.eng.wait_ge(self.s, self.n)

        ST = view(0, [MT, N])
        CR = view(128 * K, [2, CH, 512])
        CHI = view(144 * K, [2, CH, 512], F16)
        CLO = view(152 * K, [2, CH, 512], F16)
        QHI = view(160 * K, [DT, N], F16)
        QLO = view(164 * K, [DT, N], F16)
        PHI = view(160 * K, [CH, N], F16)
        PLO = view(172 * K, [CH, N], F16)
        PSUMS = view(164 * K, [N])
        RUNMAX = view(168 * K, [N])
        COLMAX = view(170 * K, [N])
        WQ = view(0, [DT, D])
        WK = view(8 * K, [DT, D])
        WQK = view(16 * K, [DT, D])
        WVT = XN
        PROJT = XT
        O = view(0, [NT, D])
        Z = view(8 * K, [DT, D])
        BIAS = view(16 * K, [D])

        s0_wqk_psum = sem("s0_wqk_psum")
        s0_wqk = sem("s0_wqk")
        s0_q_psum = sem("s0_q_psum")
        s0_q_hi = sem("s0_q_hi")
        s0_q_lo = sem("s0_q_lo")
        s0_chunk = [sem("s0_chunk0"), sem("s0_chunk1")]
        s0_hi = sem("s0_hi")
        s0_lo = sem("s0_lo")
        s0_scores = sem("s0_scores")
        s0_max = sem("s0_max")
        s0_copied = sem("s0_copied")
        s0_colmax = sem("s0_colmax")
        s0_row = [sem("s0_row0"), sem("s0_row1")]
        s0_shift = sem("s0_shift")
        s0_exp = sem("s0_exp")
        s0_p_hi = sem("s0_p_hi")
        s0_p_lo = sem("s0_p_lo")
        s0_sum = sem("s0_sum")
        s0_c_hi = sem("s0_c_hi")
        s0_c_lo = sem("s0_c_lo")
        s0_pv = sem("s0_pv")
        s0_maskc = sem("s0_maskc")
        s0_o = sem("s0_o")
        s0_z_psum = sem("s0_z_psum")
        s0_z = sem("s0_z")

        ctxT = a["ctxT"]
        ctx_rows = a["ctx"].rearrange("(k j p) c -> k p j c", j=CH, p=P)

        BANKS = 8
        AHEAD_SPLIT = 2
        AHEAD_TILES = CH + 1
        AHEAD_BANK = BANKS

        def s0_sp(sp):
            sp.dma_start(WQ, a["wq0"].rearrange("(t p) c -> p t c", p=P)).then_inc(w_in[0], 16)
            sp.dma_start(WK, a["wk0"].rearrange("(t p) c -> p t c", p=P)).then_inc(w_in[0], 16)
            sp.dma_start(MASKI[:, :], a["mask"]).then_inc(mask_in, 16)
            sp.wait_ge(pool_marks, POOL_MARK["s0_primed"])
            with sp.Fori(0, PAIRS) as i:
                for b in range(2):
                    sp.wait_ge(s0_hi, i * 2 + b + 1)
                    sp.wait_ge(s0_lo, i * 2 + b + 1)
                    sp.dma_start(CR[:, b], a["ctxT"][i * 2 + b]).then_inc(s0_chunk[b], 16)
            sp.dma_start(WVT[:, :, :], a["wvT0"].rearrange("(t p) c -> p t c", p=P)).then_inc(w_in[0], 16)
            sp.dma_start(PROJT[:, :, :], a["projT0"].rearrange("(t p) c -> p t c", p=P)).then_inc(w_in[0], 16)
            sp.wait_ge(s0_hi, NCH + AHEAD_SPLIT)
            sp.wait_ge(s0_lo, NCH + AHEAD_SPLIT)
            with sp.Fori(0, PAIRS) as i:
                for b in range(2):
                    sp.wait_ge(s0_c_hi, (i * 2 + b) * CH + 1)
                    sp.wait_ge(s0_c_lo, (i * 2 + b) * CH + 1)
                    sp.dma_start(CR[:, b], ctx_rows[i * 2 + b]).then_inc(s0_row[b], 16)
            sp.wait_ge(pe_marks, PE_MARK["s0_close"])
            sp.dma_start(BIAS, a["projb0"].partition_broadcast(P)).then_inc(bias_in, 16)
            s1_loads(sp)
            s2_loads(sp)

        def setup_pool(pool, link):
            link(pool.memset(IDENT[:, :], 0.0))
            link(pool.affine_select(out=IDENT[:, :], in_=IDENT[:, :], compare_op=ALU.not_equal, fill=1.0,
                                    base=0, pattern=[[-1, P]], channel_multiplier=1))
            link(pool.memset(ONES[:, :], 1.0))
            link(pool.affine_select(out=UPPER[:, :], in_=ONES[:, :], compare_op=ALU.is_ge, fill=0.0,
                                    base=0, pattern=[[1, P]], channel_multiplier=-1))
            link(pool.tensor_copy(IDENTB[:, :], IDENT[:, :]))
            link(pool.memset(FUTUREB[:, :], 0.0))
            link(pool.affine_select(out=FUTUREB[:, :], in_=FUTUREB[:, :], compare_op=ALU.is_ge, fill=NEG,
                                    base=0, pattern=[[1, P]], channel_multiplier=-1))
            link(pool.memset(MEANW[:, :], 1.0 / D))
            link(pool.memset(EPSC[:, :], EPS))
            link(pool.memset(ZROW[:, :], 0.0))
            pool.sem_inc(s0_hi, AHEAD_SPLIT)
            pool.sem_inc(s0_lo, AHEAD_SPLIT)
            for s in (s0_scores, s0_c_hi, s0_c_lo, s0_pv):
                pool.sem_inc(s, AHEAD_TILES)
            pool.sem_inc(s0_copied, AHEAD_BANK)
            pool.sem_inc(pool_marks, 1)
            pool.sem_inc(pool_marks, 1)

        def s0_pool(pool, link):
            with pool.Fori(0, PAIRS) as i:
                for b in range(2):
                    c = i * 2 + b
                    pool.wait_ge(s0_chunk[b], i * 16 + 16)
                    pool.wait_ge(s0_scores, c * CH + 1)
                    settle(pool)
                    pool.tensor_scalar(CHI[:, b], CR[:, b], 1.0, 0.0, ALU.mult, ALU.add).then_inc(s0_hi, 1)
                    pool.wait_ge(s0_hi, c + 1 + AHEAD_SPLIT)
                    pool.tensor_tensor(CLO[:, b], CR[:, b], CHI[:, b], ALU.subtract).then_inc(s0_lo, 1)
            pool.wait_ge(s0_max, MT + 1)
            link(pool.partition_all_reduce(COLMAX, RUNMAX, P, RMAX))
            pool.wait_ge(s0_copied, MT + AHEAD_BANK)
            pool.wait_ge(dve_marks, DVE_MARK["s0_mask"])
            with pool.Fori(0, PAIRS) as i:
                for b in range(2):
                    c = i * 2 + b
                    for j in range(CH):
                        pool.tensor_tensor(ST[:, c * CH + j, :], ST[:, c * CH + j, :], COLMAX,
                                           ALU.subtract).then_inc(s0_shift, 1)
                        if j == 0:
                            pool.wait_ge(s0_row[b], i * 16 + 16)
                            pool.wait_ge(s0_maskc, c + 1)
                            pool.wait_ge(s0_pv, c * CH + 1)
                            settle(pool)
                        pool.tensor_scalar(CHI[:, b, j, :], CR[:, b, j, :], MASKC[:, b, j:j + 1], 0.0,
                                           ALU.mult, ALU.add).then_inc(s0_c_hi, 1)

        def s0_act(act, link):
            layernorm_act(act, 0)
            for c in range(DT):
                act.wait_ge(s0_wqk_psum, c + 1)
                act.copy(WQK[:, c, :], PS[:, 4 + c, :]).then_inc(s0_wqk, 1)
            transpose_x_act(act, 0)
            for c in range(DT):
                act.wait_ge(s0_q_psum, c + 1)
                act.activation(QHI[:, c, :], PS[:, c, :], ACT.Copy, scale=Q_SCALE).then_inc(s0_q_hi, 1)
            with act.Fori(0, PAIRS) as i:
                for b in range(2):
                    for j in range(CH):
                        k = (i * 2 + b) * CH + j
                        act.wait_ge(s0_scores, k + 1 + AHEAD_TILES)
                        act.activation(ST[:, k, :], PS[:, b * CH + j, :], ACT.Copy).then_inc(s0_copied, 1)
            with act.Fori(0, PAIRS) as i:
                for b in range(2):
                    c = i * 2 + b
                    for j in range(CH):
                        k = c * CH + j
                        act.wait_ge(s0_shift, k + 1)
                        act.activation(ST[:, k, :], ST[:, k, :], ACT.Exp).then_inc(s0_exp, 1)
                        act.wait_ge(s0_exp, k + 1)
                        act.wait_ge(s0_pv, k + 2)
                        settle(act)
                        act.copy(PHI[:, j, :], ST[:, k, :]).then_inc(s0_p_hi, 1)
            for c in range(DT):
                act.wait_ge(s0_z_psum, c + 1)
                act.copy(Z[:, c, :], PS[:, 4 + c, :]).then_inc(s0_z, 1)
                if c:
                    add_round(act, c - 1)

        def s0_dve(dve, link):
            layernorm_dve(dve, 0, link)
            dve.wait_ge(mask_in, 16)
            dve.tensor_scalar(MASK[:, :], MASKI[:, :], 0.0, None, ALU.not_equal).then_inc(dve_marks, 1)
            for c in range(DT):
                dve.wait_ge(s0_q_hi, c + 1)
                dve.scalar_tensor_tensor(out=QLO[:, c, :], in0=PS[:, c, :], scalar=Q_SCALE, in1=QHI[:, c, :],
                                         op0=ALU.mult, op1=ALU.subtract).then_inc(s0_q_lo, 1)
            dve.memset(RUNMAX, -3.0e38).then_inc(s0_max, 1)
            with dve.Fori(0, PAIRS) as i:
                for b in range(2):
                    for j in range(CH):
                        k = (i * 2 + b) * CH + j
                        dve.wait_ge(s0_copied, k + 1 + AHEAD_BANK)
                        dve.wait_ge(s0_max, k + 1)
                        dve.tensor_tensor(RUNMAX, ST[:, k, :], RUNMAX, ALU.max).then_inc(s0_max, 1)
            dve.wait_ge(dve_marks, DVE_MARK["s0_mask"])
            dve.memset(PSUMS, 0.0).then_inc(s0_sum, 1)
            with dve.Fori(0, PAIRS) as i:
                for b in range(2):
                    c = i * 2 + b
                    dve.wait_ge(s0_c_lo, c * CH + 1)
                    dve.tensor_copy(MASKC[:, b, :], MASK[:, bass.ds(c * CH, CH)]).then_inc(s0_maskc, 1)
                    dve.wait_ge(s0_maskc, c + 1)
                    dve.wait_ge(s0_pv, c * CH + 1)
                    for j in range(CH):
                        k = c * CH + j
                        dve.wait_ge(s0_c_hi, k + 1 + AHEAD_TILES)
                        dve.scalar_tensor_tensor(out=CLO[:, b, j, :], in0=CR[:, b, j, :],
                                                 scalar=MASKC[:, b, j:j + 1], in1=CHI[:, b, j, :],
                                                 op0=ALU.mult, op1=ALU.subtract).then_inc(s0_c_lo, 1)
                        dve.wait_ge(s0_p_hi, k + 1)
                        dve.wait_ge(s0_pv, k + 2)
                        dve.tensor_tensor(PLO[:, j, :], ST[:, k, :], PHI[:, j, :],
                                          ALU.subtract).then_inc(s0_p_lo, 1)
                        dve.wait_ge(s0_sum, k + 1)
                        dve.tensor_tensor(PSUMS, PSUMS, ST[:, k, :], ALU.add).then_inc(s0_sum, 1)
            dve.wait_ge(pe_marks, PE_MARK["s0_den"])
            link(dve.reciprocal(COLS[:, 0:NT], PS[:, 4, 0:NT]))
            for t in range(NT):
                dve.tensor_scalar(O[:, t, :], PS[:, t, :], COLS[:, t:t + 1], None, ALU.mult).then_inc(s0_o, 1)
            for p in range(4):
                requantise(dve, link, p)
            dve.wait_ge(bias_in, 16)
            for t in range(NT):
                link(dve.tensor_tensor(X[:, t, :], X[:, t, :], BIAS, ALU.add))
            for t in range(NT):
                dve.wait_ge(out_psum, t + 1)
                dve.tensor_tensor(X[:, t, :], PS[:, t, :], X[:, t, :], ALU.add).then_inc(x_done, 1)

        def s0_pe(pe):
            pe.wait_ge(w_in[0], 32)
            for c in range(DT):
                for d in range(DT):
                    ins = pe.matmul(PS[:, 4 + c, :], WQ[:, d, c * P:(c + 1) * P], WK[:, d, :],
                                    start=(d == 0), stop=(d == DT - 1))
                ins.then_inc(s0_wqk_psum, 1)
            transpose_x_pe(pe, 0)
            pe.wait_ge(xt_ready, DT)
            pe.wait_ge(s0_wqk, DT)
            for e in range(DT):
                for c in range(DT):
                    ins = pe.matmul(PS[:, e, :], WQK[:, c, e * P:(e + 1) * P], XT[:, c, :],
                                    start=(c == 0), stop=(c == DT - 1))
                ins.then_inc(s0_q_psum, 1)
            pe.wait_ge(s0_q_hi, DT)
            pe.wait_ge(s0_q_lo, DT)
            with pe.Fori(0, PAIRS) as i:
                for b in range(2):
                    c = i * 2 + b
                    pe.wait_ge(s0_hi, c + 1 + AHEAD_SPLIT)
                    pe.wait_ge(s0_lo, c + 1 + AHEAD_SPLIT)
                    for j in range(CH):
                        k = c * CH + j
                        pe.wait_ge(s0_copied, k + 1)
                        bank = PS[:, b * CH + j, :]
                        cols = slice(j * P, (j + 1) * P)
                        for e in range(DT):
                            pe.matmul(bank, CHI[:, b, e, cols], QHI[:, e, :], start=(e == 0), stop=False)
                            pe.matmul(bank, CHI[:, b, e, cols], QLO[:, e, :], start=False, stop=False)
                            ins = pe.matmul(bank, CLO[:, b, e, cols], QHI[:, e, :], start=False,
                                            stop=(e == DT - 1))
                        ins.then_inc(s0_scores, 1)
            pe.wait_ge(s0_copied, MT + AHEAD_BANK)
            for t in range(NT):
                pe.matmul(PS[:, t, :], ZROW[:, 0:P], ZROW[:, :], start=True, stop=False)
            with pe.Fori(0, PAIRS) as i:
                for b in range(2):
                    for j in range(CH):
                        k = (i * 2 + b) * CH + j
                        pe.wait_ge(s0_c_hi, k + 1 + AHEAD_TILES)
                        pe.wait_ge(s0_c_lo, k + 1 + AHEAD_TILES)
                        pe.wait_ge(s0_p_hi, k + 1)
                        pe.wait_ge(s0_p_lo, k + 1)
                        for t in range(NT):
                            cols = slice(t * P, (t + 1) * P)
                            pe.matmul(PS[:, t, :], PHI[:, j, cols], CHI[:, b, j, :], start=False, stop=False)
                            pe.matmul(PS[:, t, :], PHI[:, j, cols], CLO[:, b, j, :], start=False, stop=False)
                            ins = pe.matmul(PS[:, t, :], PLO[:, j, cols], CHI[:, b, j, :], start=False, stop=False)
                        ins.then_inc(s0_pv, 1)
            for t in range(NT):
                ins = pe.matmul(PS[:, t, :], ZROW[:, 0:P], ZROW[:, :], start=False, stop=True)
            ins.then_inc(pe_marks, 1)
            pe.wait_ge(s0_sum, MT + 1)
            for t in range(NT):
                ins = pe.matmul(PS[:, 4, t:t + 1], PSUMS[:, t * P:(t + 1) * P], ONES[:, 0:1], start=True, stop=True)
            ins.then_inc(pe_marks, 1)
            pe.wait_ge(w_in[0], 64)
            pe.wait_ge(s0_o, NT)
            for c in range(DT):
                for t in range(NT):
                    ins = pe.matmul(PS[:, 4 + c, :], O[:, t, c * P:(c + 1) * P], PROJT[:, t, :],
                                    start=(t == 0), stop=(t == NT - 1))
                ins.then_inc(s0_z_psum, 1)
            pe.wait_ge(s0_z, DT)
            for t in range(NT):
                for c in range(DT):
                    ins = pe.matmul(PS[:, t, :], WVT[:, c, t * P:(t + 1) * P], Z[:, c, :],
                                    start=(c == 0), stop=(c == DT - 1))
                ins.then_inc(out_psum, 1)

        RW = view(18 * K, [4, DT, D])
        STATE = view(50 * K, [DT, N])
        SQ = STATE
        Y = view(58 * K, [DT, N])
        GATE = view(66 * K, [DT, N])
        RSTDB = view(74 * K, [N])
        WABS = view(0, [2, 2048])
        LAM, LNG, LNB = SM[:, 0:DT], SM[:, DT:2 * DT], SM[:, 2 * DT:3 * DT]

        s1_proj = sem("s1_proj")
        s1_state = sem("s1_state")
        s1_y = sem("s1_y")
        s1_gate = sem("s1_gate")
        s1_cent = sem("s1_cent")
        s1_sq = sem("s1_sq")
        s1_mod = sem("s1_mod")
        s1_abs = sem("s1_abs")

        def s1_loads(sp):
            for n, name in enumerate(("WvT", "WqT", "WgT", "WoT")):
                sp.dma_start(RW[:, n], a[name].rearrange("(t p) c -> p t c", p=P)).then_inc(w_in[1], 16)
            for dst, name in ((LAM, "lam"), (LNG, "lng"), (LNB, "lnb")):
                sp.dma_start(dst, a[name]).then_inc(w_in[1], 16)

        def s1_pool(pool, link):
            scale_pieces(pool, 0, 10)
            pool.wait_ge(s1_abs, 8)
            pool.partition_all_reduce(COLS[:, 56:64], COLS[:, 48:56], P, RADD).then_inc(pool_marks, 1)

        def s1_act(act, link):
            act.wait_ge(x_done, NT * 1)
            for r in range(2):
                act.dma_start(WABS[:, r, :], a["w12"][r]).then_inc(raw_in[r], 16)
            layernorm_act(act, 1)
            transpose_x_act(act, 1)
            for e in range(DT):
                for r in (2 * e, 2 * e + 1):
                    act.wait_ge(raw_in[r % 2], 16 * (r // 2 + 1))
                    act.activation(WABS[:, r % 2, :], WABS[:, r % 2, :], ACT.Abs,
                                   accum_out=COLS[:, 48 + r:49 + r]).then_inc(s1_abs, 1)
                add_round(act, 3 + e)
                if e < DT - 1:
                    for r in (2 * e + 2, 2 * e + 3):
                        act.wait_ge(s1_abs, r - 1)
                        act.dma_start(WABS[:, r % 2, :], a["w12"][r]).then_inc(raw_in[r % 2], 16)
                act.wait_ge(s1_proj, 3 * e + 3)
                act.activation(GATE[:, e, :], PS[:, (3 * e + 2) % 8, :], ACT.Silu).then_inc(s1_gate, 1)
            add_round(act, 7)
            for e in range(DT):
                act.wait_ge(s1_cent, e + 1)
                act.activation(SQ[:, e, :], Y[:, e, :], ACT.Square).then_inc(s1_sq, 1)
            act.wait_ge(pe_marks, PE_MARK["s1_var"])
            act.activation(RSTDB, PS[:, 5, :], ACT.Sqrt, bias=EPSC[:, 0:1]).then_inc(act_marks, 1)

        def s1_dve(dve, link):
            layernorm_dve(dve, 1, link)
            requantise(dve, link, 4)
            dve.wait_ge(w_in[1], 7 * 16)
            for e in range(DT):
                dve.wait_ge(s1_proj, 3 * e + 1)
                dve.tensor_tensor_scan(STATE[:, e, :], LAM[:, e:e + 1].to_broadcast([P, N]), PS[:, (3 * e) % 8, :],
                                       0.0, ALU.mult, ALU.add).then_inc(s1_state, 1)
                dve.wait_ge(s1_state, e + 1)
                dve.wait_ge(s1_proj, 3 * e + 2)
                dve.tensor_tensor(Y[:, e, :], PS[:, (3 * e + 1) % 8, :], STATE[:, e, :],
                                  ALU.mult).then_inc(s1_y, 1)
                requantise(dve, link, 5 + e)
            dve.wait_ge(s1_y, DT)
            dve.wait_ge(pe_marks, PE_MARK["s1_mean"])
            for e in range(DT):
                dve.tensor_tensor(Y[:, e, :], Y[:, e, :], PS[:, 4, :], ALU.subtract).then_inc(s1_cent, 1)
            dve.wait_ge(act_marks, ACT_MARK["s1_std"])
            dve.reciprocal(RSTDB, RSTDB).then_inc(dve_marks, 1)
            dve.wait_ge(dve_marks, DVE_MARK["s1_rstd"])
            dve.wait_ge(s1_gate, DT)
            for e in range(DT):
                link(dve.scalar_tensor_tensor(out=Y[:, e, :], in0=Y[:, e, :], scalar=LNG[:, e:e + 1], in1=RSTDB,
                                              op0=ALU.mult, op1=ALU.mult))
                dve.scalar_tensor_tensor(out=Y[:, e, :], in0=Y[:, e, :], scalar=LNB[:, e:e + 1], in1=GATE[:, e, :],
                                         op0=ALU.add, op1=ALU.mult).then_inc(s1_mod, 1)
            requantise(dve, link, 9)
            dve.wait_ge(pool_marks, POOL_MARK["s1_wall"])
            link(dve.tensor_reduce(W_MEAN[:, :], COLS[:, 56:64].rearrange("p (w n) -> p w n", w=2), AX.X, ALU.add))
            link(dve.tensor_scalar(W_MEAN[:, :], W_MEAN[:, :], 1.0 / (FF1 * D), 1e-5, ALU.mult, ALU.max))
            dve.reciprocal(W_RECIP[:, :].rearrange("p (w n) -> p w n", w=2),
                           W_MEAN[:, :].unsqueeze(2).to_broadcast([P, 2, 4])).then_inc(dve_marks, 1)
            for t in range(NT):
                dve.wait_ge(out_psum, NT * 1 + t + 1)
                dve.tensor_tensor(X[:, t, :], PS[:, t, :], X[:, t, :], ALU.add).then_inc(x_done, 1)

        def s1_pe(pe):
            transpose_x_pe(pe, 1)
            pe.wait_ge(xt_ready, DT * 2)
            pe.wait_ge(w_in[1], 7 * 16)
            for e in range(DT):
                for n in range(3):
                    g = 3 * e + n
                    if g >= 8:
                        pe.wait_ge((s1_state, s1_y, s1_gate)[(g - 8) % 3], (g - 8) // 3 + 1)
                    for c in range(DT):
                        ins = pe.matmul(PS[:, g % 8, :], RW[:, n, c, e * P:(e + 1) * P], XT[:, c, :],
                                        start=(c == 0), stop=(c == DT - 1))
                    ins.then_inc(s1_proj, 1)
            pe.wait_ge(s1_y, DT)
            pe.wait_ge(s1_gate, DT)
            for e in range(DT):
                ins = pe.matmul(PS[:, 4, :], MEANW[:, :], Y[:, e, :], start=(e == 0), stop=(e == DT - 1))
            ins.then_inc(pe_marks, 1)
            for e in range(DT):
                pe.wait_ge(s1_sq, e + 1)
                ins = pe.matmul(PS[:, 5, :], MEANW[:, :], SQ[:, e, :], start=(e == 0), stop=(e == DT - 1))
            ins.then_inc(pe_marks, 1)
            pe.wait_ge(s1_mod, DT)
            for t in range(NT):
                for e in range(DT):
                    ins = pe.matmul(PS[:, t, :], Y[:, e, t * P:(t + 1) * P], RW[:, 3, e, :],
                                    start=(e == 0), stop=(e == DT - 1))
                ins.then_inc(out_psum, 1)

        UP = view(0, [F0T, N])
        GT = view(24 * K, [F0T, N])
        SG = view(48 * K, [F0T, N])
        PIECE = FF0
        PIECES = 3 * F0T * D // PIECE
        FRAW = view(76 * K, [4, PIECE])
        NBLK = PIECE // QB
        BSC = view(100 * K, [PIECES, NBLK])
        BRC = view(102 * K + 512, [PIECES, NBLK])
        FW = view(106 * K, [3, F0T * D])
        FWP = view(106 * K, [PIECES, PIECE])
        UPW = FW[:, 0].rearrange("p (t o) -> p t o", t=DT)
        GTW = FW[:, 1].rearrange("p (t o) -> p t o", t=DT)
        DNW = FW[:, 2].rearrange("p (t o) -> p t o", t=F0T)
        TILE_MAG = view(105 * K, [2, F0T])
        SLICES = 3
        PER = F0T // SLICES
        AM = COLS[:, 8:13]
        AR = COLS[:, 16:21]
        SC = COLS[:, 24:29]
        RC = COLS[:, 32:37]

        s2_raw = [sem(f"s2_raw{i}") for i in range(4)]
        s2_brc = sem("s2_brc")
        s2_scaled = sem("s2_scaled")
        s2_rounded = sem("s2_rounded")
        s2_w = sem("s2_w")
        s2_scale = sem("s2_scale")
        s2_mag = sem("s2_mag")
        s2_tmag = sem("s2_tmag")
        s2_all = sem("s2_all")
        s2_up_psum = sem("s2_up_psum")
        s2_up = sem("s2_up")
        s2_gt_psum = sem("s2_gt_psum")
        s2_gt = sem("s2_gt")
        s2_gt_r = sem("s2_gt_r")
        s2_gt_q = sem("s2_gt_q")
        s2_up_q = sem("s2_up_q")
        s2_sg = sem("s2_sg")
        s2_sg_r = sem("s2_sg_r")
        s2_p_r = sem("s2_p_r")
        s2_h_r = sem("s2_h_r")
        s2_hid = sem("s2_hid")

        def s2_loads(sp):
            for p in range(PIECES):
                if p >= 4:
                    sp.wait_ge(s2_w, p - 3)
                sp.dma_start(FRAW[:, p % 4, :], a["ffnB"][p]).then_inc(s2_raw[p % 4], 16)

        def requantise(dve, link, p):
            if p < PIECES:
                dve.wait_ge(s2_raw[p % 4], 16 * (p // 4 + 1))
                w = FRAW[:, p % 4, :].rearrange("p (k s) -> p k s", s=QB)
                link(dve.tensor_reduce(BSC[:, p, :], w, AX.X, ALU.max, apply_absolute_value=True))
                link(dve.tensor_scalar(BSC[:, p, :], BSC[:, p, :], 1.0 / 7.0, 1e-12, ALU.mult, ALU.max))
                dve.reciprocal(BRC[:, p, :], BSC[:, p, :]).then_inc(s2_brc, 1)
            if p >= 2:
                p -= 2
                w = FRAW[:, p % 4, :].rearrange("p (k s) -> p k s", s=QB)
                dve.wait_ge(s2_rounded, p + 1)
                link(dve.scalar_tensor_tensor(out=w, in0=w, scalar=ROUND,
                                              in1=BSC[:, p, :].unsqueeze(2).to_broadcast([P, NBLK, QB]),
                                              op0=ALU.subtract, op1=ALU.mult))
                dve.transpose(FWP[:, p, :], FRAW[:, p % 4, :]).then_inc(s2_w, 1)

        def scale_pieces(pool, start, end):
            for p in range(start, end):
                w = FRAW[:, p % 4, :].rearrange("p (k s) -> p k s", s=QB)
                pool.wait_ge(s2_brc, p + 1)
                pool.tensor_tensor(w, w, BRC[:, p, :].unsqueeze(2).to_broadcast([P, NBLK, QB]),
                                   ALU.mult).then_inc(s2_scaled, 1)

        def add_round(act, p):
            act.wait_ge(s2_scaled, p + 1)
            act.activation(FRAW[:, p % 4, :], FRAW[:, p % 4, :], ACT.Copy, bias=ROUND).then_inc(s2_rounded, 1)

        def tiles(v, k):
            return v[:, k * PER:(k + 1) * PER, :]

        def s2_pool(pool, link):
            for n in range(3):
                if n == 1:
                    scale_pieces(pool, 10, PIECES)
                pool.wait_ge(s2_mag, n + 1)
                pool.partition_all_reduce(AR[:, n:n + 1], AM[:, n:n + 1], P, RMAX).then_inc(s2_all, 1)
            pool.wait_ge(s2_scale, 3)
            for k in range(SLICES):
                link(pool.tensor_scalar(tiles(UP, k), tiles(UP, k), RC[:, 2:3], ROUND, ALU.mult, ALU.add))
                pool.tensor_scalar(tiles(UP, k), tiles(UP, k), -ROUND, SC[:, 2:3], ALU.add, ALU.mult).then_inc(s2_up_q, 1)
            for n in range(3, 5):
                pool.wait_ge(s2_mag, n + 1)
                pool.partition_all_reduce(AR[:, n:n + 1], AM[:, n:n + 1], P, RMAX).then_inc(s2_all, 1)

        def s2_act(act, link):
            layernorm_act(act, 2)
            transpose_x_act(act, 2)
            for g in range(F0T):
                act.wait_ge(s2_up_psum, g + 1)
                act.copy(UP[:, g, :], PS[:, (2 * g) % 8, :]).then_inc(s2_up, 1)
                if g % 2 == 0 and g < 8:
                    add_round(act, 8 + g // 2)
            act.wait_ge(s2_scale, 2)
            for k in range(SLICES):
                act.activation(tiles(GT, k), tiles(GT, k), ACT.Copy, scale=RC[:, 1:2], bias=ROUND).then_inc(s2_gt_r, 1)
            for k in range(SLICES):
                act.wait_ge(s2_gt_q, k + 1)
                act.activation(tiles(SG, k), tiles(GT, k), ACT.Sigmoid).then_inc(s2_sg, 1)
            for k in range(SLICES):
                act.wait_ge(s2_sg, k + 1)
                act.activation(tiles(SG, k), tiles(SG, k), ACT.Copy, scale=65536.0, bias=ROUND).then_inc(s2_sg_r, 1)
            act.wait_ge(s2_scale, 4)
            for k in range(SLICES):
                act.activation(tiles(GT, k), tiles(GT, k), ACT.Copy, scale=RC[:, 3:4], bias=ROUND).then_inc(s2_p_r, 1)
            act.wait_ge(s2_scale, 5)
            for k in range(SLICES):
                act.activation(tiles(GT, k), tiles(GT, k), ACT.Copy, scale=RC[:, 4:5], bias=ROUND).then_inc(s2_h_r, 1)

        def s2_dve(dve, link):
            def scale_of(n, last=None):
                dve.wait_ge(s2_all, n + 1)
                if last is not None:
                    link(dve.tensor_scalar(AR[:, n:n + 1], AR[:, n:n + 1], SC[:, last:last + 1], None, ALU.mult))
                link(dve.tensor_scalar(SC[:, n:n + 1], AR[:, n:n + 1], 1.0 / 32767.0, 1e-12, ALU.mult, ALU.max))
                if last is None:
                    dve.reciprocal(RC[:, n:n + 1], SC[:, n:n + 1]).then_inc(s2_scale, 1)
                else:
                    link(dve.reciprocal(RC[:, n:n + 1], SC[:, n:n + 1]))
                    dve.tensor_scalar(RC[:, n:n + 1], RC[:, n:n + 1], SC[:, last:last + 1], None,
                                      ALU.mult).then_inc(s2_scale, 1)
                dve.wait_ge(s2_scale, n + 1)

            def magnitude(n, v):
                dve.tensor_reduce(AM[:, n:n + 1], v, AX.XY, ALU.max, apply_absolute_value=True).then_inc(s2_mag, 1)

            layernorm_dve(dve, 2, link, finish=False)
            link.wait()
            magnitude(0, XN[:, :, :])
            scale_of(0)
            link(dve.tensor_scalar(XN[:, :, :], XN[:, :, :], RC[:, 0:1], ROUND, ALU.mult, ALU.add))
            for t in range(NT):
                dve.tensor_scalar(XN[:, t, :], XN[:, t, :], ROUND, SC[:, 0:1], ALU.subtract, ALU.mult).then_inc(ln_xn, 1)
            def tile_magnitudes(g):
                dve.wait_ge(s2_gt, g + 1)
                dve.tensor_reduce(TILE_MAG[:, 0, g:g + 1], GT[:, g, :], AX.X, ALU.max,
                                  apply_absolute_value=True).then_inc(s2_tmag, 1)
                dve.wait_ge(s2_up, g + 1)
                dve.tensor_reduce(TILE_MAG[:, 1, g:g + 1], UP[:, g, :], AX.X, ALU.max,
                                  apply_absolute_value=True).then_inc(s2_tmag, 1)

            for g in range(F0T):
                dve.wait_ge(s2_gt_psum, g + 1)
                dve.tensor_copy(GT[:, g, :], PS[:, (2 * g + 1) % 8, :]).then_inc(s2_gt, 1)
                if g:
                    tile_magnitudes(g - 1)
                if g % 2 and g < 8:
                    requantise(dve, link, 10 + g // 2)
            tile_magnitudes(F0T - 1)
            dve.wait_ge(s2_tmag, 2 * F0T)
            for n in range(2):
                dve.tensor_reduce(AM[:, n + 1:n + 2], TILE_MAG[:, n, :], AX.X, ALU.max).then_inc(s2_mag, 1)
            scale_of(1)
            scale_of(2)
            for k in range(SLICES):
                dve.wait_ge(s2_gt_r, k + 1)
                dve.tensor_scalar(tiles(GT, k), tiles(GT, k), ROUND, SC[:, 1:2], ALU.subtract,
                                  ALU.mult).then_inc(s2_gt_q, 1)
            for k in range(SLICES):
                dve.wait_ge(s2_sg_r, k + 1)
                link(dve.tensor_scalar(tiles(SG, k), tiles(SG, k), ROUND, 65535.0, ALU.subtract, ALU.min))
                link(dve.scalar_tensor_tensor(out=tiles(GT, k), in0=tiles(SG, k), scalar=1.0 / 65536.0, in1=tiles(GT, k),
                                              op0=ALU.mult, op1=ALU.mult))
                dve.tensor_reduce(TILE_MAG[:, 0, k:k + 1], tiles(GT, k), AX.XY, ALU.max,
                                  apply_absolute_value=True).then_inc(s2_tmag, 1)
            dve.wait_ge(s2_tmag, 2 * F0T + SLICES)
            dve.tensor_reduce(AM[:, 3:4], TILE_MAG[:, 0, 0:SLICES], AX.X, ALU.max).then_inc(s2_mag, 1)
            scale_of(3)
            for k in range(SLICES):
                dve.wait_ge(s2_p_r, k + 1)
                dve.wait_ge(s2_up_q, k + 1)
                link(dve.scalar_tensor_tensor(out=tiles(GT, k), in0=tiles(GT, k), scalar=ROUND, in1=tiles(UP, k),
                                              op0=ALU.subtract, op1=ALU.mult))
                dve.tensor_reduce(TILE_MAG[:, 1, k:k + 1], tiles(GT, k), AX.XY, ALU.max,
                                  apply_absolute_value=True).then_inc(s2_tmag, 1)
            dve.wait_ge(s2_tmag, 2 * F0T + 2 * SLICES)
            dve.tensor_reduce(AM[:, 4:5], TILE_MAG[:, 1, 0:SLICES], AX.X, ALU.max).then_inc(s2_mag, 1)
            scale_of(4, last=3)
            for k in range(SLICES):
                dve.wait_ge(s2_h_r, k + 1)
                dve.tensor_scalar(tiles(GT, k), tiles(GT, k), ROUND, SC[:, 4:5], ALU.subtract,
                                  ALU.mult).then_inc(s2_hid, 1)
            for t in range(NT):
                dve.wait_ge(out_psum, NT * 2 + t + 1)
                dve.tensor_tensor(X[:, t, :], PS[:, t, :], X[:, t, :], ALU.add).then_inc(x_done, 1)

        def s2_pe(pe):
            transpose_x_pe(pe, 2)
            pe.wait_ge(xt_ready, DT * 3)
            pe.wait_ge(s2_w, 8)
            for g in range(F0T):
                if g >= 4:
                    pe.wait_ge(s2_up, g - 3)
                    pe.wait_ge(s2_gt, g - 3)
                for w, bank, done in ((UPW, (2 * g) % 8, s2_up_psum), (GTW, (2 * g + 1) % 8, s2_gt_psum)):
                    for c in range(DT):
                        ins = pe.matmul(PS[:, bank, :], w[:, c, g * P:(g + 1) * P], XT[:, c, :],
                                        start=(c == 0), stop=(c == DT - 1))
                    ins.then_inc(done, 1)
            pe.wait_ge(s2_w, PIECES)
            for g in range(F0T):
                pe.wait_ge(s2_hid, g // PER + 1)
                for t in range(NT):
                    ins = pe.matmul(PS[:, t, :], GT[:, g, t * P:(t + 1) * P], DNW[:, g, :],
                                    start=(g == 0), stop=(g == F0T - 1))
                    if g == F0T - 1:
                        ins.then_inc(out_psum, 1)

        W12B = view(53 * K, [8, 2048], BF16)
        WQ1 = view(86 * K, [DT, D])
        WK1 = view(94 * K, [DT, P])
        WV1 = view(96 * K, [DT, DH])
        WC1 = view(97 * K, [DT, D])
        CR3 = view(106 * K, [2, CH, 512])
        CHI3 = view(122 * K, [2, CH, 512], F16)
        CLO3 = view(130 * K, [2, CH, 512], F16)
        QHI3 = view(138 * K, [DT, N], F16)
        QLO3 = view(142 * K, [DT, N], F16)
        QS = view(146 * K, [DT, N])
        TRAW = view(154 * K, [2048])
        TMID = view(162 * K, [2048])
        TOP8 = view(170 * K, [2, NT, 8])
        IDX8 = view(171 * K, [2, NT, 8], U32)
        TOPV = view(172 * K, [NCH, NT])
        TOPI = view(172 * K + 512, [NCH, NT])
        FROM_END = view(173 * K, [NCH, NT], I32)
        FROM_ENDF = view(173 * K + 512, [NCH, NT])
        BEST = view(174 * K, [NT])
        MEMIDX = view(174 * K + 64, [NT], U32)
        NMAX = view(174 * K + 512, [NT * ATT_H])
        RS3 = view(175 * K, [NT * ATT_H])
        MEM = view(106 * K, [NT, D])
        MEMT = view(114 * K, [DT, N])
        MKT = view(122 * K, [N])
        MVAL = view(124 * K, [NT, DH])
        PB = view(126 * K, [6, N])
        ATTT = view(138 * K, [DT, N])
        PTB = view(154 * K, [2, NT, N])
        UNITS = NT * ATT_H
        LAG = 4

        s3_clip = sem("s3_clip")
        s3_whole = sem("s3_whole")
        s3_tern = sem("s3_tern")
        s3_piece = sem("s3_piece")
        s3_q_psum = sem("s3_q_psum")
        s3_q_hi = sem("s3_q_hi")
        s3_q_lo = sem("s3_q_lo")
        s3_qs = sem("s3_qs")
        s3_chunk = [sem("s3_chunk0"), sem("s3_chunk1")]
        s3_hi = sem("s3_hi")
        s3_lo = sem("s3_lo")
        s3_scores = sem("s3_scores")
        s3_max = sem("s3_max")
        s3_idx = sem("s3_idx")
        s3_mem = sem("s3_mem")
        s3_memt_psum = sem("s3_memt_psum")
        s3_memt = sem("s3_memt")
        s3_kv_psum = sem("s3_kv_psum")
        s3_kv = sem("s3_kv")
        s3_logits = sem("s3_logits")
        s3_nmax = sem("s3_nmax")
        s3_p = sem("s3_p")
        s3_pt_psum = sem("s3_pt_psum")
        s3_pt = [sem("s3_pt_even"), sem("s3_pt_odd")]
        s3_pv = sem("s3_pv")
        s3_rs = sem("s3_rs")
        s3_pn = sem("s3_pn")
        s3_attt = sem("s3_attt")

        def s3_sp(sp):
            sp.wait_ge(s2_w, PIECES)
            sp.dma_start(WQ1, a["Wq1T"].rearrange("(t p) c -> p t c", p=P)).then_inc(w_in[3], 16)
            sp.dma_start(WK1, a["Wk1T"].rearrange("(t p) c -> p t c", p=P)).then_inc(w_in[3], 16)
            sp.dma_start(WV1, a["Wv1T"].rearrange("(t p) c -> p t c", p=P)).then_inc(w_in[3], 16)
            sp.dma_start(WC1, a["Wc1T"].rearrange("(t p) c -> p t c", p=P)).then_inc(w_in[3], 16)
            sp.wait_ge(pool_marks, POOL_MARK["s3_primed"])
            sp.wait_ge(s2_gt_psum, F0T)
            with sp.Fori(0, PAIRS) as i:
                for b in range(2):
                    sp.wait_ge(s3_hi, i * 2 + b + 1)
                    sp.wait_ge(s3_lo, i * 2 + b + 1)
                    sp.dma_start(CR3[:, b], a["ctxT"][i * 2 + b]).then_inc(s3_chunk[b], 16)
                sp.wait_ge(x_done, NT * 3)
                sp.wait_ge(s3_clip, i + 1)
                sp.dma_start(TRAW, a["w12"][i]).then_inc(s3_piece, 16)
            s4_loads(sp)

        def s3_pool(pool, link):
            pool.sem_inc(s3_hi, AHEAD_SPLIT)
            pool.sem_inc(s3_lo, AHEAD_SPLIT)
            pool.sem_inc(s3_clip, 1)
            pool.sem_inc(s3_scores, AHEAD_TILES)
            pool.sem_inc(s3_idx, AHEAD_BANK)
            pool.sem_inc(pool_marks, 1)
            pool.wait_ge(s2_gt_psum, F0T)
            with pool.Fori(0, PAIRS) as i:
                for b in range(2):
                    c = i * 2 + b
                    pool.wait_ge(s3_chunk[b], i * 16 + 16)
                    pool.wait_ge(s3_scores, c * CH + 1)
                    settle(pool)
                    pool.tensor_scalar(CHI3[:, b], CR3[:, b], 1.0, 0.0, ALU.mult, ALU.add).then_inc(s3_hi, 1)
                    pool.wait_ge(s3_hi, c + 1 + AHEAD_SPLIT)
                    pool.tensor_tensor(CLO3[:, b], CR3[:, b], CHI3[:, b], ALU.subtract).then_inc(s3_lo, 1)
            pool.wait_ge(x_done, NT * 3)
            pool.iota(FROM_END, pattern=[[-CH * P, NCH], [0, NT]], base=M, channel_multiplier=0).then_inc(pool_marks, 1)
            pool.wait_ge(dve_marks, DVE_MARK["s3_memidx"])
            for t in range(NT):
                pool.indirect_dma_start(out=MEM[:, t, :], out_offset=None, in_=a["ctx"],
                                        in_offset=bass.IndirectOffsetOnAxis(ap=MEMIDX[:, t:t + 1], axis=0)
                                        ).then_inc(s3_mem, 16)
            for u in range(UNITS):
                pool.wait_ge(s3_rs, u + 1)
                pool.tensor_scalar(PB[:, u % 6, :], PB[:, u % 6, :], RS3[:, u:u + 1], 1.0,
                                   ALU.mult, ALU.mult).then_inc(s3_pn, 1)

        def s3_act(act, link):
            layernorm_act(act, 3)
            transpose_x_act(act, 3)
            for e in range(DT):
                act.wait_ge(s3_q_psum, e + 1)
                act.copy(QHI3[:, e, :], PS[:, 4 + e, :]).then_inc(s3_q_hi, 1)
                act.wait_ge(s3_q_lo, e + 1)
                act.activation(QS[:, e, :], PS[:, 4 + e, :], ACT.Copy, scale=float(DH) ** -0.5).then_inc(s3_qs, 1)
            for c in range(DT):
                act.wait_ge(s3_memt_psum, c + 1)
                act.copy(MEMT[:, c, :], PS[:, c, :]).then_inc(s3_memt, 1)

            def turn(u):
                h, t = u // NT, u % NT
                act.wait_ge(s3_pt_psum, u + 1)
                if h >= 2:
                    act.wait_ge(s3_pv, h - 1)
                act.copy(PTB[:, h % 2, :, t * P:(t + 1) * P],
                         PS[:, 4 + u % 2, :].rearrange("p (m l) -> p m l", m=NT)).then_inc(s3_pt[1], 1)

            for u in range(UNITS + LAG):
                if u < UNITS:
                    act.wait_ge(s3_nmax, u + 1)
                    if u >= 6:
                        act.wait_ge(s3_pt_psum, u - 5)
                    act.activation(PB[:, u % 6, :], PS[:, u % 4, :], ACT.Exp, bias=NMAX[:, u:u + 1],
                                   accum_out=RS3[:, u:u + 1]).then_inc(s3_p, 1)
                if u >= LAG and (u - LAG) % 2:
                    turn(u - LAG)
                if u >= LAG + 3 and (u - LAG - 3) % 16 == 15:
                    g = (u - LAG - 3) // 16
                    act.wait_ge(s3_pv, 4 * (g + 1))
                    act.copy(ATTT[:, g, :], PS[:, 6 + g % 2, :]).then_inc(s3_attt, 1)
            act.wait_ge(s3_pv, ATT_H)
            act.copy(ATTT[:, DT - 1, :], PS[:, 6 + (DT - 1) % 2, :]).then_inc(s3_attt, 1)

        def s3_dve(dve, link):
            layernorm_dve(dve, 3, link)
            for e in range(DT):
                dve.wait_ge(s3_q_hi, e + 1)
                dve.tensor_tensor(QLO3[:, e, :], PS[:, 4 + e, :], QHI3[:, e, :], ALU.subtract).then_inc(s3_q_lo, 1)
            with dve.Fori(0, PAIRS) as i:
                for b in range(2):
                    c = i * 2 + b
                    for t in range(NT):
                        dve.wait_ge(s3_scores, c * CH + t + 1 + AHEAD_TILES)
                        settle(dve)
                        dve.max(TOP8[:, b, t, :], PS[:, b * CH + t, :]).then_inc(s3_max, 1)
                    for t in range(NT):
                        dve.wait_ge(s3_max, c * CH + t + 1)
                        settle(dve)
                        dve.max_index(IDX8[:, b, t, :], TOP8[:, b, t, :], PS[:, b * CH + t, :]).then_inc(s3_idx, 1)
                    dve.tensor_copy(TOPV[:, c, :], TOP8[:, b, :, 0])
                    dve.wait_ge(s3_idx, c * CH + CH + AHEAD_BANK)
                    dve.tensor_copy(TOPI[:, c, :], IDX8[:, b, :, 0])
                dve.wait_ge(s3_piece, i * 16 + 16)
                dve.tensor_scalar(TMID, TRAW, W_RECIP[:, bass.ds(i, 1)], 1.0, ALU.mult, ALU.min).then_inc(s3_clip, 1)
                dve.wait_ge(s3_clip, i + 2)
                dve.tensor_scalar(TMID, TMID, -1.0, ROUND, ALU.max, ALU.add).then_inc(s3_whole, 1)
                dve.wait_ge(s3_whole, i + 1)
                dve.tensor_scalar(W12B[:, i, :], TMID, ROUND, None, ALU.subtract).then_inc(s3_tern, 1)
            dve.wait_ge(pool_marks, POOL_MARK["s3_iota"])
            link(dve.tensor_copy(FROM_ENDF, FROM_END))
            link(dve.tensor_reduce(BEST, TOPV.rearrange("p c t -> p t c"), AX.X, ALU.max))
            link(dve.tensor_tensor(TOPI, FROM_ENDF, TOPI, ALU.subtract))
            link(dve.tensor_tensor(TOPV, TOPV, BEST.unsqueeze(1).to_broadcast([P, NCH, NT]), ALU.is_equal))
            link(dve.tensor_tensor(TOPI, TOPI, TOPV, ALU.mult))
            link(dve.tensor_reduce(BEST, TOPI.rearrange("p c t -> p t c"), AX.X, ALU.max))
            dve.tensor_scalar(MEMIDX, BEST, -1.0, float(M), ALU.mult, ALU.add).then_inc(dve_marks, 1)
            dve.wait_ge(s3_kv_psum, 2)
            dve.tensor_copy(MKT, PS[:, 4, :]).then_inc(s3_kv, 1)
            dve.tensor_copy(MVAL.rearrange("p a b -> p (a b)"), PS[:, 5, 0:NT * DH]).then_inc(s3_kv, 1)

            def turn(u):
                h, t = u // NT, u % NT
                dve.wait_ge(s3_pt_psum, u + 1)
                if h >= 2:
                    dve.wait_ge(s3_pv, h - 1)
                dve.tensor_copy(PTB[:, h % 2, :, t * P:(t + 1) * P],
                                PS[:, 4 + u % 2, :].rearrange("p (m l) -> p m l", m=NT)).then_inc(s3_pt[0], 1)

            for u in range(UNITS + LAG):
                if u < UNITS:
                    dve.wait_ge(s3_logits, u + 1)
                    dve.tensor_reduce(NMAX[:, u:u + 1], PS[:, u % 4, :], AX.X, ALU.max,
                                      negate=True).then_inc(s3_nmax, 1)
                if 1 <= u <= UNITS:
                    dve.wait_ge(s3_p, u)
                    dve.reciprocal(RS3[:, u - 1:u], RS3[:, u - 1:u]).then_inc(s3_rs, 1)
                if u >= LAG and (u - LAG) % 2 == 0:
                    turn(u - LAG)
            for t in range(NT):
                dve.wait_ge(out_psum, NT * 3 + t + 1)
                dve.tensor_tensor(X[:, t, :], PS[:, 4 + t, :], X[:, t, :], ALU.add).then_inc(x_done, 1)

        def s3_pe(pe):
            transpose_x_pe(pe, 3)
            pe.wait_ge(xt_ready, DT * 4)
            pe.wait_ge(w_in[3], 64)
            for e in range(DT):
                for c in range(DT):
                    ins = pe.matmul(PS[:, 4 + e, :], WQ1[:, c, e * P:(e + 1) * P], XT[:, c, :],
                                    start=(c == 0), stop=(c == DT - 1))
                ins.then_inc(s3_q_psum, 1)
            pe.wait_ge(s3_q_lo, DT)
            pe.wait_ge(s3_qs, DT)
            with pe.Fori(0, PAIRS) as i:
                for b in range(2):
                    c = i * 2 + b
                    pe.wait_ge(s3_hi, c + 1 + AHEAD_SPLIT)
                    pe.wait_ge(s3_lo, c + 1 + AHEAD_SPLIT)
                    for t in range(NT):
                        pe.wait_ge(s3_idx, c * CH + t + 1)
                        bank = PS[:, b * CH + t, :]
                        cols = slice(t * P, (t + 1) * P)
                        for e in range(DT):
                            pe.matmul(bank, QHI3[:, e, cols], CHI3[:, b, e, :], start=(e == 0), stop=False)
                            pe.matmul(bank, QHI3[:, e, cols], CLO3[:, b, e, :], start=False, stop=False)
                            ins = pe.matmul(bank, QLO3[:, e, cols], CHI3[:, b, e, :], start=False,
                                            stop=(e == DT - 1))
                        ins.then_inc(s3_scores, 1)
            pe.wait_ge(s3_idx, MT + AHEAD_BANK)
            pe.wait_ge(s3_mem, 16 * NT)
            for c in range(DT):
                for t in range(NT):
                    ins = pe.transpose(PS[:, c, t * P:(t + 1) * P], MEM[:, t, c * P:(c + 1) * P], IDENT[:, :])
                ins.then_inc(s3_memt_psum, 1)
            pe.wait_ge(s3_memt, DT)
            for c in range(DT):
                ins = pe.matmul(PS[:, 4, :], WK1[:, c, :], MEMT[:, c, :], start=(c == 0), stop=(c == DT - 1))
            ins.then_inc(s3_kv_psum, 1)
            for t in range(NT):
                for c in range(DT):
                    ins = pe.matmul(PS[:, 5, t * DH:(t + 1) * DH], MEMT[:, c, t * P:(t + 1) * P], WV1[:, c, :],
                                    start=(c == 0), stop=(c == DT - 1))
            ins.then_inc(s3_kv_psum, 1)
            pe.wait_ge(s3_kv, 2)

            def logits(u):
                h, t = u // NT, u % NT
                rows = slice(DH * (h % 4), DH * (h % 4) + DH)
                if u >= 4:
                    pe.wait_ge(s3_p, u - 3)
                pe.matmul(PS[:, u % 4, :], QS[rows, h // 4, t * P:(t + 1) * P], MKT[rows, :],
                          start=True, stop=True).then_inc(s3_logits, 1)

            def turn(u):
                pe.wait_ge(s3_pn, u + 1)
                if u >= 2:
                    pe.wait_ge(s3_pt[u % 2], u // 2)
                for m in range(NT):
                    ins = pe.transpose(PS[:, 4 + u % 2, m * P:(m + 1) * P], PB[:, u % 6, m * P:(m + 1) * P],
                                       IDENT[:, :])
                ins.then_inc(s3_pt_psum, 1)

            def weigh(h):
                pe.wait_ge(s3_pt[0], 2 * h + 2)
                pe.wait_ge(s3_pt[1], 2 * h + 2)
                if h >= 8:
                    pe.wait_ge(s3_attt, h // 4 - 1)
                for m in range(NT):
                    ins = pe.matmul(PS[DH * (h % 4):DH * (h % 4) + DH, 6 + (h // 4) % 2, :], MVAL[:, m, :],
                                    PTB[:, h % 2, m, :], start=(m == 0), stop=(m == NT - 1))
                ins.then_inc(s3_pv, 1)

            for u in range(UNITS + LAG + 2):
                if u < UNITS:
                    logits(u)
                if LAG <= u < UNITS + LAG:
                    turn(u - LAG)
                if u >= LAG + 2 and (u - LAG - 2) % NT == NT - 1:
                    weigh((u - LAG - 2) // NT)
            pe.wait_ge(s3_attt, DT)
            for t in range(NT):
                for c in range(DT):
                    ins = pe.matmul(PS[:, 4 + t, :], ATTT[:, c, t * P:(t + 1) * P], WC1[:, c, :],
                                    start=(c == 0), stop=(c == DT - 1))
                ins.then_inc(out_psum, 1)

        WIN = view(0, [DT, PROJ])
        WOUT = view(37 * K, [IT, D])
        XBC = view(85 * K, [CVT, N + 3])
        CV = view(106 * K, [CVT, N])
        ZG = view(127 * K, [NT, SSM_I])
        YS = view(143 * K, [NT, SSM_I])
        DTX = view(85 * K, [SSM_I])
        WDTX = view(89 * K, [SSM_I])
        DECAY = view(93 * K, [SSM_H, P])
        BNAT = view(163 * K, [P])
        HS = view(101 * K, [SSM_I])
        TMP = view(159 * K, [SSM_I])
        YT = view(106 * K, [IT, N])
        SMALL = 164 * K
        CONVW = view(SMALL, [CVT, 4])
        CONVB = view(SMALL + 256, [CVT])
        DTB = view(SMALL + 512, [SSM_H])
        ALOG = view(SMALL + 768, [SSM_H])
        SSMD = view(SMALL + 1024, [SSM_H])
        NORMW = view(SMALL + 1280, [IT])
        DTV = view(SMALL + 1536, [NT, SSM_H])
        DTA = view(SMALL + 1792, [NT, SSM_H])
        DTE = view(SMALL + 2048, [NT, SSM_H])
        LA = view(SMALL + 2304, [3, SSM_H])
        ELA = view(SMALL + 2560, [3, SSM_H])
        NLA = view(SMALL + 2816, [SSM_H])
        MS = view(SMALL + 3072, [NT])
        RMS = view(SMALL + 3328, [NT])

        s4_conv_psum = sem("s4_conv_psum")
        s4_conv_in = sem("s4_conv_in")
        s4_conv = sem("s4_conv")
        s4_cv = sem("s4_cv")
        s4_z_psum = sem("s4_z_psum")
        s4_z = sem("s4_z")
        s4_small = sem("s4_small")
        s4_read = sem("s4_read")
        s4_la = sem("s4_la")
        s4_ela = sem("s4_ela")
        s4_decay_psum = sem("s4_decay_psum")
        s4_decay = sem("s4_decay")
        s4_mix = sem("s4_mix")
        s4_wdtx = sem("s4_wdtx")
        s4_intra = sem("s4_intra")
        s4_inter = sem("s4_inter")
        s4_add = sem("s4_add")
        s4_state = sem("s4_state")
        s4_hs = sem("s4_hs")
        s4_ys = sem("s4_ys")
        s4_ms = sem("s4_ms")
        s4_yn = sem("s4_yn")
        s4_yt_psum = sem("s4_yt_psum")
        s4_yt = sem("s4_yt")

        def heads(v, n=SSM_H):
            return v.rearrange("p (h c) -> p h c", h=n)

        def s4_loads(sp):
            sp.dma_start(WIN, a["WinT"].rearrange("(t p) c -> p t c", p=P)).then_inc(w_in[4], 16)
            sp.dma_start(WOUT, a["WoutT"].rearrange("(t p) c -> p t c", p=P)).then_inc(w_in[4], 16)

        def s4_sp(sp):
            sp.wait_ge(x_done, NT * 4)
            for dst, name in ((CONVW, "convw"), (CONVB, "convb"), (NORMW, "normw")):
                sp.dma_start(dst, a[name]).then_inc(small_in, 16)
            for dst, name in ((DTB, "dtb"), (ALOG, "alog"), (SSMD, "ssmd")):
                sp.dma_start(dst, a[name].partition_broadcast(P)).then_inc(small_in, 16)

        def s4_pool(pool, link):
            pool.wait_ge(x_done, NT * 4)
            pool.memset(XBC[:, :, 0:3], 0.0).then_inc(pool_marks, 1)

        def s4_act(act, link):
            layernorm_act(act, 4)
            transpose_x_act(act, 4)
            act.wait_ge(dve_marks, DVE_MARK["s4_dtb"])
            link(act.activation(DTE, DTV, ACT.Abs))
            link(act.activation(DTE, DTE, ACT.Exp, scale=-1.0))
            act.wait_ge(small_in, 6 * 16)
            link(act.activation(ALOG, ALOG, ACT.Exp))
            act.activation(DTE, DTE, ACT.Ln, bias=1.0).then_inc(act_marks, 1)
            for g in range(CVT + 2):
                if g < CVT:
                    act.wait_ge(s4_conv_psum, g + 1)
                    act.copy(XBC[:, g, 3:], PS[:, g % 4, :]).then_inc(s4_conv_in, 1)
                if g >= 2:
                    act.wait_ge(s4_conv, g - 1)
                    act.activation(CV[:, g - 2, :], CV[:, g - 2, :], ACT.Silu).then_inc(s4_cv, 1)
            for g in range(2 * NT):
                act.wait_ge(s4_z_psum, g + 1)
                act.activation(ZG[:, g // 2, (g % 2) * 512:(g % 2 + 1) * 512], PS[:, 4 + g % 2, :],
                               ACT.Silu).then_inc(s4_z, 1)
            for q in range(NT):
                act.wait_ge(s4_la, q + 1)
                act.activation(ELA, LA, ACT.Exp).then_inc(s4_ela, 1)
                if q:
                    act.wait_ge(s4_intra, q)
                for h in range(SSM_H):
                    act.wait_ge(s4_decay_psum, (SSM_H * q + h) // 4 + 1)
                    ins = act.activation(DECAY[:, h, :], PS[:, 4 + h // 4, (h % 4) * P:(h % 4 + 1) * P], ACT.Exp,
                                         bias=NLA[:, h:h + 1])
                    if h % 4 == 3:
                        ins.then_inc(s4_decay, 1)
            for q in range(NT):
                act.wait_ge(s4_ys, q + 1)
                act.activation(ZG[:, q, :], YS[:, q, :], ACT.Square, accum_out=MS[:, q:q + 1]).then_inc(s4_ms, 1)
                act.wait_ge(s4_ms, q + 1)
            act.activation(RMS, MS, ACT.Sqrt, scale=1.0 / SSM_I, bias=EPSC[:, 0:1]).then_inc(act_marks, 1)
            for c in range(IT):
                act.wait_ge(s4_yt_psum, c + 1)
                if c == 0:
                    act.wait_ge(small_in, 6 * 16)
                act.activation(YT[:, c, :], PS[:, c % 4, :], ACT.Copy, scale=NORMW[:, c:c + 1]).then_inc(s4_yt, 1)

        def s4_dve(dve, link):
            layernorm_dve(dve, 4, link)
            dve.wait_ge(small_in, 6 * 16)
            dve.wait_ge(pe_marks, PE_MARK["s4_dt_psum"])
            dve.tensor_tensor(DTV, PS[:, 6, 0:NT * SSM_H].rearrange("p (t h) -> p t h", t=NT),
                              DTB.unsqueeze(1).to_broadcast([P, NT, SSM_H]), ALU.add).then_inc(dve_marks, 1)
            dve.wait_ge(act_marks, ACT_MARK["s4_softplus"])
            link(dve.scalar_tensor_tensor(out=DTV, in0=DTV, scalar=0.0, in1=DTE, op0=ALU.max, op1=ALU.add))
            link(dve.tensor_scalar(ALOG, ALOG, -1.0, None, ALU.mult))
            dve.tensor_tensor(DTA, DTV, ALOG.unsqueeze(1).to_broadcast([P, NT, SSM_H]), ALU.mult).then_inc(dve_marks, 1)
            dve.wait_ge(pool_marks, POOL_MARK["s4_pad"])
            for g in range(CVT):
                dve.wait_ge(s4_conv_in, g + 1)
                link(dve.tensor_scalar(CV[:, g, :], XBC[:, g, 0:N], CONVW[:, g, 0:1], CONVB[:, g:g + 1],
                                       ALU.mult, ALU.add))
                for k in range(1, 4):
                    ins = dve.scalar_tensor_tensor(out=CV[:, g, :], in0=XBC[:, g, k:k + N], scalar=CONVW[:, g, k:k + 1],
                                                   in1=CV[:, g, :], op0=ALU.mult, op1=ALU.add)
                    if k < 3:
                        link(ins)
                    else:
                        ins.then_inc(s4_conv, 1)
            dve.wait_ge(s4_conv, CVT)
            dve.memset(HS, 0.0).then_inc(s4_hs, 1)
            for q in range(NT):
                dve.wait_ge(s4_small, q + 1)
                if q:
                    dve.wait_ge(s4_decay, 4 * q)
                link(dve.tensor_copy(LA[:, 0, :], PS[:, 2, P:P + SSM_H]))
                link(dve.tensor_copy(LA[:, 2, :], PS[:, 2, P + SSM_H:P + 2 * SSM_H]))
                link(dve.tensor_scalar(NLA, LA[:, 0, :], -1.0, None, ALU.mult))
                dve.tensor_tensor(LA[:, 1, :], LA[:, 2, :], LA[:, 0, :], ALU.subtract).then_inc(s4_la, 1)
                link(dve.tensor_copy(BNAT, PS[:, 2, 0:P]))
                xs = PS[:, 0:2, :].rearrange("p a (h c) -> p (a h) c", c=SSM_P)
                link(dve.tensor_tensor(heads(DTX), xs, DTV[:, q, :].unsqueeze(2).to_broadcast([P, SSM_H, SSM_P]),
                                       ALU.mult))
                dve.tensor_tensor(heads(YS[:, q, :]), xs, SSMD.unsqueeze(2).to_broadcast([P, SSM_H, SSM_P]),
                                  ALU.mult).then_inc(s4_read, 1)
                dve.wait_ge(s4_ela, q + 1)
                dve.tensor_tensor(heads(WDTX), heads(DTX), ELA[:, 1, :].unsqueeze(2).to_broadcast([P, SSM_H, SSM_P]),
                                  ALU.mult).then_inc(s4_wdtx, 1)
                for g in range(4):
                    dve.wait_ge(s4_decay, 4 * q + g + 1)
                    dve.tensor_tensor(DECAY[:, 4 * g:4 * g + 4, :], DECAY[:, 4 * g:4 * g + 4, :],
                                      PS[:, 3, 0:P].unsqueeze(1).to_broadcast([P, 4, P]), ALU.mult).then_inc(s4_mix, 1)
                dve.wait_ge(s4_read, q + 1)
                dve.wait_ge(s4_intra, q + 1)
                link(dve.tensor_tensor(YS[:, q, :], PS[:, 0:2, :].rearrange("p a b -> p (a b)"), YS[:, q, :], ALU.add))
                if q:
                    dve.wait_ge(s4_inter, q)
                    link(dve.tensor_tensor(heads(TMP), PS[:, 4:6, :].rearrange("p a (h c) -> p (a h) c", c=SSM_P),
                                           ELA[:, 0, :].unsqueeze(2).to_broadcast([P, SSM_H, SSM_P]), ALU.mult))
                    link(dve.tensor_tensor(YS[:, q, :], YS[:, q, :], TMP, ALU.add))
                dve.wait_ge(s4_z, 2 * q + 2)
                dve.tensor_tensor(YS[:, q, :], YS[:, q, :], ZG[:, q, :], ALU.mult).then_inc(s4_ys, 1)
                dve.wait_ge(s4_hs, q + 1)
                link(dve.tensor_tensor(heads(HS), heads(HS), ELA[:, 2, :].unsqueeze(2).to_broadcast([P, SSM_H, SSM_P]),
                                       ALU.mult))
                dve.wait_ge(s4_state, q + 1)
                dve.tensor_tensor(HS, HS, PS[:, 6:8, :].rearrange("p a b -> p (a b)"), ALU.add).then_inc(s4_hs, 1)
            dve.wait_ge(act_marks, ACT_MARK["s4_rms"])
            link(dve.reciprocal(RMS, RMS))
            for q in range(NT):
                dve.tensor_scalar(YS[:, q, :], YS[:, q, :], RMS[:, q:q + 1], None, ALU.mult).then_inc(s4_yn, 1)
            for t in range(NT):
                dve.wait_ge(out_psum, NT * 4 + t + 1)
                dve.tensor_tensor(X[:, t, :], PS[:, 4 + t, :], X[:, t, :], ALU.add).then_inc(x_done, 1)

        def s4_pe(pe):
            transpose_x_pe(pe, 4)
            pe.wait_ge(xt_ready, DT * 5)
            pe.wait_ge(w_in[4], 2 * 16)
            for t in range(NT):
                for c in range(DT):
                    ins = pe.matmul(PS[:, 6, t * SSM_H:(t + 1) * SSM_H], XT[:, c, t * P:(t + 1) * P],
                                    WIN[:, c, PROJ - SSM_H:PROJ], start=(c == 0), stop=(c == DT - 1))
            ins.then_inc(pe_marks, 1)
            for g in range(CVT):
                if g >= 4:
                    pe.wait_ge(s4_conv_in, g - 3)
                for c in range(DT):
                    ins = pe.matmul(PS[:, g % 4, :], WIN[:, c, SSM_I + g * P:SSM_I + (g + 1) * P], XT[:, c, :],
                                    start=(c == 0), stop=(c == DT - 1))
                ins.then_inc(s4_conv_psum, 1)
            for g in range(2 * NT):
                if g >= 2:
                    pe.wait_ge(s4_z, g - 1)
                t, half = g // 2, g % 2
                for c in range(DT):
                    ins = pe.matmul(PS[:, 4 + half, :], XT[:, c, t * P:(t + 1) * P],
                                    WIN[:, c, half * 512:(half + 1) * 512], start=(c == 0), stop=(c == DT - 1))
                ins.then_inc(s4_z_psum, 1)
            pe.wait_ge(dve_marks, DVE_MARK["s4_dta"])
            pe.wait_ge(s4_cv, CVT)
            pe.wait_ge(s4_z, 2 * NT)
            for q in range(NT):
                cols = slice(q * P, (q + 1) * P)
                if q:
                    pe.wait_ge(s4_ys, q)
                    pe.wait_ge(s4_hs, q + 1)
                for c in range(IT):
                    pe.transpose(PS[:, c // 4, (c % 4) * P:(c % 4 + 1) * P], CV[:, c, cols], IDENT[:, :])
                pe.transpose(PS[:, 2, 0:P], CV[:, IT, cols], IDENT[:, :])
                pe.matmul(PS[:, 2, P:P + SSM_H], UPPER[:, :], DTA[:, q, :], start=True, stop=True)
                pe.matmul(PS[:, 2, P + SSM_H:P + 2 * SSM_H], ONES[:, :], DTA[:, q, :], start=True, stop=True)
                pe.matmul(PS[:, 3, 0:P], CV[:, IT, cols], CV[:, IT + 1, cols], start=True, stop=True).then_inc(s4_small, 1)
                for g in range(4):
                    for h in range(4):
                        at = PS[:, 4 + g, h * P:(h + 1) * P]
                        pe.matmul(at, IDENTB[:, :], FUTUREB[:, :], start=True, stop=False)
                        ins = pe.matmul(at, DTA[:, q, 4 * g + h:4 * g + h + 1].to_broadcast([P, P]), UPPER[:, :],
                                        start=False, stop=True)
                    ins.then_inc(s4_decay_psum, 1)
                pe.wait_ge(s4_read, q + 1)
                for h in range(SSM_H):
                    pe.wait_ge(s4_mix, 4 * q + h // 4 + 1)
                    ins = pe.matmul(PS[:, h // 8, (h % 8) * SSM_P:(h % 8 + 1) * SSM_P], DECAY[:, h, :],
                                    DTX[:, h * SSM_P:(h + 1) * SSM_P], start=True, stop=True)
                ins.then_inc(s4_intra, 1)
                if q:
                    for half in range(2):
                        ins = pe.matmul(PS[:, 4 + half, :], CV[:, IT + 1, cols], HS[:, half * 512:(half + 1) * 512],
                                        start=True, stop=True)
                    ins.then_inc(s4_inter, 1)
                pe.wait_ge(s4_wdtx, q + 1)
                for half in range(2):
                    ins = pe.matmul(PS[:, 6 + half, :], BNAT, WDTX[:, half * 512:(half + 1) * 512], start=True, stop=True)
                ins.then_inc(s4_state, 1)
            pe.wait_ge(s4_yn, NT)
            pe.wait_ge(s4_hs, NT + 1)
            for c in range(IT):
                if c >= 4:
                    pe.wait_ge(s4_yt, c - 3)
                for t in range(NT):
                    ins = pe.transpose(PS[:, c % 4, t * P:(t + 1) * P], YS[:, t, c * P:(c + 1) * P], IDENT[:, :])
                ins.then_inc(s4_yt_psum, 1)
            pe.wait_ge(s4_yt, IT)
            for t in range(NT):
                for c in range(IT):
                    ins = pe.matmul(PS[:, 4 + t, :], YT[:, c, t * P:(t + 1) * P], WOUT[:, c, :],
                                    start=(c == 0), stop=(c == IT - 1))
                ins.then_inc(out_psum, 1)

        W1B = view(53 * K, [DT, FF1], BF16)
        W2B = view(69 * K, [F1T, D], BF16)
        XQT = view(85 * K, [DT, N], BF16)
        HT = view(89 * K, [F1T, N + 2])
        CO = view(122 * K, [F1T, N])
        HQ = view(154 * K, [F1T, N], BF16)
        ROWSC = view(170 * K, [N])
        AMX = view(172 * K, [N])
        AMB = view(174 * K, [N])
        HSC = view(176 * K, [N])
        FCW = view(0, [F1T, 3])
        FCB = view(1 * K, [F1T])
        HABS = view(2 * K, [2, N])
        XCL = COLS[:, 0:4]
        XSC = COLS[:, 4:8]
        XINV = COLS[:, 8:12]
        OSC = COLS[:, 20:24]

        s5_h_psum = sem("s5_h_psum")
        s5_h = sem("s5_h")
        s5_conv = sem("s5_conv")
        s5_silu = sem("s5_silu")
        s5_habs = sem("s5_habs")
        s5_mag = sem("s5_mag")
        s5_hq = sem("s5_hq")

        def s5_sp(sp):
            sp.wait_ge(x_done, NT * 5)
            sp.dma_start(FCW, a["fconvw"]).then_inc(w_in[5], 16)
            sp.dma_start(FCB, a["fconvb"]).then_inc(w_in[5], 16)

        def s5_pool(pool, link):
            pool.wait_ge(x_done, NT * 5)
            pool.memset(HT[:, :, 0:1], 0.0)
            pool.memset(HT[:, :, N + 1:N + 2], 0.0).then_inc(pool_marks, 1)
            pool.wait_ge(s5_mag, F1T + 1)
            pool.partition_all_reduce(AMB, AMX, P, RMAX).then_inc(pool_marks, 1)

        def s5_act(act, link):
            layernorm_act(act, 5)
            for c in range(DT):
                act.wait_ge(xt_psum, DT * 5 + c + 1)
                act.copy(XQT[:, c, :], PS[:, c, :]).then_inc(xt_ready, 1)
            for g in range(F1T):
                act.wait_ge(s5_conv, g + 1)
                act.activation(CO[:, g, :], CO[:, g, :], ACT.Silu).then_inc(s5_silu, 1)
                act.wait_ge(s5_silu, g + 1)
                if g >= 2:
                    act.wait_ge(s5_mag, g)
                act.activation(HABS[:, g % 2, :], CO[:, g, :], ACT.Abs).then_inc(s5_habs, 1)

        def s5_dve(dve, link):
            layernorm_dve(dve, 5, link, finish=False)
            link.wait()
            link(dve.tensor_reduce(XCL, XN[:, :, :], AX.X, ALU.max, apply_absolute_value=True))
            link(dve.tensor_scalar(XCL, XCL, 1e-5, None, ALU.max))
            link(dve.reciprocal(XSC, XCL))
            link(dve.tensor_scalar(XSC, XSC, 127.0, None, ALU.mult))
            for t in range(NT):
                link(dve.tensor_scalar(XN[:, t, :], XN[:, t, :], XSC[:, t:t + 1], ROUND, ALU.mult, ALU.add))
                dve.tensor_scalar(XN[:, t, :], XN[:, t, :], ROUND, None, ALU.subtract).then_inc(ln_xn, 1)
            dve.tensor_scalar(XINV, XCL, 1.0 / 127.0, W_MEAN[:, 0:1], ALU.mult, ALU.mult).then_inc(dve_marks, 1)
            dve.wait_ge(w_in[5], 32)
            dve.wait_ge(pe_marks, PE_MARK["s5_row_psum"])
            dve.tensor_copy(ROWSC, PS[:, 4, :]).then_inc(dve_marks, 1)
            dve.wait_ge(dve_marks, DVE_MARK["s5_row"])
            dve.wait_ge(pool_marks, POOL_MARK["s5_pad"])
            dve.memset(AMX, 0.0).then_inc(s5_mag, 1)

            def magnitude(g):
                dve.wait_ge(s5_habs, g + 1)
                dve.wait_ge(s5_mag, g + 1)
                dve.tensor_tensor(AMX, HABS[:, g % 2, :], AMX, ALU.max).then_inc(s5_mag, 1)

            for g in range(F1T):
                dve.wait_ge(s5_h_psum, g + 1)
                dve.tensor_tensor(HT[:, g, 1:N + 1], PS[:, g % 8, :], ROWSC, ALU.mult).then_inc(s5_h, 1)
                dve.wait_ge(s5_h, g + 1)
                link(dve.tensor_scalar(CO[:, g, :], HT[:, g, 0:N], FCW[:, g, 0:1], FCB[:, g:g + 1], ALU.mult, ALU.add))
                link(dve.scalar_tensor_tensor(out=CO[:, g, :], in0=HT[:, g, 1:N + 1], scalar=FCW[:, g, 1:2],
                                              in1=CO[:, g, :], op0=ALU.mult, op1=ALU.add))
                dve.scalar_tensor_tensor(out=CO[:, g, :], in0=HT[:, g, 2:N + 2], scalar=FCW[:, g, 2:3],
                                         in1=CO[:, g, :], op0=ALU.mult, op1=ALU.add).then_inc(s5_conv, 1)
                if g:
                    magnitude(g - 1)
            magnitude(F1T - 1)
            dve.wait_ge(pool_marks, POOL_MARK["s5_amb"])
            dve.tensor_scalar(AMB, AMB, 1e-5, None, ALU.max).then_inc(dve_marks, 1)
            dve.wait_ge(dve_marks, DVE_MARK["s5_amb2"])
            link(dve.reciprocal(HSC, AMB))
            link(dve.tensor_scalar(HSC, HSC, 127.0, None, ALU.mult))
            for g in range(F1T):
                link(dve.tensor_tensor(CO[:, g, :], CO[:, g, :], HSC, ALU.mult))
                dve.tensor_scalar(HQ[:, g, :], CO[:, g, :], ROUND, ROUND, ALU.add, ALU.subtract).then_inc(s5_hq, 1)
            dve.wait_ge(pe_marks, PE_MARK["s5_col_psum"])
            link(dve.tensor_scalar(OSC, PS[:, 4, 0:NT], 1.0 / 127.0, W_MEAN[:, 1:2], ALU.mult, ALU.mult))
            for t in range(NT):
                dve.wait_ge(out_psum, NT * 5 + t + 1)
                dve.scalar_tensor_tensor(out=X[:, t, :], in0=PS[:, t, :], scalar=OSC[:, t:t + 1], in1=X[:, t, :],
                                         op0=ALU.mult, op1=ALU.add).then_inc(x_done, 1)

        def s5_pe(pe):
            transpose_x_pe(pe, 5)
            pe.wait_ge(dve_marks, DVE_MARK["s5_xinv"])
            for t in range(NT):
                ins = pe.matmul(PS[:, 4, t * P:(t + 1) * P], XINV[:, t:t + 1].to_broadcast([P, P]), IDENT[:, :],
                                start=True, stop=True)
            ins.then_inc(pe_marks, 1)
            pe.wait_ge(xt_ready, DT * 6)
            pe.wait_ge(s3_tern, 8)
            pe.wait_ge(dve_marks, DVE_MARK["s5_row"])
            for g in range(F1T):
                if g >= 8:
                    pe.wait_ge(s5_h, g - 7)
                for c in range(DT):
                    ins = pe.matmul(PS[:, g % 8, :], W1B[:, c, g * P:(g + 1) * P], XQT[:, c, :],
                                    start=(c == 0), stop=(c == DT - 1))
                ins.then_inc(s5_h_psum, 1)
            pe.wait_ge(dve_marks, DVE_MARK["s5_amb2"])
            for t in range(NT):
                ins = pe.matmul(PS[:, 4, t:t + 1], AMB[0:1, t * P:(t + 1) * P], ONES[0:1, 0:1], start=True, stop=True)
            ins.then_inc(pe_marks, 1)
            pe.wait_ge(s5_hq, F1T)
            for t in range(NT):
                for g in range(F1T):
                    ins = pe.matmul(PS[:, t, :], HQ[:, g, t * P:(t + 1) * P], W2B[:, g, :],
                                    start=(g == 0), stop=(g == F1T - 1))
                ins.then_inc(out_psum, 1)

        out_done = sem("out_done")
        block = ctx.enter_context(nc.Block())

        @block.sync
        def _(sp):
            sp.dma_start(X[:, :, :], a["x"].rearrange("(t p) c -> p t c", p=P)).then_inc(x_in, 16)
            for part in (s0_sp, s3_sp, s4_sp, s5_sp):
                part(sp)
            sp.wait_ge(x_done, NT * 6)
            sp.dma_start(out.rearrange("(t p) c -> p t c", p=P), X[:, :, :]).then_inc(out_done, 16)
            sp.wait_ge(out_done, 16)

        @block.gpsimd
        def _(pool):
            link = Order(pool, pool_order)
            setup_pool(pool, link)
            for part in (s0_pool, s1_pool, s2_pool, s3_pool, s4_pool, s5_pool):
                part(pool, link)

        @block.scalar
        def _(act):
            link = Order(act, act_order)
            act.wait_ge(pool_marks, POOL_MARK["const_ready"])
            for part in (s0_act, s1_act, s2_act, s3_act, s4_act, s5_act):
                part(act, link)

        @block.vector
        def _(dve):
            link = Order(dve, dve_order)
            dve.wait_ge(x_in, 16)
            dve.wait_ge(pool_marks, POOL_MARK["const_ready"])
            for part in (s0_dve, s1_dve, s2_dve, s3_dve, s4_dve, s5_dve):
                part(dve, link)

        @block.tensor
        def _(pe):
            pe.wait_ge(pool_marks, POOL_MARK["const_ready"])
            for part in (s0_pe, s1_pe, s2_pe, s3_pe, s4_pe, s5_pe):
                part(pe)


def kernel(**inputs):
    import numpy as np
    import concourse.bacc as bacc
    from concourse import mybir as mb
    from concourse.bass_utils import run_bass_kernel_spmd

    nc = bacc.Bacc("TRN2", target_bir_lowering=False, num_devices=1)
    arrays, aps = {}, {}
    for name, value in layout(inputs, np).items():
        value = np.ascontiguousarray(value)
        arrays[f"in_{name}"] = value
        aps[name] = nc.dram_tensor(f"in_{name}", value.shape, mb.dt.from_np(value.dtype), kind="ExternalInput").ap()
    out = nc.dram_tensor("out_latents", (N, D), F32, kind="ExternalOutput").ap()
    perceiver_kernel(nc, aps, out)
    r = run_bass_kernel_spmd(nc, [arrays], core_ids=[0])
    return r.results[0]["out_latents"].reshape(1, N, D)
```

```python
from contextlib import ExitStack

import concourse.bass as bass
from concourse import mybir

F32 = mybir.dt.float32
F16 = mybir.dt.float16
BF16 = mybir.dt.bfloat16
I32 = mybir.dt.int32
U32 = mybir.dt.uint32
ALU = mybir.AluOpType
ACT = mybir.ActivationFunctionType
AX = mybir.AxisListType
RMAX = bass.bass_isa.ReduceOp.max
RADD = bass.bass_isa.ReduceOp.add

P = 128
D = 512
DT = D // P
N = 512
NT = N // P
M = 8192
MT = M // P
CH = 4
NCH = MT // CH
PAIRS = NCH // 2
EPS = 1e-5
ROUND = 12582912.0
FF0 = 1536
F0T = FF0 // P
QB = 32
ATT_H = 16
DH = D // ATT_H
SSM_H = 16
SSM_P = 64
SSM_I = SSM_H * SSM_P
SSM_N = 128
CONV = SSM_I + 2 * SSM_N
CVT = CONV // P
IT = SSM_I // P
PROJ = 2 * SSM_I + 2 * SSM_N + SSM_H
FF1 = 2048
F1T = FF1 // P
QP = PROJ // 4
W_UP = 64.0
NEG = -1e30
Q_SCALE = float(D // 8) ** -0.5


def layout(v, np):
    def arr(name):
        return np.asarray(v[name])

    def blocks32(w):
        o, i = w.shape
        return w.reshape(o // QB, QB, i // P, P // QB, QB).transpose(3, 1, 2, 0, 4).reshape(P, (i // P) * o)

    def columns(x):
        return x.reshape(-1, P).T

    ctx = arr("ctx_1024")[0]
    qkv = arr("L0_xattn_qkv_w")
    wkv = arr("L1_xattn_Wkv")
    w_in = arr("L1_attn_W_in")
    out = {
        "x": arr("x")[0],
        "ctx": ctx,
        "ctxT": ctx.T.reshape(DT, P, NCH, CH * P).transpose(2, 1, 0, 3),
        "mask": arr("mask_S2_ik0").reshape(MT, P).T,
        "wq0": qkv[:D], "wk0": qkv[D:2 * D], "wvT0": qkv[2 * D:].T,
        "projT0": arr("L0_xattn_proj_w").T, "projb0": arr("L0_xattn_proj_b"),
        "lam": columns(np.repeat(arr("L0_attn_decay")[:, 1, 0], D // 16)),
        "lng": columns(arr("L0_attn_ln_g")), "lnb": columns(arr("L0_attn_ln_b")),
        "WvT": arr("L0_attn_Wv").T, "WqT": arr("L0_attn_Wq").T, "WgT": arr("L0_attn_Wg").T,
        "WoT": arr("L0_attn_Wo").T,
        "ffnB": np.concatenate([blocks32(arr("L0_ffn_w_" + n)).reshape(P, 4, FF0) for n in ("gate", "up", "down")],
                               axis=1).transpose(1, 0, 2),
        "Wq1T": arr("L1_xattn_Wq").T,
        "Wk1T": np.tile(wkv[:DH].T, (1, P // DH)), "Wv1T": np.tile(wkv[DH:].T, (1, P // DH)),
        "Wc1T": arr("L1_xattn_Wc").T,
        "WinT": w_in.T.reshape(DT, P, 4, QP).transpose(0, 2, 1, 3).reshape(16, P, QP),
        "convw": arr("L1_attn_conv_w").reshape(CVT, P, 4).transpose(1, 0, 2), "convb": columns(arr("L1_attn_conv_b")),
        "dtb": arr("L1_attn_dt_bias"), "alog": arr("L1_attn_A_log"), "ssmd": arr("L1_attn_D"),
        "normw": columns(arr("L1_attn_norm_w")), "WoutT": arr("L1_attn_W_out").T,
        "w12": np.concatenate([arr("L1_ffn_w1").T.reshape(DT, P, FF1),
                               arr("L1_ffn_w2").T.reshape(4, F1T // 4, P, D).transpose(0, 2, 1, 3).reshape(4, P, FF1)]),
        "fconvw": arr("L1_ffn_conv_w").reshape(F1T, P, 3).transpose(1, 0, 2),
        "fconvb": columns(arr("L1_ffn_conv_b")),
    }
    return out


def perceiver_kernel(nc, a, out):
    ctx = ExitStack()
    with ctx:
        def sb(name, shape, dt):
            return ctx.enter_context(nc.sbuf_tensor(name, shape, dt))

        def sem(name):
            return ctx.enter_context(nc.semaphore(name))

        X = sb("X", [P, NT, D], F32)
        XN = sb("XN", [P, NT, D], F32)
        XT = sb("XT", [P, DT, N], F32)
        IDENT = sb("IDENT", [P, P], F32)
        ONES = sb("ONES", [P, P], F32)
        MEANW = sb("MEANW", [P, P], F32)
        UPPER = sb("UPPER", [P, P], F32)
        IDENTB = sb("IDENTB", [P, P], BF16)
        FUTUREB = sb("FUTUREB", [P, P], BF16)
        ZROW = sb("ZROW", [1, D], F16)
        MASKI = sb("MASKI", [P, MT], I32)
        MASK = sb("MASK", [P, MT], F32)
        W_RECIP = sb("W_RECIP", [P, 8], F32)
        W_MEAN = sb("W_MEAN", [P, 2], F32)
        MASKC = sb("MASKC", [P, 2, CH], F32)
        EPSC = sb("EPSC", [P, 1], F32)
        STATS = sb("STATS", [P, NT, 6], F32)
        MV = sb("MV", [P, NT, 2], F32)
        STD = sb("STD", [P, NT], F32)
        RSTD = sb("RSTD", [P, NT], F32)
        COLS = sb("COLS", [P, 64], F32)
        SM = sb("SM", [P, 64], F32)
        arena = sb("arena", [P, 178 * 256], F32)
        PS = ctx.enter_context(nc.psum_tensor("PS", [P, 8, 512], F32))

        def view(at, shape, dt=F32):
            size = 2 if dt in (F16, BF16) else 4
            n = 1
            for s in shape:
                n *= s
            v = arena[:, at // 4:(at + n * size) // 4]
            if dt != F32:
                v = v.bitcast(dt)
            if len(shape) == 1:
                return v
            if len(shape) == 2:
                return v.rearrange("p (a b) -> p a b", a=shape[0])
            return v.rearrange("p (a b c) -> p a b c", a=shape[0], b=shape[1])

        K = 1024
        def marks(*names):
            return {name: n + 1 for n, name in enumerate(names)}

        PE_MARK = marks("s0_close", "s0_den", "s1_mean", "s1_var", "s4_dt_psum", "s4_sums", "s5_row_psum", "s5_mag_psum", "s5_scale_psum")
        DVE_MARK = marks("s0_mask", "s1_rstd", "w_scale", "s3_memidx", "s4_dtb", "s4_dta", "s4_sums_read", "s4_la", "s5_xinv", "s5_row", "s5_scale",
                          "s5_out_scale")
        ACT_MARK = marks("s1_std", "s4_softplus", "s4_ela", "s4_rms")
        POOL_MARK = marks("s0_primed", "const_ready", "s1_wall", "s3_primed", "s3_iota", "s4_pad", "s4_wout", "s5_pad")
        pe_marks = sem("pe_marks")
        dve_marks = sem("dve_marks")
        act_marks = sem("act_marks")
        pool_marks = sem("pool_marks")
        w_in = {i: sem(f"w_in{i}") for i in (0, 1, 3, 4)}
        raw_in = [sem(f"raw_in{i}") for i in range(2)]
        small_in = sem("small_in")
        x_in = sem("x_in")
        x_done = sem("x_done")
        out_psum = sem("out_psum")
        ln_stats = sem("ln_stats")
        ln_var = sem("ln_var")
        ln_std = sem("ln_std")
        ln_rstd = sem("ln_rstd")
        ln_xn = sem("ln_xn")
        xt_psum = sem("xt_psum")
        xt_hi = sem("xt_hi")
        xt_ready = sem("xt_ready")
        dve_order = sem("dve_order")
        settled = sem("settled")
        act_order = sem("act_order")
        pool_order = sem("pool_order")

        def settle(eng):
            eng.sem_inc(settled, 1)

        def norm_tile(dve, stage, t):
            n = NT * stage + t + 1
            dve.bn_stats(STATS[:, t, :], X[:, t, :]).then_inc(ln_stats, 1)
            dve.wait_ge(ln_stats, n)
            dve.bn_aggr(MV[:, t, :], STATS[:, t, :]).then_inc(ln_var, 1)
            dve.wait_ge(ln_std, n)
            dve.reciprocal(RSTD[:, t:t + 1], STD[:, t:t + 1]).then_inc(ln_rstd, 1)
            dve.wait_ge(ln_rstd, n)
            return dve.tensor_scalar(XN[:, t, :], X[:, t, :], MV[:, t, 0:1], RSTD[:, t:t + 1],
                                     ALU.subtract, ALU.mult)

        def norm_act(act, stage):
            for t in range(NT):
                act.wait_ge(ln_var, NT * stage + t + 1)
                act.activation(STD[:, t:t + 1], MV[:, t, 1:2], ACT.Sqrt, bias=EPSC[:, 0:1]).then_inc(ln_std, 1)

        def add_tile(dve, stage, t, scale=None):
            dve.wait_ge(out_psum, NT * stage + t + 1)
            if scale is None:
                ins = dve.tensor_tensor(X[:, t, :], PS[:, 4 + t, :], X[:, t, :], ALU.add)
            else:
                ins = dve.scalar_tensor_tensor(out=X[:, t, :], in0=PS[:, 4 + t, :], scalar=scale, in1=X[:, t, :],
                                               op0=ALU.mult, op1=ALU.add)
            ins.then_inc(x_done, 1)
            dve.wait_ge(x_done, NT * stage + t + 1)

        def turn_tile(pe, stage, t):
            pe.wait_ge(ln_xn, NT * stage + t + 1)
            for c in range(DT):
                ins = pe.transpose(PS[:, c, t * P:(t + 1) * P], XN[:, t, c * P:(c + 1) * P], IDENT[:, :])
                if t == NT - 1:
                    ins.then_inc(xt_psum, 1)

        def keep_warm(pe, bank, rounds):
            with pe.Fori(0, rounds):
                for _ in range(8):
                    pe.matmul(PS[:, bank, 0:P], IDENT[:, :], ONES[:, :], start=True, stop=True)

        def matmul_split(pe, out, weights, moving, c, n):
            (w_hi, w_lo), (m_hi, m_lo) = weights, moving
            pe.matmul(out, w_hi, m_hi, start=(c == 0), stop=False)
            pe.matmul(out, w_hi, m_lo, start=False, stop=False)
            return pe.matmul(out, w_lo, m_hi, start=False, stop=(c == n - 1))

        def transpose_x_act(act, stage):
            for c in range(DT):
                act.wait_ge(xt_psum, DT * stage + c + 1)
                act.copy(XT[:, c, :], PS[:, c, :]).then_inc(xt_ready, 1)

        class Order:

            def __init__(self, eng, s):
                self.eng, self.s, self.n = eng, s, 0

            def __call__(self, ins):
                self.n += 1
                ins.then_inc(self.s, 1)
                self.eng.wait_ge(self.s, self.n)

            def note(self, ins):
                self.n += 1
                ins.then_inc(self.s, 1)

            def wait(self):
                self.eng.wait_ge(self.s, self.n)

        XT_HI = XT[:, 0:2, :].rearrange("p a b -> p (a b)").bitcast(F16).rearrange("p (c n) -> p c n", c=DT)
        XT_LO = XT[:, 2:4, :].rearrange("p a b -> p (a b)").bitcast(F16).rearrange("p (c n) -> p c n", c=DT)

        def split_x_act(act, stage):
            for c in range(DT):
                act.wait_ge(xt_psum, DT * stage + c + 1)
                act.copy(XT_HI[:, c, :], PS[:, c, :]).then_inc(xt_hi, 1)

        def split_x_dve(dve, before):
            for c in range(DT):
                dve.wait_ge(xt_hi, DT * before + c + 1)
                dve.tensor_tensor(XT_LO[:, c, :], PS[:, c, :], XT_HI[:, c, :], ALU.subtract).then_inc(xt_ready, 1)

        ST = view(0, [MT, N])
        CR = view(128 * K, [2, CH, 512])
        CHI = view(144 * K, [2, CH, 512], F16)
        CLO = view(152 * K, [2, CH, 512], F16)
        QHI = view(160 * K, [DT, N], F16)
        QLO = view(164 * K, [DT, N], F16)
        PHI = view(160 * K, [CH, N], F16)
        PLO = view(172 * K, [CH, N], F16)
        PSUMS = view(164 * K, [N])
        RUNMAX = view(168 * K, [N])
        COLMAX = view(170 * K, [N])
        WQ = view(0, [DT, D])
        WK = view(8 * K, [DT, D])
        WQK = view(16 * K, [DT, D])
        PROJT = XN
        WVT = XT
        O = view(0, [NT, D])
        Z = view(8 * K, [DT, D])
        BIAS = view(16 * K, [D])

        s0_w = [sem("s0_w0"), sem("s0_w1")]
        s0_wqk_psum = sem("s0_wqk_psum")
        s0_wqk = sem("s0_wqk")
        s0_q_psum = sem("s0_q_psum")
        s0_q_hi = sem("s0_q_hi")
        s0_q_lo = sem("s0_q_lo")
        s0_chunk = [sem("s0_chunk0"), sem("s0_chunk1")]
        s0_hi = sem("s0_hi")
        s0_lo = sem("s0_lo")
        s0_scores = sem("s0_scores")
        s0_max = sem("s0_max")
        s0_copied = sem("s0_copied")
        s0_row = [sem("s0_row0"), sem("s0_row1")]
        s0_shift = sem("s0_shift")
        s0_exp = sem("s0_exp")
        s0_p_hi = sem("s0_p_hi")
        s0_p_lo = sem("s0_p_lo")
        s0_sum = sem("s0_sum")
        s0_c_hi = sem("s0_c_hi")
        s0_c_lo = sem("s0_c_lo")
        s0_pv = sem("s0_pv")
        s0_maskc = sem("s0_maskc")
        s0_o = sem("s0_o")
        s0_z_psum = sem("s0_z_psum")
        s0_z = sem("s0_z")

        ctxT = a["ctxT"]
        ctx_rows = a["ctx"].rearrange("(k j p) c -> k p j c", j=CH, p=P)

        BANKS = 8
        AHEAD_SPLIT = 2
        AHEAD_TILES = CH + 1
        AHEAD_BANK = BANKS

        def s0_sp(sp):
            for h in range(2):
                tiles = slice(2 * h, 2 * h + 2)
                for dst, name in ((WQ, "wq0"), (WK, "wk0")):
                    sp.dma_start(dst[:, tiles, :],
                                 a[name].rearrange("(t p) c -> p t c", p=P)[:, tiles, :]).then_inc(s0_w[h], 16)
                if h == 0:
                    sp.dma_start(X[:, :, :], a["x"].rearrange("(t p) c -> p t c", p=P)).then_inc(x_in, 16)
            sp.dma_start(MASKI[:, :], a["mask"]).then_inc(small_in, 16)
            sp.wait_ge(pool_marks, POOL_MARK["s0_primed"])
            with sp.Fori(0, PAIRS) as i:
                for b in range(2):
                    sp.wait_ge(s0_hi, i * 2 + b + 1)
                    sp.wait_ge(s0_lo, i * 2 + b + 1)
                    sp.dma_start(CR[:, b], a["ctxT"][i * 2 + b]).then_inc(s0_chunk[b], 16)
            sp.dma_start(WVT[:, :, :], a["wvT0"].rearrange("(t p) c -> p t c", p=P)).then_inc(w_in[0], 16)
            sp.dma_start(PROJT[:, :, :], a["projT0"].rearrange("(t p) c -> p t c", p=P)).then_inc(w_in[0], 16)
            sp.wait_ge(s0_hi, NCH + AHEAD_SPLIT)
            sp.wait_ge(s0_lo, NCH + AHEAD_SPLIT)
            with sp.Fori(0, PAIRS) as i:
                for b in range(2):
                    sp.wait_ge(s0_c_hi, (i * 2 + b) * CH + 1)
                    sp.wait_ge(s0_c_lo, (i * 2 + b) * CH + 1)
                    sp.dma_start(CR[:, b], ctx_rows[i * 2 + b]).then_inc(s0_row[b], 16)
            sp.wait_ge(pe_marks, PE_MARK["s0_close"])
            sp.dma_start(BIAS, a["projb0"].partition_broadcast(P)).then_inc(small_in, 16)
            s1_loads(sp)
            s2_loads(sp)

        def setup_pool(pool, link):
            link(pool.memset(IDENT[:, :], 0.0))
            link(pool.affine_select(out=IDENT[:, :], in_=IDENT[:, :], compare_op=ALU.not_equal, fill=1.0,
                                    base=0, pattern=[[-1, P]], channel_multiplier=1))
            link(pool.memset(ONES[:, :], 1.0))
            link(pool.affine_select(out=UPPER[:, :], in_=ONES[:, :], compare_op=ALU.is_ge, fill=0.0,
                                    base=0, pattern=[[1, P]], channel_multiplier=-1))
            link(pool.tensor_copy(IDENTB[:, :], IDENT[:, :]))
            link(pool.memset(FUTUREB[:, :], 0.0))
            link(pool.affine_select(out=FUTUREB[:, :], in_=FUTUREB[:, :], compare_op=ALU.is_ge, fill=NEG,
                                    base=0, pattern=[[1, P]], channel_multiplier=-1))
            link(pool.memset(MEANW[:, :], 1.0 / D))
            link(pool.memset(EPSC[:, :], EPS))
            link(pool.memset(ZROW[:, :], 0.0))
            pool.sem_inc(s0_hi, AHEAD_SPLIT)
            pool.sem_inc(s0_lo, AHEAD_SPLIT)
            for s in (s0_scores, s0_c_hi, s0_c_lo, s0_pv):
                pool.sem_inc(s, AHEAD_TILES)
            pool.sem_inc(s0_copied, AHEAD_BANK)
            pool.sem_inc(pool_marks, 1)
            pool.sem_inc(pool_marks, 1)

        def s0_pool(pool, link):
            with pool.Fori(0, PAIRS) as i:
                for b in range(2):
                    c = i * 2 + b
                    pool.wait_ge(s0_chunk[b], i * 16 + 16)
                    pool.wait_ge(s0_scores, c * CH + 1)
                    settle(pool)
                    pool.tensor_scalar(CHI[:, b], CR[:, b], 1.0, 0.0, ALU.mult, ALU.add).then_inc(s0_hi, 1)
                    pool.wait_ge(s0_hi, c + 1 + AHEAD_SPLIT)
                    pool.tensor_tensor(CLO[:, b], CR[:, b], CHI[:, b], ALU.subtract).then_inc(s0_lo, 1)
            pool.wait_ge(s0_max, MT + 1)
            link(pool.partition_all_reduce(COLMAX, RUNMAX, P, RMAX))
            pool.wait_ge(s0_copied, MT + AHEAD_BANK)
            pool.wait_ge(dve_marks, DVE_MARK["s0_mask"])
            with pool.Fori(0, PAIRS) as i:
                for b in range(2):
                    c = i * 2 + b
                    for j in range(CH):
                        pool.tensor_tensor(ST[:, c * CH + j, :], ST[:, c * CH + j, :], COLMAX,
                                           ALU.subtract).then_inc(s0_shift, 1)
                        if j == 0:
                            pool.wait_ge(s0_row[b], i * 16 + 16)
                            pool.wait_ge(s0_maskc, c + 1)
                            pool.wait_ge(s0_pv, c * CH + 1)
                            settle(pool)
                        pool.tensor_scalar(CHI[:, b, j, :], CR[:, b, j, :], MASKC[:, b, j:j + 1], 0.0,
                                           ALU.mult, ALU.add).then_inc(s0_c_hi, 1)

        def s0_act(act, link):
            norm_act(act, 0)
            for c in range(DT):
                act.wait_ge(s0_wqk_psum, c + 1)
                act.copy(WQK[:, c, :], PS[:, 4 + c, :]).then_inc(s0_wqk, 1)
            transpose_x_act(act, 0)
            for c in range(DT):
                act.wait_ge(s0_q_psum, c + 1)
                act.activation(QHI[:, c, :], PS[:, c, :], ACT.Copy, scale=Q_SCALE).then_inc(s0_q_hi, 1)
            with act.Fori(0, PAIRS) as i:
                for b in range(2):
                    for j in range(CH):
                        k = (i * 2 + b) * CH + j
                        act.wait_ge(s0_scores, k + 1 + AHEAD_TILES)
                        act.activation(ST[:, k, :], PS[:, b * CH + j, :], ACT.Copy).then_inc(s0_copied, 1)
            with act.Fori(0, PAIRS) as i:
                for b in range(2):
                    c = i * 2 + b
                    for j in range(CH):
                        k = c * CH + j
                        act.wait_ge(s0_shift, k + 1)
                        act.activation(ST[:, k, :], ST[:, k, :], ACT.Exp).then_inc(s0_exp, 1)
                        act.wait_ge(s0_exp, k + 1)
                        act.wait_ge(s0_pv, k + 2)
                        settle(act)
                        act.copy(PHI[:, j, :], ST[:, k, :]).then_inc(s0_p_hi, 1)
            for c in range(DT):
                act.wait_ge(s0_z_psum, c + 1)
                act.copy(Z[:, c, :], PS[:, c, :]).then_inc(s0_z, 1)
                if c:
                    add_round(act, c - 1)
            norm_act(act, 1)

        def s0_dve(dve, link):
            for t in range(NT):
                norm_tile(dve, 0, t).then_inc(ln_xn, 1)
            dve.wait_ge(small_in, 16)
            dve.tensor_scalar(MASK[:, :], MASKI[:, :], 0.0, None, ALU.not_equal).then_inc(dve_marks, 1)
            for c in range(DT):
                dve.wait_ge(s0_q_hi, c + 1)
                dve.scalar_tensor_tensor(out=QLO[:, c, :], in0=PS[:, c, :], scalar=Q_SCALE, in1=QHI[:, c, :],
                                         op0=ALU.mult, op1=ALU.subtract).then_inc(s0_q_lo, 1)
            dve.memset(RUNMAX, -3.0e38).then_inc(s0_max, 1)
            with dve.Fori(0, PAIRS) as i:
                for b in range(2):
                    for j in range(CH):
                        k = (i * 2 + b) * CH + j
                        dve.wait_ge(s0_copied, k + 1 + AHEAD_BANK)
                        dve.wait_ge(s0_max, k + 1)
                        dve.tensor_tensor(RUNMAX, ST[:, k, :], RUNMAX, ALU.max).then_inc(s0_max, 1)
            dve.wait_ge(dve_marks, DVE_MARK["s0_mask"])
            dve.memset(PSUMS, 0.0).then_inc(s0_sum, 1)
            with dve.Fori(0, PAIRS) as i:
                for b in range(2):
                    c = i * 2 + b
                    dve.wait_ge(s0_c_lo, c * CH + 1)
                    dve.tensor_copy(MASKC[:, b, :], MASK[:, bass.ds(c * CH, CH)]).then_inc(s0_maskc, 1)
                    dve.wait_ge(s0_maskc, c + 1)
                    dve.wait_ge(s0_pv, c * CH + 1)
                    for j in range(CH):
                        k = c * CH + j
                        dve.wait_ge(s0_c_hi, k + 1 + AHEAD_TILES)
                        dve.scalar_tensor_tensor(out=CLO[:, b, j, :], in0=CR[:, b, j, :],
                                                 scalar=MASKC[:, b, j:j + 1], in1=CHI[:, b, j, :],
                                                 op0=ALU.mult, op1=ALU.subtract).then_inc(s0_c_lo, 1)
                        dve.wait_ge(s0_p_hi, k + 1)
                        dve.wait_ge(s0_pv, k + 2)
                        dve.tensor_tensor(PLO[:, j, :], ST[:, k, :], PHI[:, j, :],
                                          ALU.subtract).then_inc(s0_p_lo, 1)
                        dve.wait_ge(s0_sum, k + 1)
                        dve.tensor_tensor(PSUMS, PSUMS, ST[:, k, :], ALU.add).then_inc(s0_sum, 1)
            dve.wait_ge(pe_marks, PE_MARK["s0_den"])
            link(dve.reciprocal(COLS[:, 0:NT], PS[:, 4, 0:NT]))
            for t in range(NT):
                dve.tensor_scalar(O[:, t, :], PS[:, t, :], COLS[:, t:t + 1], None, ALU.mult).then_inc(s0_o, 1)
            for p in range(4):
                requantise(dve, link, p)
            dve.wait_ge(small_in, 2 * 16)
            for t in range(NT):
                link(dve.tensor_tensor(X[:, t, :], X[:, t, :], BIAS, ALU.add))
            for t in range(NT):
                add_tile(dve, 0, t)
                norm_tile(dve, 1, t).then_inc(ln_xn, 1)

        def s0_pe(pe):
            for d in range(DT):
                pe.wait_ge(s0_w[d // 2], 32)
                for c in range(DT):
                    ins = pe.matmul(PS[:, 4 + c, :], WQ[:, d, c * P:(c + 1) * P], WK[:, d, :],
                                    start=(d == 0), stop=(d == DT - 1))
                    if d == DT - 1:
                        ins.then_inc(s0_wqk_psum, 1)
            for t in range(NT):
                turn_tile(pe, 0, t)
            pe.wait_ge(xt_ready, DT)
            pe.wait_ge(s0_wqk, DT)
            for e in range(DT):
                for c in range(DT):
                    ins = pe.matmul(PS[:, e, :], WQK[:, c, e * P:(e + 1) * P], XT[:, c, :],
                                    start=(c == 0), stop=(c == DT - 1))
                ins.then_inc(s0_q_psum, 1)
            pe.wait_ge(s0_q_hi, DT)
            pe.wait_ge(s0_q_lo, DT)
            with pe.Fori(0, PAIRS) as i:
                for b in range(2):
                    c = i * 2 + b
                    pe.wait_ge(s0_hi, c + 1 + AHEAD_SPLIT)
                    pe.wait_ge(s0_lo, c + 1 + AHEAD_SPLIT)
                    for j in range(CH):
                        k = c * CH + j
                        pe.wait_ge(s0_copied, k + 1)
                        bank = PS[:, b * CH + j, :]
                        cols = slice(j * P, (j + 1) * P)
                        for e in range(DT):
                            pe.matmul(bank, CHI[:, b, e, cols], QHI[:, e, :], start=(e == 0), stop=False)
                            pe.matmul(bank, CHI[:, b, e, cols], QLO[:, e, :], start=False, stop=False)
                            ins = pe.matmul(bank, CLO[:, b, e, cols], QHI[:, e, :], start=False,
                                            stop=(e == DT - 1))
                        ins.then_inc(s0_scores, 1)
            pe.wait_ge(s0_copied, MT + AHEAD_BANK)
            for t in range(NT):
                pe.matmul(PS[:, t, :], ZROW[:, 0:P], ZROW[:, :], start=True, stop=False)
            with pe.Fori(0, PAIRS) as i:
                for b in range(2):
                    for j in range(CH):
                        k = (i * 2 + b) * CH + j
                        pe.wait_ge(s0_c_hi, k + 1 + AHEAD_TILES)
                        pe.wait_ge(s0_c_lo, k + 1 + AHEAD_TILES)
                        pe.wait_ge(s0_p_hi, k + 1)
                        pe.wait_ge(s0_p_lo, k + 1)
                        for t in range(NT):
                            cols = slice(t * P, (t + 1) * P)
                            pe.matmul(PS[:, t, :], PHI[:, j, cols], CHI[:, b, j, :], start=False, stop=False)
                            pe.matmul(PS[:, t, :], PHI[:, j, cols], CLO[:, b, j, :], start=False, stop=False)
                            ins = pe.matmul(PS[:, t, :], PLO[:, j, cols], CHI[:, b, j, :], start=False, stop=False)
                        ins.then_inc(s0_pv, 1)
            for t in range(NT):
                ins = pe.matmul(PS[:, t, :], ZROW[:, 0:P], ZROW[:, :], start=False, stop=True)
            ins.then_inc(pe_marks, 1)
            pe.wait_ge(s0_sum, MT + 1)
            for t in range(NT):
                ins = pe.matmul(PS[:, 4, t:t + 1], PSUMS[:, t * P:(t + 1) * P], ONES[:, 0:1], start=True, stop=True)
            ins.then_inc(pe_marks, 1)
            pe.wait_ge(w_in[0], 32)
            pe.wait_ge(s0_o, NT)
            for c in range(DT):
                for t in range(NT):
                    ins = pe.matmul(PS[:, c, :], O[:, t, c * P:(c + 1) * P], PROJT[:, t, :],
                                    start=(t == 0), stop=(t == NT - 1))
                ins.then_inc(s0_z_psum, 1)
            pe.wait_ge(s0_z, DT)
            for t in range(NT):
                for c in range(DT):
                    ins = pe.matmul(PS[:, 4 + t, :], WVT[:, c, t * P:(t + 1) * P], Z[:, c, :],
                                    start=(c == 0), stop=(c == DT - 1))
                ins.then_inc(out_psum, 1)
                if t:
                    turn_tile(pe, 1, t - 1)
            turn_tile(pe, 1, NT - 1)

        RW = view(18 * K, [4, DT, D])
        STATE = view(50 * K, [DT, N])
        SQ = STATE
        Y = view(58 * K, [DT, N])
        GATE = view(66 * K, [DT, N])
        RSTDB = view(74 * K, [N])
        WABS = view(0, [2, 2048])
        LAM, LNG, LNB = SM[:, 0:DT], SM[:, DT:2 * DT], SM[:, 2 * DT:3 * DT]

        s1_proj = sem("s1_proj")
        s1_state = sem("s1_state")
        s1_y = sem("s1_y")
        s1_gate = sem("s1_gate")
        s1_cent = sem("s1_cent")
        s1_sq = sem("s1_sq")
        s1_mod = sem("s1_mod")
        s1_abs = sem("s1_abs")

        def s1_loads(sp):
            for n, name in enumerate(("WvT", "WqT", "WgT", "WoT")):
                sp.dma_start(RW[:, n], a[name].rearrange("(t p) c -> p t c", p=P)).then_inc(w_in[1], 16)
            for dst, name in ((LAM, "lam"), (LNG, "lng"), (LNB, "lnb")):
                sp.dma_start(dst, a[name]).then_inc(w_in[1], 16)

        def s1_pool(pool, link):
            scale_pieces(pool, 0, 9)
            pool.wait_ge(s1_abs, 8)
            pool.partition_all_reduce(COLS[:, 56:64], COLS[:, 48:56], P, RADD).then_inc(pool_marks, 1)

        def s1_act(act, link):
            act.wait_ge(x_done, NT * 1)
            for r in range(2):
                act.dma_start(WABS[:, r, :], a["w12"][r]).then_inc(raw_in[r], 16)
            transpose_x_act(act, 1)
            for e in range(DT):
                for r in (2 * e, 2 * e + 1):
                    act.wait_ge(raw_in[r % 2], 16 * (r // 2 + 1))
                    act.activation(WABS[:, r % 2, :], WABS[:, r % 2, :], ACT.Abs,
                                   accum_out=COLS[:, 48 + r:49 + r]).then_inc(s1_abs, 1)
                add_round(act, 3 + e)
                if e < DT - 1:
                    for r in (2 * e + 2, 2 * e + 3):
                        act.wait_ge(s1_abs, r - 1)
                        act.dma_start(WABS[:, r % 2, :], a["w12"][r]).then_inc(raw_in[r % 2], 16)
                act.wait_ge(s1_proj, 3 * e + 3)
                act.activation(GATE[:, e, :], PS[:, (3 * e + 2) % 8, :], ACT.Silu).then_inc(s1_gate, 1)
            add_round(act, 7)
            for e in range(DT):
                act.wait_ge(s1_cent, e + 1)
                act.activation(SQ[:, e, :], Y[:, e, :], ACT.Square).then_inc(s1_sq, 1)
            act.wait_ge(pe_marks, PE_MARK["s1_var"])
            act.activation(RSTDB, PS[:, 5, :], ACT.Sqrt, bias=EPSC[:, 0:1]).then_inc(act_marks, 1)
            norm_act(act, 2)

        def s1_dve(dve, link):
            requantise(dve, link, 4)
            dve.wait_ge(w_in[1], 7 * 16)
            for e in range(DT):
                dve.wait_ge(s1_proj, 3 * e + 1)
                dve.tensor_tensor_scan(STATE[:, e, :], LAM[:, e:e + 1].to_broadcast([P, N]), PS[:, (3 * e) % 8, :],
                                       0.0, ALU.mult, ALU.add).then_inc(s1_state, 1)
                dve.wait_ge(s1_state, e + 1)
                dve.wait_ge(s1_proj, 3 * e + 2)
                dve.tensor_tensor(Y[:, e, :], PS[:, (3 * e + 1) % 8, :], STATE[:, e, :],
                                  ALU.mult).then_inc(s1_y, 1)
                requantise(dve, link, 5 + e)
            dve.wait_ge(s1_y, DT)
            dve.wait_ge(pe_marks, PE_MARK["s1_mean"])
            for e in range(DT):
                dve.tensor_tensor(Y[:, e, :], Y[:, e, :], PS[:, 4, :], ALU.subtract).then_inc(s1_cent, 1)
            dve.wait_ge(act_marks, ACT_MARK["s1_std"])
            dve.reciprocal(RSTDB, RSTDB).then_inc(dve_marks, 1)
            dve.wait_ge(dve_marks, DVE_MARK["s1_rstd"])
            dve.wait_ge(s1_gate, DT)
            for e in range(DT):
                link(dve.scalar_tensor_tensor(out=Y[:, e, :], in0=Y[:, e, :], scalar=LNG[:, e:e + 1], in1=RSTDB,
                                              op0=ALU.mult, op1=ALU.mult))
                dve.scalar_tensor_tensor(out=Y[:, e, :], in0=Y[:, e, :], scalar=LNB[:, e:e + 1], in1=GATE[:, e, :],
                                         op0=ALU.add, op1=ALU.mult).then_inc(s1_mod, 1)
            requantise(dve, link, 9)
            dve.wait_ge(pool_marks, POOL_MARK["s1_wall"])
            link(dve.tensor_reduce(W_MEAN[:, :], COLS[:, 56:64].rearrange("p (w n) -> p w n", w=2), AX.X, ALU.add))
            link(dve.tensor_scalar(W_MEAN[:, :], W_MEAN[:, :], 1.0 / (FF1 * D), 1e-5, ALU.mult, ALU.max))
            dve.reciprocal(W_RECIP[:, :].rearrange("p (w n) -> p w n", w=2),
                           W_MEAN[:, :].unsqueeze(2).to_broadcast([P, 2, 4])).then_inc(dve_marks, 1)
            for t in range(NT):
                add_tile(dve, 1, t)
                link(norm_tile(dve, 2, t))
                dve.tensor_reduce(TILE_MAG[:, 0, t:t + 1], XN[:, t, :], AX.X, ALU.max,
                                  apply_absolute_value=True).then_inc(s2_tmag, 1)

        def s1_pe(pe):
            pe.wait_ge(w_in[1], 7 * 16)
            for e in range(DT):
                for n in range(3):
                    g = 3 * e + n
                    if g >= 8:
                        pe.wait_ge((s1_state, s1_y, s1_gate)[(g - 8) % 3], (g - 8) // 3 + 1)
                    for c in range(DT):
                        if g == 0:
                            pe.wait_ge(xt_ready, DT + c + 1)
                        ins = pe.matmul(PS[:, g % 8, :], RW[:, n, c, e * P:(e + 1) * P], XT[:, c, :],
                                        start=(c == 0), stop=(c == DT - 1))
                    ins.then_inc(s1_proj, 1)
            pe.wait_ge(s1_y, DT)
            pe.wait_ge(s1_gate, DT)
            for e in range(DT):
                ins = pe.matmul(PS[:, 4, :], MEANW[:, :], Y[:, e, :], start=(e == 0), stop=(e == DT - 1))
            ins.then_inc(pe_marks, 1)
            for e in range(DT):
                pe.wait_ge(s1_sq, e + 1)
                ins = pe.matmul(PS[:, 5, :], MEANW[:, :], SQ[:, e, :], start=(e == 0), stop=(e == DT - 1))
            ins.then_inc(pe_marks, 1)
            pe.wait_ge(s1_mod, DT)
            for t in range(NT):
                for e in range(DT):
                    ins = pe.matmul(PS[:, 4 + t, :], Y[:, e, t * P:(t + 1) * P], RW[:, 3, e, :],
                                    start=(e == 0), stop=(e == DT - 1))
                ins.then_inc(out_psum, 1)

        UP = view(0, [F0T, N])
        GT = view(24 * K, [F0T, N])
        SG = view(48 * K, [F0T, N])
        PIECE = FF0
        PIECES = 3 * F0T * D // PIECE
        FRAW = view(76 * K, [4, PIECE])
        NBLK = PIECE // QB
        BSC = view(100 * K, [PIECES, NBLK])
        BRC = view(102 * K + 512, [PIECES, NBLK])
        SPLIT = 8
        FW_HI = view(106 * K, [SPLIT, PIECE], F16)
        FW_LO = view(130 * K, [SPLIT, PIECE], F16)
        FWP = view(154 * K, [PIECES - SPLIT, PIECE])
        GU_HI = view(106 * K, [2, DT, FF0], F16)
        GU_LO = view(130 * K, [2, DT, FF0], F16)
        DNW = view(154 * K, [F0T, D])
        TILE_MAG = SM[:, 40:64].rearrange("p (a b) -> p a b", a=2)
        SLICES = 3
        PER = F0T // SLICES
        AM = COLS[:, 8:13]
        AR = COLS[:, 16:21]
        SC = COLS[:, 24:29]
        RC = COLS[:, 32:37]

        s2_raw = [sem(f"s2_raw{i}") for i in range(4)]
        s2_brc = sem("s2_brc")
        s2_scaled = sem("s2_scaled")
        s2_rounded = sem("s2_rounded")
        s2_w = sem("s2_w")
        s2_w_hi = sem("s2_w_hi")
        s2_w_lo = sem("s2_w_lo")
        s2_scale = sem("s2_scale")
        s2_mag = sem("s2_mag")
        s2_tmag = sem("s2_tmag")
        s2_all = sem("s2_all")
        s2_up_psum = sem("s2_up_psum")
        s2_up = sem("s2_up")
        s2_gt_psum = sem("s2_gt_psum")
        s2_gt = sem("s2_gt")
        s2_gt_r = sem("s2_gt_r")
        s2_gt_q = sem("s2_gt_q")
        s2_up_q = sem("s2_up_q")
        s2_sg_r = sem("s2_sg_r")
        s2_p_r = sem("s2_p_r")
        s2_h_r = sem("s2_h_r")
        s2_hid = sem("s2_hid")

        def s2_loads(sp):
            for p in range(PIECES):
                if p >= 4:
                    sp.wait_ge(s2_w, p - 3)
                sp.dma_start(FRAW[:, p % 4, :], a["ffnB"][p]).then_inc(s2_raw[p % 4], 16)

        def requantise(dve, link, p):
            if p < PIECES:
                dve.wait_ge(s2_raw[p % 4], 16 * (p // 4 + 1))
                w = FRAW[:, p % 4, :].rearrange("p (k s) -> p k s", s=QB)
                link(dve.tensor_reduce(BSC[:, p, :], w, AX.X, ALU.max, apply_absolute_value=True))
                link(dve.tensor_scalar(BSC[:, p, :], BSC[:, p, :], 1.0 / 7.0, 1e-12, ALU.mult, ALU.max))
                dve.reciprocal(BRC[:, p, :], BSC[:, p, :]).then_inc(s2_brc, 1)
                if p < SPLIT:
                    dve.wait_ge(s2_brc, p + 1)
                    link(dve.tensor_scalar(BSC[:, p, :], BSC[:, p, :], W_UP, None, ALU.mult))
            if p >= 2:
                p -= 2
                w = FRAW[:, p % 4, :].rearrange("p (k s) -> p k s", s=QB)
                dve.wait_ge(s2_rounded, p + 1)
                link(dve.scalar_tensor_tensor(out=w, in0=w, scalar=ROUND,
                                              in1=BSC[:, p, :].unsqueeze(2).to_broadcast([P, NBLK, QB]),
                                              op0=ALU.subtract, op1=ALU.mult))
                if p >= 2:
                    dve.wait_ge(s2_w_lo, min(p - 1, SPLIT))
                dve.transpose(FWP[:, p % 2 if p < SPLIT else p - SPLIT, :], FRAW[:, p % 4, :]).then_inc(s2_w, 1)

        def piece_low(pool, p):
            pool.wait_ge(s2_w_hi, p + 1)
            pool.tensor_tensor(FW_LO[:, p, :], FWP[:, p % 2, :], FW_HI[:, p, :], ALU.subtract).then_inc(s2_w_lo, 1)

        def scale_pieces(pool, start, end):
            for p in range(start, end):
                w = FRAW[:, p % 4, :].rearrange("p (k s) -> p k s", s=QB)
                pool.wait_ge(s2_brc, p + 1)
                pool.tensor_tensor(w, w, BRC[:, p, :].unsqueeze(2).to_broadcast([P, NBLK, QB]),
                                   ALU.mult).then_inc(s2_scaled, 1)
                if 3 <= p < SPLIT + 3:
                    piece_low(pool, p - 3)

        def add_round(act, p):
            act.wait_ge(s2_scaled, p + 1)
            act.activation(FRAW[:, p % 4, :], FRAW[:, p % 4, :], ACT.Copy, bias=ROUND).then_inc(s2_rounded, 1)
            if 2 <= p < SPLIT + 2:
                act.wait_ge(s2_w, p - 1)
                act.activation(FW_HI[:, p - 2, :], FWP[:, p % 2, :], ACT.Copy).then_inc(s2_w_hi, 1)

        def tiles(v, k):
            return v[:, k * PER:(k + 1) * PER, :]

        def s2_pool(pool, link):
            for n in range(4):
                if n == 1:
                    scale_pieces(pool, 9, PIECES)
                pool.wait_ge(s2_mag, n + 1)
                pool.partition_all_reduce(AR[:, n:n + 1], AM[:, n:n + 1], P, RMAX).then_inc(s2_all, 1)
            pool.wait_ge(s2_scale, 4)
            for k in range(SLICES):
                link(pool.tensor_scalar(tiles(UP, k), tiles(UP, k), RC[:, 3:4], ROUND, ALU.mult, ALU.add))
                pool.tensor_scalar(tiles(UP, k), tiles(UP, k), -ROUND, SC[:, 3:4], ALU.add, ALU.mult).then_inc(s2_up_q, 1)
            pool.wait_ge(s2_mag, 5)
            pool.partition_all_reduce(AR[:, 4:5], AM[:, 4:5], P, RMAX).then_inc(s2_all, 1)

        def take_up(act, start, end):
            for g in range(start, end):
                act.wait_ge(s2_up_psum, g + 1)
                act.activation(UP[:, g, :], PS[:, (F0T + g) % 8, :], ACT.Copy, scale=1.0 / W_UP).then_inc(s2_up, 1)

        def s2_act(act, link):
            split_x_act(act, 2)
            for g in range(F0T):
                act.wait_ge(s2_gt_psum, g + 1)
                act.activation(GT[:, g, :], PS[:, g % 8, :], ACT.Copy, scale=1.0 / W_UP).then_inc(s2_gt, 1)
                if g % 2 == 0 and g < 8:
                    add_round(act, 8 + g // 2)
            act.wait_ge(s2_scale, 2)
            for k in range(SLICES):
                act.activation(tiles(GT, k), tiles(GT, k), ACT.Copy, scale=RC[:, 1:2], bias=ROUND).then_inc(s2_gt_r, 1)
            take_up(act, 0, 3)
            for k in range(SLICES):
                act.wait_ge(s2_gt_q, k + 1)
                link.note(act.activation(tiles(SG, k), tiles(GT, k), ACT.Sigmoid))
                take_up(act, 3 + k, 4 + k)
            link.wait()
            for k in range(SLICES):
                act.activation(tiles(SG, k), tiles(SG, k), ACT.Copy, scale=65536.0, bias=ROUND).then_inc(s2_sg_r, 1)
                take_up(act, 6 + k, 7 + k)
            take_up(act, 9, F0T)
            act.wait_ge(s2_scale, 3)
            for k in range(SLICES):
                act.activation(tiles(GT, k), tiles(GT, k), ACT.Copy, scale=RC[:, 2:3], bias=ROUND).then_inc(s2_p_r, 1)
            act.wait_ge(s2_scale, 5)
            for k in range(SLICES):
                act.activation(tiles(GT, k), tiles(GT, k), ACT.Copy, scale=RC[:, 4:5], bias=ROUND).then_inc(s2_h_r, 1)
            norm_act(act, 3)

        def s2_dve(dve, link):
            def scale_of(n, last=None):
                dve.wait_ge(s2_all, n + 1)
                if last is not None:
                    link(dve.tensor_scalar(AR[:, n:n + 1], AR[:, n:n + 1], SC[:, last:last + 1], None, ALU.mult))
                link(dve.tensor_scalar(SC[:, n:n + 1], AR[:, n:n + 1], 1.0 / 32767.0, 1e-12, ALU.mult, ALU.max))
                if last is None:
                    dve.reciprocal(RC[:, n:n + 1], SC[:, n:n + 1]).then_inc(s2_scale, 1)
                else:
                    link(dve.reciprocal(RC[:, n:n + 1], SC[:, n:n + 1]))
                    dve.tensor_scalar(RC[:, n:n + 1], RC[:, n:n + 1], SC[:, last:last + 1], None,
                                      ALU.mult).then_inc(s2_scale, 1)
                dve.wait_ge(s2_scale, n + 1)

            dve.wait_ge(s2_tmag, NT)
            dve.tensor_reduce(AM[:, 0:1], TILE_MAG[:, 0, 0:NT], AX.X, ALU.max).then_inc(s2_mag, 1)
            scale_of(0)
            link(dve.tensor_scalar(XN[:, :, :], XN[:, :, :], RC[:, 0:1], ROUND, ALU.mult, ALU.add))
            for t in range(NT):
                dve.tensor_scalar(XN[:, t, :], XN[:, t, :], ROUND, SC[:, 0:1], ALU.subtract, ALU.mult).then_inc(ln_xn, 1)

            split_x_dve(dve, 0)

            def tile_magnitude(n, v, g, copied):
                dve.wait_ge(copied, g + 1)
                dve.tensor_reduce(TILE_MAG[:, n, g:g + 1], v[:, g, :], AX.X, ALU.max,
                                  apply_absolute_value=True).then_inc(s2_tmag, 1)

            for g in range(F0T):
                tile_magnitude(0, GT, g, s2_gt)
                if g % 2 and g < 8:
                    requantise(dve, link, 10 + g // 2)
            dve.wait_ge(s2_tmag, NT + F0T)
            dve.tensor_reduce(AM[:, 1:2], TILE_MAG[:, 0, :], AX.X, ALU.max).then_inc(s2_mag, 1)
            scale_of(1)
            for k in range(SLICES):
                dve.wait_ge(s2_gt_r, k + 1)
                dve.tensor_scalar(tiles(GT, k), tiles(GT, k), ROUND, SC[:, 1:2], ALU.subtract,
                                  ALU.mult).then_inc(s2_gt_q, 1)
            for g in range(4):
                tile_magnitude(1, UP, g, s2_up)
            for k in range(SLICES):
                dve.wait_ge(s2_sg_r, k + 1)
                link(dve.tensor_scalar(tiles(SG, k), tiles(SG, k), ROUND, 65535.0, ALU.subtract, ALU.min))
                link(dve.scalar_tensor_tensor(out=tiles(GT, k), in0=tiles(SG, k), scalar=1.0 / 65536.0, in1=tiles(GT, k),
                                              op0=ALU.mult, op1=ALU.mult))
                dve.tensor_reduce(TILE_MAG[:, 0, k:k + 1], tiles(GT, k), AX.XY, ALU.max,
                                  apply_absolute_value=True).then_inc(s2_tmag, 1)
                if k < 2:
                    for g in range(4 + 2 * k, 6 + 2 * k):
                        tile_magnitude(1, UP, g, s2_up)
            dve.wait_ge(s2_tmag, NT + F0T + 8 + SLICES)
            dve.tensor_reduce(AM[:, 2:3], TILE_MAG[:, 0, 0:SLICES], AX.X, ALU.max).then_inc(s2_mag, 1)
            scale_of(2)
            for g in range(8, F0T):
                tile_magnitude(1, UP, g, s2_up)
            dve.wait_ge(s2_tmag, NT + 2 * F0T + SLICES)
            dve.tensor_reduce(AM[:, 3:4], TILE_MAG[:, 1, :], AX.X, ALU.max).then_inc(s2_mag, 1)
            scale_of(3)
            for k in range(SLICES):
                dve.wait_ge(s2_p_r, k + 1)
                dve.wait_ge(s2_up_q, k + 1)
                link(dve.scalar_tensor_tensor(out=tiles(GT, k), in0=tiles(GT, k), scalar=ROUND, in1=tiles(UP, k),
                                              op0=ALU.subtract, op1=ALU.mult))
                dve.tensor_reduce(TILE_MAG[:, 1, k:k + 1], tiles(GT, k), AX.XY, ALU.max,
                                  apply_absolute_value=True).then_inc(s2_tmag, 1)
            dve.wait_ge(s2_tmag, NT + 2 * F0T + 2 * SLICES)
            dve.tensor_reduce(AM[:, 4:5], TILE_MAG[:, 1, 0:SLICES], AX.X, ALU.max).then_inc(s2_mag, 1)
            scale_of(4, last=2)
            for k in range(SLICES):
                dve.wait_ge(s2_h_r, k + 1)
                dve.tensor_scalar(tiles(GT, k), tiles(GT, k), ROUND, SC[:, 4:5], ALU.subtract,
                                  ALU.mult).then_inc(s2_hid, 1)
            for t in range(NT):
                add_tile(dve, 2, t)
                norm_tile(dve, 3, t).then_inc(ln_xn, 1)

        def s2_pe(pe):
            for t in range(NT):
                turn_tile(pe, 2, t)
            for n, psum in enumerate((s2_gt_psum, s2_up_psum)):
                pe.wait_ge(s2_w_lo, 4 * n + 4)
                for g in range(F0T):
                    at = n * F0T + g
                    if at >= 8:
                        if at - 8 < F0T:
                            pe.wait_ge(s2_gt, at - 7)
                        else:
                            pe.wait_ge(s2_up, at - 7 - F0T)
                    for c in range(DT):
                        if at == 0:
                            pe.wait_ge(xt_ready, DT * 2 + c + 1)
                        cols = slice(g * P, (g + 1) * P)
                        ins = matmul_split(pe, PS[:, at % 8, :], (GU_HI[:, n, c, cols], GU_LO[:, n, c, cols]),
                                           (XT_HI[:, c, :], XT_LO[:, c, :]), c, DT)
                    ins.then_inc(psum, 1)
            pe.wait_ge(s2_w, PIECES)
            for g in range(F0T):
                pe.wait_ge(s2_hid, g // PER + 1)
                for t in range(NT):
                    ins = pe.matmul(PS[:, 4 + t, :], GT[:, g, t * P:(t + 1) * P], DNW[:, g, :],
                                    start=(g == 0), stop=(g == F0T - 1))
                    if g == F0T - 1:
                        ins.then_inc(out_psum, 1)
            for t in range(NT):
                turn_tile(pe, 3, t)

        W12B = view(53 * K, [8, 2048], BF16)
        WQ1 = view(86 * K, [DT, D])
        WK1 = view(94 * K, [DT, P])
        WV1 = view(96 * K, [DT, P])
        WC1 = view(98 * K, [DT, D])
        CR3 = view(106 * K, [2, CH, 512])
        CHI3 = view(122 * K, [2, CH, 512], F16)
        CLO3 = view(130 * K, [2, CH, 512], F16)
        QHI3 = view(138 * K, [DT, N], F16)
        QLO3 = view(142 * K, [DT, N], F16)
        QS = view(146 * K, [DT, N])
        TRAW = view(154 * K, [2048])
        TMID = view(162 * K, [2048])
        TOP8 = view(170 * K, [2, NT, 8])
        IDX8 = view(171 * K, [2, NT, 8], U32)
        TOPV = view(172 * K, [NCH, NT])
        TOPI = view(172 * K + 512, [NCH, NT])
        FROM_END = view(173 * K, [NCH, NT], I32)
        FROM_ENDF = view(173 * K + 512, [NCH, NT])
        BEST = view(174 * K, [NT])
        MEMIDX = view(174 * K + 64, [NT], U32)
        NMAX = view(174 * K + 512, [NT * ATT_H])
        RS3 = view(175 * K, [NT * ATT_H])
        MEM = view(106 * K, [NT, D])
        MEMT = view(114 * K, [DT, N])
        MKT = view(122 * K, [N])
        MVAL = view(124 * K, [NT, DH])
        PB = view(126 * K, [6, N])
        ATTT = view(138 * K, [DT, N])
        PTB = view(154 * K, [2, NT, N])
        WINH = view(0, [4 * DT, QP], F16)
        WINL = view(18 * K + 512, [4 * DT, QP], F16)
        WINRAW = [XN[:, 2 * b:2 * b + 2, :].rearrange("p a b -> p (a b)")[:, 0:QP] for b in range(2)]
        UNITS = NT * ATT_H
        LAG = 4

        s3_clip = sem("s3_clip")
        s3_whole = sem("s3_whole")
        s3_tern = sem("s3_tern")
        s3_win = [sem("s3_win0"), sem("s3_win1")]
        s3_win_up = sem("s3_win_up")
        s3_win_hi = sem("s3_win_hi")
        s3_win_lo = sem("s3_win_lo")
        s3_piece = sem("s3_piece")
        s3_q_psum = sem("s3_q_psum")
        s3_q_hi = sem("s3_q_hi")
        s3_q_lo = sem("s3_q_lo")
        s3_qs = sem("s3_qs")
        s3_chunk = [sem("s3_chunk0"), sem("s3_chunk1")]
        s3_hi = sem("s3_hi")
        s3_lo = sem("s3_lo")
        s3_scores = sem("s3_scores")
        s3_max = sem("s3_max")
        s3_idx = sem("s3_idx")
        s3_mem = sem("s3_mem")
        s3_memt_psum = sem("s3_memt_psum")
        s3_memt = sem("s3_memt")
        s3_kv_psum = sem("s3_kv_psum")
        s3_kv = sem("s3_kv")
        s3_logits = sem("s3_logits")
        s3_nmax = sem("s3_nmax")
        s3_p = sem("s3_p")
        s3_pt_psum = sem("s3_pt_psum")
        s3_pt = [sem("s3_pt_even"), sem("s3_pt_odd")]
        s3_pv = sem("s3_pv")
        s3_rs = sem("s3_rs")
        s3_pn = sem("s3_pn")
        s3_attt = sem("s3_attt")

        def s3_sp(sp):
            sp.wait_ge(s2_w, PIECES)
            sp.dma_start(WQ1, a["Wq1T"].rearrange("(t p) c -> p t c", p=P)).then_inc(w_in[3], 16)
            sp.dma_start(WK1, a["Wk1T"].rearrange("(t p) c -> p t c", p=P)).then_inc(w_in[3], 16)
            sp.dma_start(WV1, a["Wv1T"].rearrange("(t p) c -> p t c", p=P)).then_inc(w_in[3], 16)
            sp.dma_start(WC1, a["Wc1T"].rearrange("(t p) c -> p t c", p=P)).then_inc(w_in[3], 16)
            sp.wait_ge(pool_marks, POOL_MARK["s3_primed"])
            sp.wait_ge(s2_up_psum, F0T)
            with sp.Fori(0, PAIRS) as i:
                for b in range(2):
                    sp.wait_ge(s3_hi, i * 2 + b + 1)
                    sp.wait_ge(s3_lo, i * 2 + b + 1)
                    sp.dma_start(CR3[:, b], a["ctxT"][i * 2 + b]).then_inc(s3_chunk[b], 16)
                sp.wait_ge(xt_psum, DT * 4)
                for b in range(2):
                    sp.wait_ge(s3_win_lo, i * 2 + b + 1)
                    sp.dma_start(WINRAW[b], a["WinT"][i * 2 + b]).then_inc(s3_win[b], 16)
                sp.wait_ge(s3_clip, i + 1)
                sp.dma_start(TRAW, a["w12"][i]).then_inc(s3_piece, 16)
            s4_loads(sp)

        def s3_pool(pool, link):
            pool.sem_inc(s3_hi, AHEAD_SPLIT)
            pool.sem_inc(s3_lo, AHEAD_SPLIT)
            pool.sem_inc(s3_clip, 1)
            pool.sem_inc(s3_win_lo, 2)
            pool.sem_inc(s3_scores, AHEAD_TILES)
            pool.sem_inc(s3_idx, AHEAD_BANK)
            pool.sem_inc(pool_marks, 1)
            pool.wait_ge(s2_up_psum, F0T)
            with pool.Fori(0, PAIRS) as i:
                for b in range(2):
                    c = i * 2 + b
                    pool.wait_ge(s3_chunk[b], i * 16 + 16)
                    pool.wait_ge(s3_scores, c * CH + 1)
                    settle(pool)
                    pool.tensor_scalar(CHI3[:, b], CR3[:, b], 1.0, 0.0, ALU.mult, ALU.add).then_inc(s3_hi, 1)
                    pool.wait_ge(s3_hi, c + 1 + AHEAD_SPLIT)
                    pool.tensor_tensor(CLO3[:, b], CR3[:, b], CHI3[:, b], ALU.subtract).then_inc(s3_lo, 1)
                    pool.wait_ge(s3_win_hi, c + 1)
                    pool.tensor_tensor(WINL[:, c, :], WINRAW[b], WINH[:, c, :], ALU.subtract).then_inc(s3_win_lo, 1)
            pool.wait_ge(x_done, NT * 3)
            pool.iota(FROM_END, pattern=[[-CH * P, NCH], [0, NT]], base=M, channel_multiplier=0).then_inc(pool_marks, 1)
            pool.wait_ge(dve_marks, DVE_MARK["s3_memidx"])
            for t in range(NT):
                pool.indirect_dma_start(out=MEM[:, t, :], out_offset=None, in_=a["ctx"],
                                        in_offset=bass.IndirectOffsetOnAxis(ap=MEMIDX[:, t:t + 1], axis=0)
                                        ).then_inc(s3_mem, 16)
            for u in range(UNITS):
                pool.wait_ge(s3_rs, u + 1)
                pool.tensor_scalar(PB[:, u % 6, :], PB[:, u % 6, :], RS3[:, u:u + 1], 1.0,
                                   ALU.mult, ALU.mult).then_inc(s3_pn, 1)

        def s3_act(act, link):
            transpose_x_act(act, 3)
            for e in range(DT):
                act.wait_ge(s3_q_psum, e + 1)
                act.copy(QHI3[:, e, :], PS[:, 4 + e, :]).then_inc(s3_q_hi, 1)
                act.wait_ge(s3_q_lo, e + 1)
                act.activation(QS[:, e, :], PS[:, 4 + e, :], ACT.Copy, scale=float(DH) ** -0.5).then_inc(s3_qs, 1)
            with act.Fori(0, PAIRS) as i:
                for b in range(2):
                    c = i * 2 + b
                    act.wait_ge(s3_win[b], i * 16 + 16)
                    act.activation(WINRAW[b], WINRAW[b], ACT.Copy, scale=W_UP).then_inc(s3_win_up, 1)
                    act.wait_ge(s3_win_up, c + 1)
                    act.activation(WINH[:, c, :], WINRAW[b], ACT.Copy).then_inc(s3_win_hi, 1)
            for c in range(DT):
                act.wait_ge(s3_memt_psum, c + 1)
                act.copy(MEMT[:, c, :], PS[:, c, :]).then_inc(s3_memt, 1)

            def turn(u):
                h, t = u // NT, u % NT
                act.wait_ge(s3_pt_psum, u + 1)
                if h >= 2:
                    act.wait_ge(s3_pv, h - 1)
                act.copy(PTB[:, h % 2, :, t * P:(t + 1) * P],
                         PS[:, 4 + u % 2, :].rearrange("p (m l) -> p m l", m=NT)).then_inc(s3_pt[1], 1)

            for u in range(UNITS + LAG):
                if u < UNITS:
                    act.wait_ge(s3_nmax, u + 1)
                    if u >= 6:
                        act.wait_ge(s3_pt_psum, u - 5)
                    act.activation(PB[:, u % 6, :], PS[:, u % 4, :], ACT.Exp, bias=NMAX[:, u:u + 1],
                                   accum_out=RS3[:, u:u + 1]).then_inc(s3_p, 1)
                if u >= LAG and (u - LAG) % 2:
                    turn(u - LAG)
                if u >= LAG + 3 and (u - LAG - 3) % 16 == 15:
                    g = (u - LAG - 3) // 16
                    act.wait_ge(s3_pv, 4 * (g + 1))
                    act.copy(ATTT[:, g, :], PS[:, 6 + g % 2, :]).then_inc(s3_attt, 1)
            act.wait_ge(s3_pv, ATT_H)
            act.copy(ATTT[:, DT - 1, :], PS[:, 6 + (DT - 1) % 2, :]).then_inc(s3_attt, 1)
            norm_act(act, 4)

        def s3_dve(dve, link):
            for e in range(DT):
                dve.wait_ge(s3_q_hi, e + 1)
                dve.tensor_tensor(QLO3[:, e, :], PS[:, 4 + e, :], QHI3[:, e, :], ALU.subtract).then_inc(s3_q_lo, 1)
            with dve.Fori(0, PAIRS) as i:
                for b in range(2):
                    c = i * 2 + b
                    for t in range(NT):
                        dve.wait_ge(s3_scores, c * CH + t + 1 + AHEAD_TILES)
                        settle(dve)
                        dve.max(TOP8[:, b, t, :], PS[:, b * CH + t, :]).then_inc(s3_max, 1)
                    for t in range(NT):
                        dve.wait_ge(s3_max, c * CH + t + 1)
                        settle(dve)
                        dve.max_index(IDX8[:, b, t, :], TOP8[:, b, t, :], PS[:, b * CH + t, :]).then_inc(s3_idx, 1)
                    dve.tensor_copy(TOPV[:, c, :], TOP8[:, b, :, 0])
                    dve.wait_ge(s3_idx, c * CH + CH + AHEAD_BANK)
                    dve.tensor_copy(TOPI[:, c, :], IDX8[:, b, :, 0])
                dve.wait_ge(s3_piece, i * 16 + 16)
                dve.tensor_scalar(TMID, TRAW, W_RECIP[:, bass.ds(i, 1)], 1.0, ALU.mult, ALU.min).then_inc(s3_clip, 1)
                dve.wait_ge(s3_clip, i + 2)
                dve.tensor_scalar(TMID, TMID, -1.0, ROUND, ALU.max, ALU.add).then_inc(s3_whole, 1)
                dve.wait_ge(s3_whole, i + 1)
                dve.tensor_scalar(W12B[:, i, :], TMID, ROUND, None, ALU.subtract).then_inc(s3_tern, 1)
            dve.wait_ge(pool_marks, POOL_MARK["s3_iota"])
            link(dve.tensor_copy(FROM_ENDF, FROM_END))
            link(dve.tensor_reduce(BEST, TOPV.rearrange("p c t -> p t c"), AX.X, ALU.max))
            link(dve.tensor_tensor(TOPI, FROM_ENDF, TOPI, ALU.subtract))
            link(dve.tensor_tensor(TOPV, TOPV, BEST.unsqueeze(1).to_broadcast([P, NCH, NT]), ALU.is_equal))
            link(dve.tensor_tensor(TOPI, TOPI, TOPV, ALU.mult))
            link(dve.tensor_reduce(BEST, TOPI.rearrange("p c t -> p t c"), AX.X, ALU.max))
            dve.tensor_scalar(MEMIDX, BEST, -1.0, float(M), ALU.mult, ALU.add).then_inc(dve_marks, 1)
            dve.wait_ge(s3_kv_psum, 2)
            dve.tensor_copy(MKT, PS[:, 4, :]).then_inc(s3_kv, 1)
            dve.tensor_copy(MVAL, PS[:, 5, :].rearrange("p (a b) -> p a b", a=NT)[:, :, 0:DH]).then_inc(s3_kv, 1)

            def turn(u):
                h, t = u // NT, u % NT
                dve.wait_ge(s3_pt_psum, u + 1)
                if h >= 2:
                    dve.wait_ge(s3_pv, h - 1)
                dve.tensor_copy(PTB[:, h % 2, :, t * P:(t + 1) * P],
                                PS[:, 4 + u % 2, :].rearrange("p (m l) -> p m l", m=NT)).then_inc(s3_pt[0], 1)

            for u in range(UNITS + LAG):
                if u < UNITS:
                    dve.wait_ge(s3_logits, u + 1)
                    dve.tensor_reduce(NMAX[:, u:u + 1], PS[:, u % 4, :], AX.X, ALU.max,
                                      negate=True).then_inc(s3_nmax, 1)
                if 1 <= u <= UNITS:
                    dve.wait_ge(s3_p, u)
                    dve.reciprocal(RS3[:, u - 1:u], RS3[:, u - 1:u]).then_inc(s3_rs, 1)
                if u >= LAG and (u - LAG) % 2 == 0:
                    turn(u - LAG)
            for t in range(NT):
                add_tile(dve, 3, t)
                norm_tile(dve, 4, t).then_inc(ln_xn, 1)

        def s3_pe(pe):
            pe.wait_ge(w_in[3], 64)
            for e in range(DT):
                for c in range(DT):
                    if e == 0:
                        pe.wait_ge(xt_ready, DT * 3 + c + 1)
                    ins = pe.matmul(PS[:, 4 + e, :], WQ1[:, c, e * P:(e + 1) * P], XT[:, c, :],
                                    start=(c == 0), stop=(c == DT - 1))
                ins.then_inc(s3_q_psum, 1)
            pe.wait_ge(s3_q_lo, DT)
            pe.wait_ge(s3_qs, DT)
            with pe.Fori(0, PAIRS) as i:
                for b in range(2):
                    c = i * 2 + b
                    pe.wait_ge(s3_hi, c + 1 + AHEAD_SPLIT)
                    pe.wait_ge(s3_lo, c + 1 + AHEAD_SPLIT)
                    for t in range(NT):
                        pe.wait_ge(s3_idx, c * CH + t + 1)
                        bank = PS[:, b * CH + t, :]
                        cols = slice(t * P, (t + 1) * P)
                        for e in range(DT):
                            pe.matmul(bank, QHI3[:, e, cols], CHI3[:, b, e, :], start=(e == 0), stop=False)
                            pe.matmul(bank, QHI3[:, e, cols], CLO3[:, b, e, :], start=False, stop=False)
                            ins = pe.matmul(bank, QLO3[:, e, cols], CHI3[:, b, e, :], start=False,
                                            stop=(e == DT - 1))
                        ins.then_inc(s3_scores, 1)
            pe.wait_ge(s3_idx, MT + AHEAD_BANK)
            keep_warm(pe, 7, 6)
            pe.wait_ge(s3_mem, 16 * NT)
            for c in range(DT):
                for t in range(NT):
                    ins = pe.transpose(PS[:, c, t * P:(t + 1) * P], MEM[:, t, c * P:(c + 1) * P], IDENT[:, :])
                ins.then_inc(s3_memt_psum, 1)
            pe.wait_ge(s3_memt, DT)
            for c in range(DT):
                ins = pe.matmul(PS[:, 4, :], WK1[:, c, :], MEMT[:, c, :], start=(c == 0), stop=(c == DT - 1))
            ins.then_inc(s3_kv_psum, 1)
            for t in range(NT):
                for c in range(DT):
                    ins = pe.matmul(PS[:, 5, t * P:(t + 1) * P], MEMT[:, c, t * P:(t + 1) * P], WV1[:, c, :],
                                    start=(c == 0), stop=(c == DT - 1))
            ins.then_inc(s3_kv_psum, 1)
            pe.wait_ge(s3_kv, 2)

            def logits(u):
                h, t = u // NT, u % NT
                rows = slice(DH * (h % 4), DH * (h % 4) + DH)
                if u >= 4:
                    pe.wait_ge(s3_p, u - 3)
                pe.matmul(PS[:, u % 4, :], QS[rows, h // 4, t * P:(t + 1) * P], MKT[rows, :],
                          start=True, stop=True).then_inc(s3_logits, 1)

            def turn(u):
                pe.wait_ge(s3_pn, u + 1)
                if u >= 2:
                    pe.wait_ge(s3_pt[u % 2], u // 2)
                for m in range(NT):
                    ins = pe.transpose(PS[:, 4 + u % 2, m * P:(m + 1) * P], PB[:, u % 6, m * P:(m + 1) * P],
                                       IDENT[:, :])
                ins.then_inc(s3_pt_psum, 1)

            def weigh(h):
                pe.wait_ge(s3_pt[0], 2 * h + 2)
                pe.wait_ge(s3_pt[1], 2 * h + 2)
                if h >= 8:
                    pe.wait_ge(s3_attt, h // 4 - 1)
                for m in range(NT):
                    ins = pe.matmul(PS[DH * (h % 4):DH * (h % 4) + DH, 6 + (h // 4) % 2, :], MVAL[:, m, :],
                                    PTB[:, h % 2, m, :], start=(m == 0), stop=(m == NT - 1))
                ins.then_inc(s3_pv, 1)

            for u in range(UNITS + LAG + 2):
                if u < UNITS:
                    logits(u)
                if LAG <= u < UNITS + LAG:
                    turn(u - LAG)
                if u >= LAG + 2 and (u - LAG - 2) % NT == NT - 1:
                    weigh((u - LAG - 2) // NT)
            pe.wait_ge(s3_attt, DT)
            for t in range(NT):
                for c in range(DT):
                    ins = pe.matmul(PS[:, 4 + t, :], ATTT[:, c, t * P:(t + 1) * P], WC1[:, c, :],
                                    start=(c == 0), stop=(c == DT - 1))
                ins.then_inc(out_psum, 1)
                if t:
                    turn_tile(pe, 4, t - 1)
            turn_tile(pe, 4, NT - 1)

        WIN_HI = view(0, [DT, PROJ], F16)
        WIN_LO = view(18 * K + 512, [DT, PROJ], F16)
        WOUT = view(37 * K, [IT, D])
        XBC = view(85 * K, [CVT, N + 3])
        CV = view(106 * K, [CVT, N])
        ZG = view(127 * K, [NT, SSM_I])
        YS = view(143 * K, [NT, SSM_I])
        DTX = view(85 * K, [SSM_I + SSM_P])
        WDTX = view(90 * K, [SSM_I])
        DECAY = view(94 * K, [SSM_H, P])
        BNAT = view(163 * K, [P])
        HS = view(102 * K, [SSM_I])
        TMP = view(159 * K, [SSM_I])
        YT_HI = view(106 * K, [IT, N], F16)
        YT_LO = view(114 * K, [IT, N], F16)
        WOUT_HI = view(0, [IT, D], F16)
        WOUT_LO = view(8 * K, [IT, D], F16)
        SMALL = 164 * K
        CONVW = view(SMALL, [CVT, 4])
        CONVB = view(SMALL + 256, [CVT])
        DTB = view(SMALL + 512, [SSM_H])
        ALOG = view(SMALL + 768, [SSM_H])
        SSMD = view(SMALL + 1024, [SSM_H])
        NORMW = view(SMALL + 1280, [IT])
        DTV = view(SMALL + 1536, [NT, SSM_H])
        DTA = view(SMALL + 1792, [NT, SSM_H])
        DTVA = view(SMALL + 1536, [2 * NT, SSM_H])
        SUMS = view(SMALL + 3584, [2, NT, SSM_H])
        DTE = view(SMALL + 2048, [NT, SSM_H])
        LA = view(SMALL + 4096, [3, NT, SSM_H])
        ELA = view(SMALL + 5120, [3, NT, SSM_H])
        NLA = view(SMALL + 2304, [NT, SSM_H])
        MS = view(SMALL + 3072, [NT])
        RMS = view(SMALL + 3328, [NT])

        s4_conv_psum = sem("s4_conv_psum")
        s4_conv_in = sem("s4_conv_in")
        s4_conv = sem("s4_conv")
        s4_cv = sem("s4_cv")
        s4_z_psum = sem("s4_z_psum")
        s4_z = sem("s4_z")
        s4_small = sem("s4_small")
        s4_read = sem("s4_read")
        s4_decay_psum = sem("s4_decay_psum")
        s4_decay = sem("s4_decay")
        s4_mix = sem("s4_mix")
        s4_dtx = sem("s4_dtx")
        s4_wdtx = sem("s4_wdtx")
        s4_intra = sem("s4_intra")
        s4_inter = sem("s4_inter")
        s4_taken = sem("s4_taken")
        s4_faded = sem("s4_faded")
        s4_y = sem("s4_y")
        s4_state = sem("s4_state")
        s4_hs = sem("s4_hs")
        s4_ys = sem("s4_ys")
        s4_yn = sem("s4_yn")
        s4_yt_psum = sem("s4_yt_psum")
        s4_yt = sem("s4_yt")

        def heads(v, n=SSM_H):
            return v.rearrange("p (h c) -> p h c", h=n)

        def s4_loads(sp):
            sp.dma_start(WOUT, a["WoutT"].rearrange("(t p) c -> p t c", p=P)).then_inc(w_in[4], 16)

        def s4_sp(sp):
            sp.wait_ge(x_done, NT * 4)
            for dst, name in ((CONVW, "convw"), (CONVB, "convb"), (NORMW, "normw")):
                sp.dma_start(dst, a[name]).then_inc(small_in, 16)
            for dst, name in ((DTB, "dtb"), (ALOG, "alog"), (SSMD, "ssmd")):
                sp.dma_start(dst, a[name].partition_broadcast(P)).then_inc(small_in, 16)

        def s4_pool(pool, link):
            pool.wait_ge(x_done, NT * 4)
            pool.memset(XBC[:, :, 0:3], 0.0).then_inc(pool_marks, 1)
            pool.wait_ge(act_marks, ACT_MARK["s4_ela"])
            for q in range(NT):
                if q < NT - 1:
                    pool.wait_ge(s4_dtx, q + 1)
                    if q:
                        pool.wait_ge(s4_state, q)
                    pool.tensor_tensor(heads(WDTX), heads(DTX[:, 0:SSM_I]),
                                       ELA[:, 1, q, :].unsqueeze(2).to_broadcast([P, SSM_H, SSM_P]),
                                       ALU.mult).then_inc(s4_wdtx, 1)
                    pool.wait_ge(s4_hs, q + 1)
                    if q:
                        pool.wait_ge(s4_inter, q)
                    pool.tensor_tensor(heads(HS), heads(HS),
                                       ELA[:, 2, q, :].unsqueeze(2).to_broadcast([P, SSM_H, SSM_P]),
                                       ALU.mult).then_inc(s4_faded, 1)
                if q == 0:
                    pool.wait_ge(w_in[4], 16)
                w = slice(2 * q, 2 * q + 2)
                link(pool.tensor_scalar(WOUT[:, w, :], WOUT[:, w, :], W_UP, 1.0, ALU.mult, ALU.mult))
                link(pool.tensor_scalar(WOUT_HI[:, w, :], WOUT[:, w, :], 1.0, 0.0, ALU.mult, ALU.add))
                link.note(pool.tensor_tensor(WOUT_LO[:, w, :], WOUT[:, w, :], WOUT_HI[:, w, :], ALU.subtract))
                if q == NT - 1:
                    link.wait()
                    pool.sem_inc(pool_marks, 1)
                if q < NT - 1:
                    pool.wait_ge(s4_y, q + 1)
                    pool.tensor_tensor(YS[:, q, :], YS[:, q, :], ZG[:, q, :], ALU.mult).then_inc(s4_ys, 1)

        def s4_act(act, link):
            split_x_act(act, 4)
            act.wait_ge(dve_marks, DVE_MARK["s4_dtb"])
            link(act.activation(DTE, DTV, ACT.Abs))
            link(act.activation(DTE, DTE, ACT.Exp, scale=-1.0))
            act.wait_ge(small_in, 8 * 16)
            link(act.activation(ALOG, ALOG, ACT.Exp))
            act.activation(DTE, DTE, ACT.Ln, bias=1.0).then_inc(act_marks, 1)
            for g in range(CVT + 2):
                if g < CVT:
                    act.wait_ge(s4_conv_psum, g + 1)
                    act.activation(XBC[:, g, 3:], PS[:, g % 4, :], ACT.Copy, scale=1.0 / W_UP).then_inc(s4_conv_in, 1)
                if g >= 2:
                    act.wait_ge(s4_conv, g - 1)
                    act.activation(CV[:, g - 2, :], CV[:, g - 2, :], ACT.Silu).then_inc(s4_cv, 1)
            for g in range(2 * NT):
                act.wait_ge(s4_z_psum, g + 1)
                act.activation(ZG[:, g // 2, (g % 2) * 512:(g % 2 + 1) * 512], PS[:, 4 + g % 2, :],
                               ACT.Silu, scale=1.0 / W_UP).then_inc(s4_z, 1)
            act.wait_ge(dve_marks, DVE_MARK["s4_la"])
            act.activation(ELA, LA, ACT.Exp).then_inc(act_marks, 1)
            for q in range(NT):
                if q:
                    act.wait_ge(s4_intra, q)
                for h in range(SSM_H):
                    act.wait_ge(s4_decay_psum, (SSM_H * q + h) // 4 + 1)
                    ins = act.activation(DECAY[:, h, :], PS[:, 4 + h // 4, (h % 4) * P:(h % 4 + 1) * P], ACT.Exp,
                                         bias=NLA[:, q, h:h + 1])
                    if h % 4 == 3:
                        ins.then_inc(s4_decay, 1)
            for q in range(NT):
                act.wait_ge(s4_ys, q + 1)
                link(act.activation(ZG[:, q, :], YS[:, q, :], ACT.Square, accum_out=MS[:, q:q + 1]))
            act.activation(RMS, MS, ACT.Sqrt, scale=1.0 / SSM_I, bias=EPSC[:, 0:1]).then_inc(act_marks, 1)
            for c in range(IT):
                act.wait_ge(s4_yt_psum, c + 1)
                if c == 0:
                    act.wait_ge(small_in, 8 * 16)
                act.activation(YT_HI[:, c, :], PS[:, c % 4, :], ACT.Copy, scale=NORMW[:, c:c + 1]).then_inc(xt_hi, 1)
            norm_act(act, 5)

        def s4_dve(dve, link):
            split_x_dve(dve, 1)
            dve.wait_ge(small_in, 8 * 16)
            dve.wait_ge(pe_marks, PE_MARK["s4_dt_psum"])
            dve.scalar_tensor_tensor(out=DTV, in0=PS[:, 6, :].rearrange("p (t c) -> p t c", t=NT)[:, :, P - SSM_H:],
                                     scalar=1.0 / W_UP, in1=DTB.unsqueeze(1).to_broadcast([P, NT, SSM_H]),
                                     op0=ALU.mult, op1=ALU.add).then_inc(dve_marks, 1)
            dve.wait_ge(act_marks, ACT_MARK["s4_softplus"])
            link(dve.scalar_tensor_tensor(out=DTV, in0=DTV, scalar=0.0, in1=DTE, op0=ALU.max, op1=ALU.add))
            link(dve.tensor_scalar(ALOG, ALOG, -1.0, None, ALU.mult))
            dve.tensor_tensor(DTA, DTV, ALOG.unsqueeze(1).to_broadcast([P, NT, SSM_H]), ALU.mult).then_inc(dve_marks, 1)
            dve.wait_ge(pool_marks, POOL_MARK["s4_pad"])
            for g in range(CVT):
                dve.wait_ge(s4_conv_in, g + 1)
                link(dve.tensor_scalar(CV[:, g, :], XBC[:, g, 0:N], CONVW[:, g, 0:1], CONVB[:, g:g + 1],
                                       ALU.mult, ALU.add))
                for k in range(1, 4):
                    ins = dve.scalar_tensor_tensor(out=CV[:, g, :], in0=XBC[:, g, k:k + N], scalar=CONVW[:, g, k:k + 1],
                                                   in1=CV[:, g, :], op0=ALU.mult, op1=ALU.add)
                    if k < 3:
                        link(ins)
                    else:
                        ins.then_inc(s4_conv, 1)
            dve.wait_ge(s4_conv, CVT)
            link(dve.memset(DTX[:, SSM_I:], 0.0))
            dve.memset(HS, 0.0).then_inc(s4_hs, 1)
            dve.wait_ge(pe_marks, PE_MARK["s4_sums"])
            for k in range(2):
                link(dve.tensor_copy(SUMS[:, k], PS[:, 6, k * P + P // 2:(k + 1) * P].rearrange("p (t h) -> p t h", t=NT)))
            dve.sem_inc(dve_marks, 1)
            link.note(dve.tensor_copy(LA[:, 0], SUMS[:, 0]))
            link.note(dve.tensor_copy(LA[:, 2], SUMS[:, 1]))
            link.note(dve.tensor_scalar(NLA, SUMS[:, 0], -1.0, None, ALU.mult))
            link(dve.tensor_tensor(LA[:, 1], SUMS[:, 1], SUMS[:, 0], ALU.subtract))
            dve.sem_inc(dve_marks, 1)
            dve.wait_ge(s4_z, 2 * NT)
            for q in range(NT):
                dve.wait_ge(s4_small, q + 1)
                xs = PS[:, 0:2, :].rearrange("p a (h c) -> p (a h) c", c=SSM_P)
                dve.tensor_tensor(heads(DTX[:, 0:SSM_I]), xs, DTV[:, q, :].unsqueeze(2).to_broadcast([P, SSM_H, SSM_P]),
                                  ALU.mult).then_inc(s4_dtx, 1)
                link.note(dve.tensor_copy(BNAT, PS[:, 2, 0:P]))
                dve.tensor_tensor(heads(YS[:, q, :]), xs, SSMD.unsqueeze(2).to_broadcast([P, SSM_H, SSM_P]),
                                  ALU.mult).then_inc(s4_read, 1)
                for g in range(4):
                    dve.wait_ge(s4_decay, 4 * q + g + 1)
                    dve.tensor_tensor(DECAY[:, 4 * g:4 * g + 4, :], DECAY[:, 4 * g:4 * g + 4, :],
                                      PS[:, 3, 0:P].unsqueeze(1).to_broadcast([P, 4, P]), ALU.mult).then_inc(s4_mix, 1)
                if q:
                    dve.wait_ge(s4_inter, q)
                    link.note(dve.tensor_tensor(heads(TMP), PS[:, 0:2, :].rearrange("p a (h c) -> p (a h) c", c=SSM_P),
                                                ELA[:, 0, q, :].unsqueeze(2).to_broadcast([P, SSM_H, SSM_P]), ALU.mult))
                dve.wait_ge(s4_read, q + 1)
                dve.wait_ge(s4_intra, q + 1)
                ins = dve.tensor_tensor(heads(YS[:, q, :]), PS[:, 4:8, :].rearrange("p a (h c) -> p (a h) c", c=P)[:, :, 0:SSM_P],
                                        heads(YS[:, q, :]), ALU.add)
                ins.then_inc(s4_taken, 1)
                if q < NT - 1:
                    dve.wait_ge(s4_faded, q + 1)
                    dve.wait_ge(s4_state, q + 1)
                    dve.tensor_tensor(HS, HS, PS[:, 2:4, :].rearrange("p a b -> p (a b)"), ALU.add).then_inc(s4_hs, 1)
                if q:
                    link.wait()
                    dve.wait_ge(s4_taken, q + 1)
                    dve.tensor_tensor(YS[:, q, :], YS[:, q, :], TMP, ALU.add).then_inc(s4_y, 1)
                else:
                    dve.wait_ge(s4_taken, 1)
                    dve.sem_inc(s4_y, 1)
            dve.wait_ge(s4_y, NT)
            dve.wait_ge(s4_ys, NT - 1)
            dve.tensor_tensor(YS[:, NT - 1, :], YS[:, NT - 1, :], ZG[:, NT - 1, :], ALU.mult).then_inc(s4_ys, 1)
            dve.wait_ge(act_marks, ACT_MARK["s4_rms"])
            link(dve.reciprocal(RMS, RMS))
            for q in range(NT):
                dve.tensor_scalar(YS[:, q, :], YS[:, q, :], RMS[:, q:q + 1], None, ALU.mult).then_inc(s4_yn, 1)
            for c in range(IT):
                dve.wait_ge(xt_hi, 2 * DT + c + 1)
                dve.scalar_tensor_tensor(out=YT_LO[:, c, :], in0=PS[:, c % 4, :], scalar=NORMW[:, c:c + 1],
                                         in1=YT_HI[:, c, :], op0=ALU.mult, op1=ALU.subtract).then_inc(s4_yt, 1)
            for t in range(NT):
                add_tile(dve, 4, t, scale=1.0 / W_UP)
                quantise_row_tile(dve, link, t)

        def s4_pe(pe):
            pe.wait_ge(s3_win_lo, 4 * DT + 2)
            for t in range(NT):
                cols = slice(t * P, (t + 1) * P)
                for c in range(DT):
                    if t == 0:
                        pe.wait_ge(xt_ready, DT * 4 + c + 1)
                    ins = matmul_split(pe, PS[:, 6, cols], (XT_HI[:, c, cols], XT_LO[:, c, cols]),
                                       (WIN_HI[:, c, PROJ - P:PROJ], WIN_LO[:, c, PROJ - P:PROJ]), c, DT)
            ins.then_inc(pe_marks, 1)
            for g in range(CVT):
                if g >= 4:
                    pe.wait_ge(s4_conv_in, g - 3)
                cols = slice(SSM_I + g * P, SSM_I + (g + 1) * P)
                for c in range(DT):
                    ins = matmul_split(pe, PS[:, g % 4, :], (WIN_HI[:, c, cols], WIN_LO[:, c, cols]),
                                       (XT_HI[:, c, :], XT_LO[:, c, :]), c, DT)
                ins.then_inc(s4_conv_psum, 1)
            for g in range(2 * NT):
                if g >= 2:
                    pe.wait_ge(s4_z, g - 1)
                t, half = g // 2, g % 2
                rows, cols = slice(t * P, (t + 1) * P), slice(half * 512, (half + 1) * 512)
                for c in range(DT):
                    ins = matmul_split(pe, PS[:, 4 + half, :], (XT_HI[:, c, rows], XT_LO[:, c, rows]),
                                       (WIN_HI[:, c, cols], WIN_LO[:, c, cols]), c, DT)
                ins.then_inc(s4_z_psum, 1)
            pe.wait_ge(dve_marks, DVE_MARK["s4_dta"])
            for k, rows in enumerate((UPPER, ONES)):
                ins = pe.matmul(PS[:, 6, k * P:(k + 1) * P], rows[:, :], DTVA.rearrange("p t h -> p (t h)"),
                                start=True, stop=True)
            ins.then_inc(pe_marks, 1)
            pe.wait_ge(s4_cv, CVT)
            pe.wait_ge(s4_z, 2 * NT)
            for q in range(NT):
                cols = slice(q * P, (q + 1) * P)
                if q:
                    pe.wait_ge(s4_taken, q)
                for c in range(IT):
                    pe.transpose(PS[:, c // 4, (c % 4) * P:(c % 4 + 1) * P], CV[:, c, cols], IDENT[:, :])
                if q:
                    pe.wait_ge(s4_hs, q + 1)
                pe.transpose(PS[:, 2, 0:P], CV[:, IT, cols], IDENT[:, :])
                pe.matmul(PS[:, 3, 0:P], CV[:, IT, cols], CV[:, IT + 1, cols], start=True, stop=True).then_inc(s4_small, 1)
                if q == 0:
                    pe.wait_ge(dve_marks, DVE_MARK["s4_sums_read"])
                for g in range(4):
                    for h in range(4):
                        at = PS[:, 4 + g, h * P:(h + 1) * P]
                        pe.matmul(at, IDENTB[:, :], FUTUREB[:, :], start=True, stop=False)
                        ins = pe.matmul(at, DTA[:, q, 4 * g + h:4 * g + h + 1].to_broadcast([P, P]), UPPER[:, :],
                                        start=False, stop=True)
                    ins.then_inc(s4_decay_psum, 1)
                pe.wait_ge(s4_read, q + 1)
                if q:
                    for half in range(2):
                        ins = pe.matmul(PS[:, half, :], CV[:, IT + 1, cols], HS[:, half * 512:(half + 1) * 512],
                                        start=True, stop=True)
                    ins.then_inc(s4_inter, 1)
                for h in range(SSM_H):
                    pe.wait_ge(s4_mix, 4 * q + h // 4 + 1)
                    ins = pe.matmul(PS[:, 4 + h // 4, (h % 4) * P:(h % 4 + 1) * P], DECAY[:, h, :],
                                    DTX[:, h * SSM_P:h * SSM_P + P], start=True, stop=True)
                ins.then_inc(s4_intra, 1)
                if q < NT - 1:
                    pe.wait_ge(s4_wdtx, q + 1)
                    for half in range(2):
                        ins = pe.matmul(PS[:, 2 + half, :], BNAT, WDTX[:, half * 512:(half + 1) * 512],
                                        start=True, stop=True)
                    ins.then_inc(s4_state, 1)
            pe.wait_ge(s4_yn, NT)
            pe.wait_ge(s4_hs, NT)
            for c in range(IT):
                if c >= 4:
                    pe.wait_ge(s4_yt, c - 3)
                for t in range(NT):
                    ins = pe.transpose(PS[:, c % 4, t * P:(t + 1) * P], YS[:, t, c * P:(c + 1) * P], IDENT[:, :])
                ins.then_inc(s4_yt_psum, 1)
            pe.wait_ge(s4_yt, IT)
            pe.wait_ge(pool_marks, POOL_MARK["s4_wout"])
            for t in range(NT):
                for c in range(IT):
                    rows = slice(t * P, (t + 1) * P)
                    ins = matmul_split(pe, PS[:, 4 + t, :], (YT_HI[:, c, rows], YT_LO[:, c, rows]),
                                       (WOUT_HI[:, c, :], WOUT_LO[:, c, :]), c, IT)
                ins.then_inc(out_psum, 1)
                if t:
                    turn_tile(pe, 5, t - 1)
            turn_tile(pe, 5, NT - 1)

        W1B = view(53 * K, [DT, FF1], BF16)
        W2B = view(69 * K, [F1T, D], BF16)
        XQT = view(85 * K, [DT, N], BF16)
        HT = view(89 * K, [F1T, N + 2])
        CO = view(122 * K, [F1T, N])
        HQ = view(154 * K, [F1T, N], BF16)
        ROWSC = view(170 * K, [N])
        AMX = view(172 * K, [N])
        FCW = view(0, [F1T, 3])
        FCB = view(1 * K, [F1T])
        HABS = view(2 * K, [4, N])
        TAP1 = view(10 * K, [2, N])
        XCL = COLS[:, 0:4]
        XSC = COLS[:, 4:8]
        XINV = COLS[:, 8:12]
        HCL = COLS[:, 12:16]
        HSC = COLS[:, 16:20]
        OSC = COLS[:, 20:24]

        s5_h_psum = sem("s5_h_psum")
        s5_h = sem("s5_h")
        s5_tap0 = sem("s5_tap0")
        s5_tap = sem("s5_tap")
        s5_conv = sem("s5_conv")
        s5_habs = sem("s5_habs")
        s5_mag = sem("s5_mag")
        s5_scaled = sem("s5_scaled")
        s5_rounded = sem("s5_rounded")
        s5_hq = sem("s5_hq")

        def s5_sp(sp):
            sp.wait_ge(x_done, NT * 5)
            sp.dma_start(FCW, a["fconvw"]).then_inc(small_in, 16)
            sp.dma_start(FCB, a["fconvb"]).then_inc(small_in, 16)

        def s5_pool(pool, link):
            pool.wait_ge(x_done, NT * 5)
            pool.memset(HT[:, :, 0:1], 0.0)
            pool.memset(HT[:, :, N + 1:N + 2], 0.0).then_inc(pool_marks, 1)
            for g in range(F1T):
                pool.wait_ge(s5_h, g + 1)
                if g >= 2:
                    pool.wait_ge(s5_tap, g - 1)
                link(pool.tensor_scalar(TAP1[:, g % 2, :], HT[:, g, 1:N + 1], FCW[:, g, 1:2], 1.0,
                                        ALU.mult, ALU.mult))
                pool.wait_ge(s5_tap0, g + 1)
                pool.tensor_tensor(CO[:, g, :], CO[:, g, :], TAP1[:, g % 2, :], ALU.add).then_inc(s5_tap, 1)
            for g in range(F1T):
                pool.wait_ge(s5_rounded, g + 1)
                pool.tensor_scalar(HQ[:, g, :], CO[:, g, :], 1.0, -ROUND, ALU.mult, ALU.add).then_inc(s5_hq, 1)

        def s5_act(act, link):
            for c in range(DT):
                act.wait_ge(xt_psum, DT * 5 + c + 1)
                act.copy(XQT[:, c, :], PS[:, c, :]).then_inc(xt_ready, 1)
            act.wait_ge(small_in, 10 * 16)
            act.wait_ge(pool_marks, POOL_MARK["s5_pad"])
            for g in range(F1T + 2):
                if g < F1T:
                    act.wait_ge(s5_h, g + 1)
                    act.activation(CO[:, g, :], HT[:, g, 0:N], ACT.Identity, scale=FCW[:, g, 0:1],
                                   bias=FCB[:, g:g + 1]).then_inc(s5_tap0, 1)
                if g >= 2:
                    d = g - 2
                    act.wait_ge(s5_conv, d + 1)
                    link(act.activation(CO[:, d, :], CO[:, d, :], ACT.Silu))
                    if d >= 4:
                        act.wait_ge(s5_mag, d - 2)
                    act.activation(HABS[:, d % 4, :], CO[:, d, :], ACT.Abs).then_inc(s5_habs, 1)
            for g in range(F1T):
                act.wait_ge(s5_scaled, g + 1)
                act.activation(CO[:, g, :], CO[:, g, :], ACT.Copy, bias=ROUND).then_inc(s5_rounded, 1)

        def quantise_row_tile(dve, link, t):
            link(norm_tile(dve, 5, t))
            link(dve.tensor_reduce(XCL[:, t:t + 1], XN[:, t, :], AX.X, ALU.max, apply_absolute_value=True))
            link(dve.tensor_scalar(XCL[:, t:t + 1], XCL[:, t:t + 1], 1e-5, None, ALU.max))
            link(dve.reciprocal(XSC[:, t:t + 1], XCL[:, t:t + 1]))
            link(dve.tensor_scalar(XSC[:, t:t + 1], XSC[:, t:t + 1], 127.0, None, ALU.mult))
            link(dve.tensor_scalar(XN[:, t, :], XN[:, t, :], XSC[:, t:t + 1], ROUND, ALU.mult, ALU.add))
            dve.tensor_scalar(XN[:, t, :], XN[:, t, :], ROUND, None, ALU.subtract).then_inc(ln_xn, 1)

        def s5_dve(dve, link):
            dve.tensor_scalar(XINV, XCL, 1.0 / 127.0, W_MEAN[:, 0:1], ALU.mult, ALU.mult).then_inc(dve_marks, 1)
            dve.wait_ge(small_in, 10 * 16)
            dve.wait_ge(pe_marks, PE_MARK["s5_row_psum"])
            dve.tensor_copy(ROWSC, PS[:, 4, :]).then_inc(dve_marks, 1)
            dve.wait_ge(dve_marks, DVE_MARK["s5_row"])

            dve.memset(AMX, 0.0).then_inc(s5_mag, 1)
            for g in range(F1T + 4):
                if g < F1T:
                    dve.wait_ge(s5_h_psum, g + 1)
                    dve.tensor_tensor(HT[:, g, 1:N + 1], PS[:, g % 8, :], ROWSC, ALU.mult).then_inc(s5_h, 1)
                if 2 <= g < F1T + 2:
                    d = g - 2
                    dve.wait_ge(s5_tap, d + 1)
                    dve.scalar_tensor_tensor(out=CO[:, d, :], in0=HT[:, d, 2:N + 2], scalar=FCW[:, d, 2:3],
                                             in1=CO[:, d, :], op0=ALU.mult, op1=ALU.add).then_inc(s5_conv, 1)
                if g >= 4:
                    d = g - 4
                    dve.wait_ge(s5_habs, d + 1)
                    dve.wait_ge(s5_mag, d + 1)
                    dve.tensor_tensor(AMX, HABS[:, d % 4, :], AMX, ALU.max).then_inc(s5_mag, 1)
            dve.wait_ge(pe_marks, PE_MARK["s5_mag_psum"])
            link(dve.tensor_reduce(HCL, PS[:, 5, :].rearrange("p (t c) -> p t c", t=NT), AX.X, ALU.max))
            link(dve.tensor_scalar(HCL, HCL, 1e-5, None, ALU.max))
            link(dve.reciprocal(HSC, HCL))
            dve.tensor_scalar(HSC, HSC, 127.0, None, ALU.mult).then_inc(dve_marks, 1)
            dve.tensor_scalar(OSC, HCL, 1.0 / 127.0, W_MEAN[:, 1:2], ALU.mult, ALU.mult).then_inc(dve_marks, 1)
            dve.wait_ge(pe_marks, PE_MARK["s5_scale_psum"])
            for g in range(F1T):
                dve.tensor_tensor(CO[:, g, :], CO[:, g, :], PS[:, 6, :], ALU.mult).then_inc(s5_scaled, 1)
            dve.wait_ge(dve_marks, DVE_MARK["s5_out_scale"])
            for t in range(NT):
                dve.wait_ge(out_psum, NT * 5 + t + 1)
                dve.scalar_tensor_tensor(out=X[:, t, :], in0=PS[:, t, :], scalar=OSC[:, t:t + 1], in1=X[:, t, :],
                                         op0=ALU.mult, op1=ALU.add).then_inc(x_done, 1)

        def s5_pe(pe):
            pe.wait_ge(dve_marks, DVE_MARK["s5_xinv"])
            for t in range(NT):
                ins = pe.matmul(PS[:, 4, t * P:(t + 1) * P], XINV[:, t:t + 1].to_broadcast([P, P]), IDENT[:, :],
                                start=True, stop=True)
            ins.then_inc(pe_marks, 1)
            pe.wait_ge(s3_tern, 8)
            pe.wait_ge(dve_marks, DVE_MARK["s5_row"])
            for g in range(F1T):
                if g >= 8:
                    pe.wait_ge(s5_h, g - 7)
                for c in range(DT):
                    if g == 0:
                        pe.wait_ge(xt_ready, DT * 5 + c + 1)
                    ins = pe.matmul(PS[:, g % 8, :], W1B[:, c, g * P:(g + 1) * P], XQT[:, c, :],
                                    start=(c == 0), stop=(c == DT - 1))
                ins.then_inc(s5_h_psum, 1)
            pe.wait_ge(s5_mag, F1T + 1)
            for t in range(NT):
                ins = pe.transpose(PS[:, 5, t * P:(t + 1) * P], AMX[:, t * P:(t + 1) * P], IDENT[:, :])
            ins.then_inc(pe_marks, 1)
            pe.wait_ge(dve_marks, DVE_MARK["s5_scale"])
            for t in range(NT):
                ins = pe.matmul(PS[:, 6, t * P:(t + 1) * P], HSC[:, t:t + 1].to_broadcast([P, P]), IDENT[:, :],
                                start=True, stop=True)
            ins.then_inc(pe_marks, 1)
            for g in range(F1T):
                pe.wait_ge(s5_hq, g + 1)
                for t in range(NT):
                    ins = pe.matmul(PS[:, t, :], HQ[:, g, t * P:(t + 1) * P], W2B[:, g, :],
                                    start=(g == 0), stop=(g == F1T - 1))
                    if g == F1T - 1:
                        ins.then_inc(out_psum, 1)

        out_done = sem("out_done")
        block = ctx.enter_context(nc.Block())

        @block.sync
        def _(sp):
            for part in (s0_sp, s3_sp, s4_sp, s5_sp):
                part(sp)
            sp.wait_ge(x_done, NT * 6)
            sp.dma_start(out.rearrange("(t p) c -> p t c", p=P), X[:, :, :]).then_inc(out_done, 16)
            sp.wait_ge(out_done, 16)

        @block.gpsimd
        def _(pool):
            link = Order(pool, pool_order)
            setup_pool(pool, link)
            for part in (s0_pool, s1_pool, s2_pool, s3_pool, s4_pool, s5_pool):
                part(pool, link)

        @block.scalar
        def _(act):
            link = Order(act, act_order)
            act.wait_ge(pool_marks, POOL_MARK["const_ready"])
            for part in (s0_act, s1_act, s2_act, s3_act, s4_act, s5_act):
                part(act, link)

        @block.vector
        def _(dve):
            link = Order(dve, dve_order)
            dve.wait_ge(x_in, 16)
            dve.wait_ge(pool_marks, POOL_MARK["const_ready"])
            for part in (s0_dve, s1_dve, s2_dve, s3_dve, s4_dve, s5_dve):
                part(dve, link)

        @block.tensor
        def _(pe):
            pe.wait_ge(pool_marks, POOL_MARK["const_ready"])
            for part in (s0_pe, s1_pe, s2_pe, s3_pe, s4_pe, s5_pe):
                part(pe)


def kernel(**inputs):
    import numpy as np
    import concourse.bacc as bacc
    from concourse import mybir as mb
    from concourse.bass_utils import run_bass_kernel_spmd

    nc = bacc.Bacc("TRN2", target_bir_lowering=False, num_devices=1)
    arrays, aps = {}, {}
    for name, value in layout(inputs, np).items():
        value = np.ascontiguousarray(value)
        arrays[f"in_{name}"] = value
        aps[name] = nc.dram_tensor(f"in_{name}", value.shape, mb.dt.from_np(value.dtype), kind="ExternalInput").ap()
    out = nc.dram_tensor("out_latents", (N, D), F32, kind="ExternalOutput").ap()
    perceiver_kernel(nc, aps, out)
    r = run_bass_kernel_spmd(nc, [arrays], core_ids=[0])
    return r.results[0]["out_latents"].reshape(1, N, D)
```
